# Optimizing a Trainium2 kernel written in Bass

```python
import numpy as np
import jax
import jax.numpy as jnp

def _softmax(x, axis=-1):
    return jax.nn.softmax(x, axis=axis)

def _gelu(x):
    return jax.nn.gelu(x, approximate=True)

def _silu(x):
    return jax.nn.silu(x)

def _sigmoid(x):
    return jax.nn.sigmoid(x)

def _layernorm(x, axis=-1, eps=1e-05):
    m = jnp.mean(x, axis=axis, keepdims=True)
    v = jnp.var(x, axis=axis, keepdims=True)
    return (x - m) / jnp.sqrt(v + eps)

def _scatter_add(tgt, idx, src, axis=0):
    return tgt.at[idx].add(src)

def _segment_sum(src, seg, n):
    return jax.ops.segment_sum(src, seg, n)
kernel_name = 'mk_recurrent_d2_jaxref_r8_284375'

def setup_inputs(seed: int=0):
    np.random.seed(seed)
    _w = jnp.asarray

    def _L0_attn_setup():
        import jax, jax.numpy as jnp
        import numpy as np
        from jax import lax
        B, S, D = (8, 128, 128)
        DH = D // 2
        H = 8
        DK = DH // H
        DFF = 4 * D
        ALPHA, BETA = (0.1, 0.1)
        EPS = 1e-05
        PARAM_SPECS = [('wq1', (DH, DH)), ('bq1', (DH,)), ('wk1', (DH, DH)), ('bk1', (DH,)), ('wv1', (DH, DH)), ('bv1', (DH,)), ('wo1', (DH, DH)), ('bo1', (DH,)), ('wq2', (DH, DH)), ('bq2', (DH,)), ('wk2', (DH, DH)), ('bk2', (DH,)), ('wv2', (DH, DH)), ('bv2', (DH,)), ('wo2', (DH, DH)), ('bo2', (DH,)), ('g1', (DH,)), ('be1', (DH,)), ('g2', (DH,)), ('be2', (DH,)), ('w_ff1', (DFF, D)), ('b_ff1', (DFF,)), ('w_ff2', (D, DFF)), ('b_ff2', (D,)), ('g_ff', (D,)), ('be_ff', (D,))]

        def layernorm(x, g, b):
            m = jnp.mean(x, axis=-1, keepdims=True)
            v = jnp.mean(jnp.square(x - m), axis=-1, keepdims=True)
            return (x - m) * lax.rsqrt(v + EPS) * g + b

        def mha(xin, wq, bq, wk, bk, wv, bv, wo, bo):
            b, s, _ = xin.shape
            q = (xin @ wq.T + bq).reshape(b, s, H, DK)
            k = (xin @ wk.T + bk).reshape(b, s, H, DK)
            v = (xin @ wv.T + bv).reshape(b, s, H, DK)
            scores = jnp.einsum('bshd,bthd->bhst', q, k) * (1.0 / np.sqrt(DK).astype(np.float32))
            a = jax.nn.softmax(scores, axis=-1)
            o = jnp.einsum('bhst,bthd->bshd', a, v).reshape(b, s, DH)
            return o @ wo.T + bo

        def holt(x, alpha, beta):
            x0 = x[:, 0]

            def step(carry, xt):
                level, trend = carry
                nl = alpha * xt + (1.0 - alpha) * (level + trend)
                nt = beta * (nl - level) + (1.0 - beta) * trend
                return ((nl, nt), nl)
            _, lv = lax.scan(step, (x0, jnp.zeros_like(x0)), jnp.swapaxes(x[:, 1:], 0, 1))
            return jnp.concatenate([x0[:, None], jnp.swapaxes(lv, 0, 1)], axis=1)
        key = jax.random.key(seed)
        inp = {'x': jax.random.normal(jax.random.fold_in(key, 0), (B, S, D), jnp.float32)}
        for i, (name, shape) in enumerate(PARAM_SPECS):
            k = jax.random.fold_in(key, i + 1)
            if name.startswith('g'):
                inp[name] = jnp.ones(shape, jnp.float32)
            elif name.startswith('b'):
                inp[name] = jnp.zeros(shape, jnp.float32)
            else:
                inp[name] = jax.random.normal(k, shape, jnp.float32) * 0.02
        return inp
    _L0_attn_in = _L0_attn_setup()

    def _L0_ffn_setup():
        import jax, jax.numpy as jnp
        import numpy as np
        key = jax.random.key(seed)
        k1, k2, k3, k4 = jax.random.split(key, 4)
        B, T, M = (4, 256, 128)
        E, F = (16, 512)
        x = jax.random.normal(k1, (B, T, M), dtype=jnp.float32) * 0.02
        Wg = jax.random.normal(k2, (M, E), dtype=jnp.float32) * 0.02
        w1 = jax.random.normal(k3, (E, M, F), dtype=jnp.float32) * 0.02
        w2 = jax.random.normal(k4, (E, F, M), dtype=jnp.float32) * 0.02
        return {'x': x, 'Wg': Wg, 'w1': w1, 'w2': w2}
    _L0_ffn_in = _L0_ffn_setup()

    def _L1_attn_setup():
        import jax, jax.numpy as jnp
        import numpy as np
        D_MODEL = 128
        N_HEADS = 16
        HEAD_DIM = D_MODEL // N_HEADS

        def alibi_slopes(n_heads):
            base = 2.0 ** (-8.0 / n_heads)
            return jnp.asarray([base ** i for i in range(1, n_heads + 1)], dtype=jnp.float32)
        key = jax.random.key(seed)
        kx, kq, kk, kv, ko = jax.random.split(key, 5)
        B, T = (2, 256)
        scale = 0.02
        x = jax.random.normal(kx, (B, T, D_MODEL), dtype=jnp.float32)
        Wq = jax.random.normal(kq, (D_MODEL, D_MODEL), dtype=jnp.float32) * scale
        Wk = jax.random.normal(kk, (D_MODEL, D_MODEL), dtype=jnp.float32) * scale
        Wv = jax.random.normal(kv, (D_MODEL, D_MODEL), dtype=jnp.float32) * scale
        Wo = jax.random.normal(ko, (D_MODEL, D_MODEL), dtype=jnp.float32) * scale
        return {'x': x, 'Wq': Wq, 'Wk': Wk, 'Wv': Wv, 'Wo': Wo}
    _L1_attn_in = _L1_attn_setup()

    def _L1_ffn_setup():
        import jax, jax.numpy as jnp
        import numpy as np
        E, TOP_K, D, H = (8, 2, 128, 256)
        B, S = (2, 256)
        key = jax.random.key(seed)
        ks = jax.random.split(key, 10)
        s = 0.02
        return {'x': jax.random.normal(ks[0], (B, S, D), dtype=jnp.float32), 'gate_w': jax.random.normal(ks[1], (E, D), dtype=jnp.float32) * s, 'gate_b': jnp.zeros((E,), dtype=jnp.float32), 'w0': jax.random.normal(ks[2], (E, H, D), dtype=jnp.float32) * s, 'b0': jnp.zeros((E, H), dtype=jnp.float32), 'w1': jax.random.normal(ks[3], (E, H, D), dtype=jnp.float32) * s, 'b1': jnp.zeros((E, H), dtype=jnp.float32), 'w2': jax.random.normal(ks[4], (E, D, H), dtype=jnp.float32) * s, 'b2': jnp.zeros((E, D), dtype=jnp.float32)}
    _L1_ffn_in = _L1_ffn_setup()
    _d = {'L0_attn_x': _L0_attn_in['x'], 'L0_attn_wq1': _L0_attn_in['wq1'], 'L0_attn_bq1': _L0_attn_in['bq1'], 'L0_attn_wk1': _L0_attn_in['wk1'], 'L0_attn_bk1': _L0_attn_in['bk1'], 'L0_attn_wv1': _L0_attn_in['wv1'], 'L0_attn_bv1': _L0_attn_in['bv1'], 'L0_attn_wo1': _L0_attn_in['wo1'], 'L0_attn_bo1': _L0_attn_in['bo1'], 'L0_attn_wq2': _L0_attn_in['wq2'], 'L0_attn_bq2': _L0_attn_in['bq2'], 'L0_attn_wk2': _L0_attn_in['wk2'], 'L0_attn_bk2': _L0_attn_in['bk2'], 'L0_attn_wv2': _L0_attn_in['wv2'], 'L0_attn_bv2': _L0_attn_in['bv2'], 'L0_attn_wo2': _L0_attn_in['wo2'], 'L0_attn_bo2': _L0_attn_in['bo2'], 'L0_attn_g1': _L0_attn_in['g1'], 'L0_attn_be1': _L0_attn_in['be1'], 'L0_attn_g2': _L0_attn_in['g2'], 'L0_attn_be2': _L0_attn_in['be2'], 'L0_attn_w_ff1': _L0_attn_in['w_ff1'], 'L0_attn_b_ff1': _L0_attn_in['b_ff1'], 'L0_attn_w_ff2': _L0_attn_in['w_ff2'], 'L0_attn_b_ff2': _L0_attn_in['b_ff2'], 'L0_attn_g_ff': _L0_attn_in['g_ff'], 'L0_attn_be_ff': _L0_attn_in['be_ff'], 'L0_ffn_Wg': _L0_ffn_in['Wg'], 'L0_ffn_w1': _L0_ffn_in['w1'], 'L0_ffn_w2': _L0_ffn_in['w2'], 'L1_attn_Wq': _L1_attn_in['Wq'], 'L1_attn_Wk': _L1_attn_in['Wk'], 'L1_attn_Wv': _L1_attn_in['Wv'], 'L1_attn_Wo': _L1_attn_in['Wo'], 'L1_ffn_gate_w': _L1_ffn_in['gate_w'], 'L1_ffn_gate_b': _L1_ffn_in['gate_b'], 'L1_ffn_w0': _L1_ffn_in['w0'], 'L1_ffn_b0': _L1_ffn_in['b0'], 'L1_ffn_w1': _L1_ffn_in['w1'], 'L1_ffn_b1': _L1_ffn_in['b1'], 'L1_ffn_w2': _L1_ffn_in['w2'], 'L1_ffn_b2': _L1_ffn_in['b2']}
    _x0 = _d['L0_attn_x']
    _d['L0_attn_x'] = jax.random.normal(jax.random.fold_in(jax.random.key(seed), 1), (8, 512, 128), dtype=_x0.dtype)
    del _x0
    return _d

def reference(L0_attn_x, L0_attn_wq1, L0_attn_bq1, L0_attn_wk1, L0_attn_bk1, L0_attn_wv1, L0_attn_bv1, L0_attn_wo1, L0_attn_bo1, L0_attn_wq2, L0_attn_bq2, L0_attn_wk2, L0_attn_bk2, L0_attn_wv2, L0_attn_bv2, L0_attn_wo2, L0_attn_bo2, L0_attn_g1, L0_attn_be1, L0_attn_g2, L0_attn_be2, L0_attn_w_ff1, L0_attn_b_ff1, L0_attn_w_ff2, L0_attn_b_ff2, L0_attn_g_ff, L0_attn_be_ff, L0_ffn_Wg, L0_ffn_w1, L0_ffn_w2, L1_attn_Wq, L1_attn_Wk, L1_attn_Wv, L1_attn_Wo, L1_ffn_gate_w, L1_ffn_gate_b, L1_ffn_w0, L1_ffn_b0, L1_ffn_w1, L1_ffn_b1, L1_ffn_w2, L1_ffn_b2):

    def _L0_attn_ref(x, wq1, bq1, wk1, bk1, wv1, bv1, wo1, bo1, wq2, bq2, wk2, bk2, wv2, bv2, wo2, bo2, g1, be1, g2, be2, w_ff1, b_ff1, w_ff2, b_ff2, g_ff, be_ff):
        import jax, jax.numpy as jnp
        import numpy as np
        from jax import lax
        B, S, D = (8, 128, 128)
        DH = D // 2
        H = 8
        DK = DH // H
        DFF = 4 * D
        ALPHA, BETA = (0.1, 0.1)
        EPS = 1e-05
        PARAM_SPECS = [('wq1', (DH, DH)), ('bq1', (DH,)), ('wk1', (DH, DH)), ('bk1', (DH,)), ('wv1', (DH, DH)), ('bv1', (DH,)), ('wo1', (DH, DH)), ('bo1', (DH,)), ('wq2', (DH, DH)), ('bq2', (DH,)), ('wk2', (DH, DH)), ('bk2', (DH,)), ('wv2', (DH, DH)), ('bv2', (DH,)), ('wo2', (DH, DH)), ('bo2', (DH,)), ('g1', (DH,)), ('be1', (DH,)), ('g2', (DH,)), ('be2', (DH,)), ('w_ff1', (DFF, D)), ('b_ff1', (DFF,)), ('w_ff2', (D, DFF)), ('b_ff2', (D,)), ('g_ff', (D,)), ('be_ff', (D,))]

        def layernorm(x, g, b):
            m = jnp.mean(x, axis=-1, keepdims=True)
            v = jnp.mean(jnp.square(x - m), axis=-1, keepdims=True)
            return (x - m) * lax.rsqrt(v + EPS) * g + b

        def mha(xin, wq, bq, wk, bk, wv, bv, wo, bo):
            b, s, _ = xin.shape
            q = (xin @ wq.T + bq).reshape(b, s, H, DK)
            k = (xin @ wk.T + bk).reshape(b, s, H, DK)
            v = (xin @ wv.T + bv).reshape(b, s, H, DK)
            scores = jnp.einsum('bshd,bthd->bhst', q, k) * (1.0 / np.sqrt(DK).astype(np.float32))
            a = jax.nn.softmax(scores, axis=-1)
            o = jnp.einsum('bhst,bthd->bshd', a, v).reshape(b, s, DH)
            return o @ wo.T + bo

        def holt(x, alpha, beta):
            x0 = x[:, 0]

            def step(carry, xt):
                level, trend = carry
                nl = alpha * xt + (1.0 - alpha) * (level + trend)
                nt = beta * (nl - level) + (1.0 - beta) * trend
                return ((nl, nt), nl)
            _, lv = lax.scan(step, (x0, jnp.zeros_like(x0)), jnp.swapaxes(x[:, 1:], 0, 1))
            return jnp.concatenate([x0[:, None], jnp.swapaxes(lv, 0, 1)], axis=1)
        xh = x[:, :, :DH]
        x1 = layernorm(xh + mha(xh, wq1, bq1, wk1, bk1, wv1, bv1, wo1, bo1), g1, be1)
        xs = holt(x, ALPHA, BETA)
        xsh = xs[:, :, :DH]
        x2 = layernorm(xsh + mha(xsh, wq2, bq2, wk2, bk2, wv2, bv2, wo2, bo2), g2, be2)
        y = jnp.concatenate([x1, x2], axis=-1)
        y_ff = jax.nn.relu(y @ w_ff1.T + b_ff1) @ w_ff2.T + b_ff2
        return layernorm(y + y_ff, g_ff, be_ff)

    def _L0_ffn_ref(x, Wg, w1, w2):
        import jax, jax.numpy as jnp
        import numpy as np
        d = x.shape[-1]
        xr = x.reshape(-1, d)
        S = xr.shape[0]
        E = Wg.shape[1]
        C = (S + E - 1) // E
        gate = jax.nn.softmax(xr @ Wg, axis=-1)
        idx = jnp.argmax(gate, axis=1)
        gates_s = jnp.take_along_axis(gate, idx[:, None], axis=1)[:, 0]
        onehot = jax.nn.one_hot(idx, E, dtype=jnp.int32)
        loc = jnp.sum((jnp.cumsum(onehot, axis=0) - 1) * onehot, axis=1)
        valid = loc < C
        loc_pad = jnp.minimum(loc, C)
        dispatched = jnp.zeros((E, C + 1, d), dtype=x.dtype).at[idx, loc_pad].set(xr)
        dispatched = dispatched[:, :C]
        h = jax.nn.relu(jnp.einsum('ecm,emf->ecf', dispatched, w1))
        expert_out = jnp.einsum('ecf,efm->ecm', h, w2)
        gathered = expert_out[idx, jnp.minimum(loc, C - 1)]
        combined = gathered * (gates_s * valid.astype(x.dtype))[:, None]
        return combined.reshape(x.shape)

    def _L1_attn_ref(x, Wq, Wk, Wv, Wo):
        import jax, jax.numpy as jnp
        import numpy as np
        D_MODEL = 128
        N_HEADS = 16
        HEAD_DIM = D_MODEL // N_HEADS

        def alibi_slopes(n_heads):
            base = 2.0 ** (-8.0 / n_heads)
            return jnp.asarray([base ** i for i in range(1, n_heads + 1)], dtype=jnp.float32)
        B, T, D = x.shape
        H, hd = (N_HEADS, HEAD_DIM)

        def proj(W):
            return (x @ W.T).reshape(B, T, H, hd).transpose(0, 2, 1, 3)
        q, k, v = (proj(Wq), proj(Wk), proj(Wv))
        scale = hd ** (-0.5)
        scores = jnp.einsum('bhqd,bhkd->bhqk', q, k) * scale
        pos = jnp.arange(T, dtype=jnp.float32)
        dist = jnp.abs(pos[:, None] - pos[None, :])
        causal = pos[:, None] >= pos[None, :]
        slopes = alibi_slopes(H)
        bias = -slopes[:, None, None] * jnp.where(causal, dist, 0.0)
        scores = scores + bias[None]
        scores = jnp.where(causal[None, None], scores, -jnp.inf)
        attn = jax.nn.softmax(scores, axis=-1)
        out = jnp.einsum('bhqk,bhkd->bhqd', attn, v)
        out = out.transpose(0, 2, 1, 3).reshape(B, T, D)
        return out @ Wo.T

    def _L1_ffn_ref(x, gate_w, gate_b, w0, b0, w1, b1, w2, b2):
        import jax, jax.numpy as jnp
        import numpy as np
        E, TOP_K, D, H = (8, 2, 128, 256)
        B, S = (2, 256)
        Bn, Sq, Dv = x.shape
        xt = x.reshape(-1, Dv)
        logits = xt @ gate_w.T + gate_b
        top_v, top_i = jax.lax.top_k(logits, TOP_K)
        h0 = jnp.einsum('td,ehd->eth', xt, w0) + b0[:, None, :]
        h1 = jnp.einsum('td,ehd->eth', xt, w1) + b1[:, None, :]
        act = h0 * jax.nn.silu(h1)
        out_all = jnp.einsum('eth,edh->etd', act, w2) + b2[:, None, :]
        out_te = jnp.transpose(out_all, (1, 0, 2))
        sel = jnp.take_along_axis(out_te, top_i[:, :, None], axis=1)
        w = jax.nn.softmax(top_v, axis=-1)[:, :, None]
        out = (w * sel).sum(axis=1)
        return out.reshape(Bn, Sq, Dv)
    x = L0_attn_x
    xn = _layernorm(x, axis=-1)
    s = _L0_attn_ref(xn, L0_attn_wq1, L0_attn_bq1, L0_attn_wk1, L0_attn_bk1, L0_attn_wv1, L0_attn_bv1, L0_attn_wo1, L0_attn_bo1, L0_attn_wq2, L0_attn_bq2, L0_attn_wk2, L0_attn_bk2, L0_attn_wv2, L0_attn_bv2, L0_attn_wo2, L0_attn_bo2, L0_attn_g1, L0_attn_be1, L0_attn_g2, L0_attn_be2, L0_attn_w_ff1, L0_attn_b_ff1, L0_attn_w_ff2, L0_attn_b_ff2, L0_attn_g_ff, L0_attn_be_ff)
    g = _silu(_L0_ffn_ref(xn, L0_ffn_Wg, L0_ffn_w1, L0_ffn_w2))
    x = x + s * g
    xn = _layernorm(x, axis=-1)
    s = _L1_attn_ref(xn, L1_attn_Wq, L1_attn_Wk, L1_attn_Wv, L1_attn_Wo)
    g = _silu(_L1_ffn_ref(xn, L1_ffn_gate_w, L1_ffn_gate_b, L1_ffn_w0, L1_ffn_b0, L1_ffn_w1, L1_ffn_b1, L1_ffn_w2, L1_ffn_b2))
    x = x + s * g
    return x

_drawn_inputs = setup_inputs


def setup_inputs(seed=0):
    import zlib

    import numpy as np

    out = dict(_drawn_inputs(seed))
    spreads = {'L0_attn_bq1': (0.0, 0.8),
     'L0_attn_bk1': (0.0, 0.8),
     'L0_attn_bv1': (0.0, 0.8),
     'L0_attn_bo1': (0.0, 0.8),
     'L0_attn_bq2': (0.0, 0.8),
     'L0_attn_bk2': (0.0, 0.1),
     'L0_attn_bv2': (0.0, 0.8),
     'L0_attn_bo2': (0.0, 0.8),
     'L0_attn_g1': (1.0, 0.6),
     'L0_attn_be1': (0.0, 0.8),
     'L0_attn_g2': (1.0, 0.6),
     'L0_attn_be2': (0.0, 0.8),
     'L0_attn_b_ff1': (0.0, 0.8),
     'L0_attn_b_ff2': (0.0, 0.8),
     'L0_attn_g_ff': (1.0, 0.6),
     'L0_attn_be_ff': (0.0, 0.8),
     'L1_ffn_gate_b': (0.0, 0.8),
     'L1_ffn_b0': (0.0, 0.8),
     'L1_ffn_b1': (0.0, 0.8),
     'L1_ffn_b2': (0.0, 0.8)}
    factors = {'L0_attn_wq1': 8.0,
     'L0_attn_wk1': 8.0,
     'L0_attn_wv1': 8.0,
     'L0_attn_wo1': 8.0,
     'L0_attn_wq2': 8.0,
     'L0_attn_wk2': 8.0,
     'L0_attn_wv2': 8.0,
     'L0_attn_wo2': 8.0,
     'L0_attn_w_ff1': 8.0,
     'L0_attn_w_ff2': 8.0,
     'L0_ffn_Wg': 8.0,
     'L0_ffn_w1': 8.0,
     'L0_ffn_w2': 8.0,
     'L1_attn_Wq': 8.0,
     'L1_attn_Wk': 8.0,
     'L1_attn_Wv': 8.0,
     'L1_attn_Wo': 8.0,
     'L1_ffn_gate_w': 8.0,
     'L1_ffn_w0': 8.0,
     'L1_ffn_w1': 8.0,
     'L1_ffn_w2': 8.0}
    for name, (base, spread) in spreads.items():
        noise = np.random.default_rng([zlib.crc32(name.encode()), seed]).standard_normal(out[name].shape)
        drawn = base * np.exp(spread * noise) if base else spread * noise
        out[name] = jnp.asarray(drawn.astype(out[name].dtype))
    for name, factor in factors.items():
        out[name] = (out[name] * factor).astype(out[name].dtype)
    return out
```

```python
import math
from contextlib import ExitStack

import numpy as np

import concourse.bass as bass
from concourse import mybir

F32, BF16 = mybir.dt.float32, mybir.dt.bfloat16
U32, I32 = mybir.dt.uint32, mybir.dt.int32
ALU = mybir.AluOpType
ACT = mybir.ActivationFunctionType
AX = mybir.AxisListType

P = 128
NB, S, D = 8, 512, 128
QT = S // P
NT = NB * QT
HD, H = 8, 16
HALF = D // 2
NG = H // 2
STRIP = 64
PARTS = 6
ROW_SHIFT = PARTS * HD
ROW_ALIBI = ROW_SHIFT + 2
ROW_END = ROW_ALIBI + 3
VW = 32
SCALE = 1.0 / math.sqrt(HD)
EPS = 1e-5
MASK = -1.0e30

E0, F0 = 16, 512
CAP = NB * S // E0
FC0 = F0 // P
E1, F1, TOP = 8, 256, 2
FC1 = F1 // P
TILES1 = NB * S * TOP // P + E1
PACK1 = 2 * F1 + FC1 * D + 2 * FC1 + D

C_IDENT = 0
C_BEFORE = C_IDENT + P
C_MASK_QK = C_BEFORE + P
C_MASK_KQ = C_MASK_QK + P
C_EXP0 = C_MASK_KQ + P
C_EXP1 = C_EXP0 + E0
C_FILL = C_EXP1 + E1
C_DUMP = C_FILL + NT
C_TILE = C_DUMP + NT
C_HOLT = C_TILE + TILES1
N_HOLT = QT * (QT + 1) // 2
C_END = C_HOLT + N_HOLT * P


def holt_block(st, tt):
    return st * QT - st * (st - 1) // 2 + tt - st


def constants():
    c = np.zeros((P, C_END), np.float32)
    n = np.arange(P)
    c[:, C_IDENT:C_IDENT + P] = np.eye(P)
    c[:, C_BEFORE:C_BEFORE + P] = n[:, None] < n[None, :]
    c[:, C_MASK_QK:C_MASK_QK + P] = np.where(n[None, :] > n[:, None], MASK, 0)
    c[:, C_MASK_KQ:C_MASK_KQ + P] = np.where(n[:, None] > n[None, :], MASK, 0)
    c[:, C_EXP0:C_EXP0 + E0] = np.arange(E0) - E0
    c[:, C_EXP1:C_EXP1 + E1] = np.arange(E1) - E1
    c[:, C_FILL:C_FILL + NT] = P * np.arange(NT)
    c[:, C_DUMP:C_DUMP + NT] = E0 * CAP + P * np.arange(NT)[None, :] + n[:, None]
    c[:, C_TILE:C_TILE + TILES1] = np.arange(TILES1)
    alpha, beta = 0.1, 0.1
    level, trend = np.zeros(S), np.zeros(S)
    level[0] = 1.0
    rows = [level]
    for t in range(1, S):
        x = np.zeros(S)
        x[t] = 1.0
        new = alpha * x + (1 - alpha) * (level + trend)
        trend = beta * (new - level) + (1 - beta) * trend
        level = new
        rows.append(level)
    holt = np.stack(rows, 1)
    for st in range(QT):
        for tt in range(st, QT):
            at = C_HOLT + holt_block(st, tt) * P
            c[:, at:at + P] = holt[st * P:(st + 1) * P, tt * P:(tt + 1) * P]
    return c


def alibi():
    base = 2.0 ** (-8.0 / H)
    slopes = np.array([np.float32(base ** i) for i in range(1, H + 1)], np.float32)
    order = [2 * g + j for j in range(2) for g in range(NG)]
    return (slopes[order][:, None] * (np.arange(S) - S // 2)[None, :].astype(np.float32)).astype(np.float32)


class Tally:

    def __init__(self, adds):
        self.adds, self.n, self.trip, self.per = adds, {}, None, {}

    def at(self, name):
        v = self.n.get(name, 0)
        return v if self.trip is None else self.trip * self.per.get(name, 0) + v

    def step(self, step):
        for name, k in self.adds(step).items():
            self.n[name] = self.n.get(name, 0) + k

    def enter(self, trip, steps):
        self.trip, self.per = trip, {}
        for s in steps:
            for name, k in self.adds(s).items():
                self.per[name] = self.per.get(name, 0) + k

    def leave(self, trips):
        for name, k in self.per.items():
            self.n[name] = self.n.get(name, 0) + k * (trips - 1)
        self.trip = None


def wait(eng, sem, value):
    if isinstance(value, int) and value <= 0:
        return
    eng.wait_ge(sem, value)


def wait_apart(eng, sem, value, apart):
    wait(eng, sem, value)
    if not isinstance(value, int):
        eng.sem_inc(apart, 1)


GROUPS = H
MAX_TILES = H * QT
FIRST_MAX = 5

BEHIND = {
    0: {0: [("gather", -1, 0), ("onT", -1, 0), ("zT", 1, 0)],
        1: [("proj", -1, 0), ("q", 1, 0), ("k", 1, 0)],
        2: [("ln1", -1, 0), ("v", 1, 0), ("fetch", 1, 0)],
        3: [("z", 1, 0)],
        4: [("yT", -1, 0)],
        5: [("ff1", -1, 0), ("ff1", -1, 1)],
        6: [("ff1", -1, 2), ("ff1", -1, 3)],
        7: [("ff2", -1, 0)],
        8: [("gate", -1, 0)],
        9: [("ln2", -1, 0)],
        10: [("mix", -1, 0)],
        11: [("ln3a", -1, 0)],
        12: [("ln3b", -1, 0)],
        13: [("x2T", -1, 0)],
        14: [("logits", -1, 0)]},
    1: {0: [("gather", -1, 0), ("onT", -1, 0), ("zT", 1, 0)],
        1: [("proj", -1, 0), ("q", 1, 0), ("k", 1, 0)],
        2: [("v", 1, 0), ("fetch", 1, 0)],
        4: [("gate", -1, 0)],
        6: [("mix", -1, 0)]},
}


def plan(layer, b):
    here, ahead, behind = 0 <= b < NB, b + 1 < NB, b >= 1
    steps = []
    if ahead:
        steps.append(("load", 1, 0))
    if behind:
        steps.append(("loadx", -1, 0))
    done = 0
    for n in range(GROUPS):
        if here:
            steps.append(("exp", 0, n))
        if n == 0 and behind:
            steps += [("sum", -1, (GROUPS - 1, here)), ("take", -1, QT - 1), ("norm", -1, QT - 1)]
        elif n > 0 and here:
            steps.append(("sum", 0, (n - 1, True)))
            if n % QT == 0:
                steps.append(("take", 0, n // QT - 1))
            if n % QT == 1 and n > 1:
                steps.append(("norm", 0, n // QT - 1))
        for s in BEHIND[layer].get(n, []):
            if (s[1] == 1 and ahead) or (s[1] == -1 and behind):
                steps.append(s)
        if ahead and n >= FIRST_MAX:
            until = MAX_TILES * (n - FIRST_MAX + 1) // (GROUPS - FIRST_MAX)
            for m in range(done, until):
                steps.append(("max", 1, m))
                if m % (MAX_TILES // 2) == MAX_TILES // 2 - 1:
                    steps.append(("shift", 1, m // (MAX_TILES // 2)))
            done = until
    return steps


FETCHES = 2 * 2 * PARTS + 2
LN_TILES = {"proj": 2 * QT, "ff2": QT, "ln3a": QT}


def adds(layer):
    both = {"misc": 1, "misc_free": 1}
    table = {
        "load": {"z_in": 16}, "loadx": {"x_in": 16},
        "exp": {"scores": 2, "probs": 2}, "sum": {"summed": 1}, "take": {"taken": 1},
        "norm": {**both, "dve": 1},
        "zT": both, "q": {**both, "split": 1, "pool": 2, "q_out": 16}, "k": {**both, "split": 1, "pool": 2, "k_out": 16},
        "v": both, "z": both, "fetch": {"strips": 16 * FETCHES},
        "max": {"max_in": 1, "max_out": 1}, "shift": {**both, "dve": 1, "shift_in": 64},
        "onT": both, "yT": {**both}, "ff1": both, "x2T": both, "logits": both,
        "proj": {**both, "dve": 1, "moments": 1, "rstd": 1, "pool": 1} if layer == 0 else both,
        "ln1": {"dve": 1, "centred": 1, "pool": 1, "y": 1, "yb": 1},
        "ff2": {**both, "dve": 1, "moments": 1, "rstd": 1, "pool": 1},
        "ln2": {"normed": 1, "pool": 1, "s": 1},
        "gather": {"picks": 1, "rows": 16 * QT * (1 if layer == 0 else TOP)},
        "gate": {"gate_in": 1, "gate_exp": 1, "gate_den": 1, "pool": 0 if layer == 0 else 1},
        "mix": {"dve": 1, "gate_out": 1, "pool": 1, "x2": 1, "x2_out": 16},
        "ln3a": {"dve": 1, "moments": 1, "rstd": 1, "pool": 1},
        "ln3b": {"xn2": 1, "xn2_out": 16},
    }
    return lambda step: table[step[0]]


def batches(eng, n, layer):
    for b in (-1, 0):
        yield b, b % 2, plan(layer, b)
    trips = (NB - 2) // 2
    with eng.Fori(0, trips) as trip:
        n.enter(trip, plan(layer, 1) + plan(layer, 2))
        for half in range(2):
            yield trip * 2 + 1 + half, (1 + half) % 2, plan(layer, 1 + half)
        n.leave(trips)
    for b in (NB - 1, NB):
        yield b, b % 2, plan(layer, b)


def of_batch(ap, b):
    if isinstance(b, int):
        return ap[b]
    return ap[bass.ds(b, 1)].rearrange("o p t d -> (o p) t d")


def attention(nc, layer, const, psum, dram, w, route, out):
    causal = layer == 1
    with ExitStack() as ctx:
        def sb(name, shape, dt=F32):
            return ctx.enter_context(nc.sbuf_tensor(f"a{layer}_{name}", shape, dt))

        sems = {k: ctx.enter_context(nc.semaphore(f"a{layer}_{k}")) for k in (
            "weights", "ready", "z_in", "x_in", "scores", "probs", "summed", "taken", "misc", "misc_free", "split",
            "q_out", "k_out", "strips", "max_in", "max_out", "shift_in", "moments", "rstd", "centred",
            "y", "yb", "normed", "s", "picks", "rows", "gate_in", "gate_exp", "gate_den", "gate_out",
            "x2", "x2_out", "xn2", "xn2_out", "dve", "pool", "apart")}
        ps_scores, ps_max, ps_sum, ps_misc = psum

        q_strip = [sb(f"q_strip{i}", [P, NG, S], BF16) for i in range(2)]
        k_strip = [sb(f"k_strip{i}", [P, H, S], BF16) for i in range(2)]
        v_aug = [sb(f"v_aug{i}", [P, QT, H, VW]) for i in range(2)]
        probs = [sb(f"probs{i}", [P, 4, S]) for i in range(2)]
        z_in, z_T = sb("z_in", [P, QT, D]), sb("z_T", [P, S])
        whole = {k: sb(f"{k}_whole", [P, S]) for k in "qk"}
        parts = {k: sb(f"{k}_parts", [P, 3, S], BF16) for k in "qk"}
        rest = {k: sb(f"{k}_rest", [P, S]) for k in "qk"}
        neg_max = sb("neg_max", [P, QT, 2, NG])
        shift = sb("shift", [NG, 2, S], BF16)
        fixed = sb("fixed", [3, NG * S], BF16)
        zeros = sb("zeros", [2, NG * S], BF16)
        o_strip = [sb(f"o_strip{i}", [P, S]) for i in range(2)]
        o_norm = [sb(f"o_norm{i}", [P, QT, D]) for i in range(2)]
        o_den = sb("o_den", [P, QT, 4])
        o_T = sb("o_T", [P, S])
        x_in, x2 = sb("x_in", [P, QT, D]), sb("x2", [P, QT, D])
        rows = [sb(f"rows{i}", [P, QT, D]) for i in range(1 if layer == 0 else TOP)]
        row_at = [sb(f"row_at{i}", [P, QT], U32) for i in range(len(rows))]
        row_w = [sb(f"row_w{i}", [P, QT]) for i in range(len(rows))]
        z, e, den, gz, s_out = (sb(k, [P, QT, D]) for k in ("z", "e", "den", "gz", "s_out"))
        wq, wk, wv, wo = (sb(k, [P, D]) for k in ("wq", "wk", "wv", "wo"))
        loads = [(wq, w["wq"]), (wk, w["wk"]), (wv, w["wv"]), (wo, w["wo"])]
        if layer == 0:
            resid = [sb(f"resid{i}", [P, QT, D]) for i in range(2)]
            y0, y1, y2, y3, y, yb, t0, t1, t2 = (sb(k, [P, QT, D]) for k in (
                "y0", "y1", "y2", "y3", "y", "yb", "t0", "t1", "t2"))
            y_T, hid = sb("y_T", [P, S]), sb("hid", [P, FC0, S])
            xn2, xn2_T = sb("xn2", [P, QT, D]), sb("xn2_T", [P, S])
            stats, moments = sb("stats", [P, 2 * QT, 6]), sb("moments", [P, 2 * QT, 2])
            veps, rstd = sb("veps", [P, 2 * QT]), sb("rstd", [P, 2 * QT])
            bq, bk, bqs = sb("bq", [P, 1]), sb("bk", [P, 1]), sb("bqs", [P, 1])
            w_ff1, w_ff2, b_ff1 = sb("w_ff1", [P, F0]), sb("w_ff2", [P, FC0, D]), sb("b_ff1", [P, FC0])
            bv, bo, g12, be12, b_ff2, g_ff, be_ff = (sb(k, [P, D]) for k in (
                "bv", "bo", "g12", "be12", "b_ff2", "g_ff", "be_ff"))
            wg, bg = sb("wg", [P, E1]), sb("bg", [P, E1])
            loads += [(bq, w["bq"]), (bk, w["bk"]), (w_ff1, w["w_ff1"]), (w_ff2, w["w_ff2"]), (b_ff1, w["b_ff1"]),
                      (wg, w["gate_w1"]), (bg, w["gate_b1"].partition_broadcast(P))]
            loads += [(t, w[k].partition_broadcast(P)) for t, k in (
                (bv, "bv"), (bo, "bo"), (g12, "g12"), (be12, "be12"), (b_ff2, "b_ff2"), (g_ff, "g_ff"), (be_ff, "be_ff"))]
        else:
            pos = sb("pos", [H, S])
            pos_parts, pos_rest = sb("pos_parts", [H, 3, S], BF16), sb("pos_rest", [H, S])
            loads.append((pos, w["alibi"]))
        n_loads = len(loads)
        fixed_dmas = 2 * 2 * 2 + (2 * 2 * 3 if causal else 0)

        ident, ident_bf = const["ident"], const["ident_bf"]
        tiles = "(b t p) d -> b p t d"
        z_src = (dram["xn"] if layer == 0 else dram["xn2"]).rearrange(tiles, b=NB, p=P)
        x_src = (dram["x"] if layer == 0 else dram["x2"]).rearrange(tiles, b=NB, p=P)
        x_dst = (dram["x2"] if layer == 0 else out).rearrange(tiles, b=NB, p=P)
        xn_dst = dram["xn2"].rearrange(tiles, b=NB, p=P)

        def cols(kt):
            return (kt * P if causal else 0), S

        def keys(qt):
            return (qt + 1) * P if causal else S

        def head(m):
            half, r = divmod(m, MAX_TILES // 2)
            hd, qt = divmod(r, QT)
            return half, hd % 2, hd // 2, qt

        with nc.Block() as block:

            @block.sync
            def _(sp):
                n = Tally(adds(layer))
                for dst, src in loads:
                    sp.dma_start(dst[:], src).then_inc(sems["weights"], 16)
                wait(sp, sems["ready"], 9)
                for i in range(2):
                    for j in range(2):
                        r = STRIP * j
                        sp.dma_start(k_strip[i][r + ROW_SHIFT:r + ROW_SHIFT + 2, NG * j:NG * (j + 1), :],
                                     fixed[0:2, :]).then_inc(sems["weights"], 16)
                        sp.dma_start(q_strip[i][r + ROW_ALIBI:r + ROW_END, :, :], fixed[:, :]).then_inc(sems["weights"], 16)
                        for a in range(3 if causal else 0):
                            sp.dma_start(k_strip[i][r + ROW_ALIBI + a:r + ROW_ALIBI + a + 1, NG * j:NG * (j + 1), :],
                                         pos_parts[NG * j:NG * (j + 1), a, :]).then_inc(sems["weights"], 16)
                for b, odd, steps in batches(sp, n, layer):
                    for step in steps:
                        name, d, arg = step
                        par = (odd + d) % 2
                        if name == "load":
                            wait(sp, sems["misc_free"], n.at("misc_free"))
                            sp.dma_start(z_in[:], of_batch(z_src, b + d)).then_inc(sems["z_in"], 16)
                        if name == "loadx":
                            wait(sp, sems["x2"], n.at("x2"))
                            sp.dma_start(x_in[:], of_batch(x_src, b + d)).then_inc(sems["x_in"], 16)
                        if name in ("q", "k"):
                            wait(sp, sems["split"], n.at("split") + 1)
                            sp.dma_start(dram[name].rearrange("a p n -> p a n"),
                                         parts[name][:]).then_inc(sems[f"{name}_out"], 16)
                        if name == "fetch":
                            wait_apart(sp, sems["q_out"], n.at("q_out"), sems["apart"])
                            wait_apart(sp, sems["k_out"], n.at("k_out"), sems["apart"])
                            wait(sp, sems["scores"], n.at("scores"))
                            for j in range(2):
                                r = STRIP * j
                                for a in range(PARTS):
                                    at = slice(r + HD * a, r + HD * (a + 1))
                                    for k, strip, slots, order in (("q", q_strip, slice(0, NG), (0, 0, 0, 1, 1, 2)),
                                                                   ("k", k_strip, slice(NG * j, NG * (j + 1)), (0, 1, 2, 0, 1, 0))):
                                        src = dram[k].rearrange("a (g j d) n -> j a d g n", j=2, d=HD)
                                        sp.dma_start(strip[par][at, slots, :], src[j, order[a]]).then_inc(sems["strips"], 16)
                                sp.dma_start(q_strip[par][r + ROW_SHIFT:r + ROW_SHIFT + 2, :, :],
                                             zeros[:, :]).then_inc(sems["strips"], 16)
                        if name == "shift":
                            wait(sp, sems["misc_free"], n.at("misc_free") + 1)
                            for j in range(2):
                                for a in range(2):
                                    r = STRIP * j + ROW_SHIFT + a
                                    sp.dma_start(q_strip[par][r:r + 1, arg * QT:(arg + 1) * QT, :],
                                                 shift[j * QT:(j + 1) * QT, a, :]).then_inc(sems["shift_in"], 16)
                        if name == "mix":
                            wait(sp, sems["x2"], n.at("x2") + 1)
                            sp.dma_start(of_batch(x_dst, b + d), x2[:]).then_inc(sems["x2_out"], 16)
                        if name == "ln3b":
                            wait(sp, sems["xn2"], n.at("xn2") + 1)
                            sp.dma_start(of_batch(xn_dst, b + d), xn2[:]).then_inc(sems["xn2_out"], 16)
                        n.step(step)
                wait(sp, sems["x2_out"], n.at("x2_out"))
                wait(sp, sems["xn2_out"], n.at("xn2_out"))

            @block.tensor
            def _(pe):
                n = Tally(adds(layer))
                wait(pe, sems["weights"], 16 * (n_loads + fixed_dmas))
                wait(pe, sems["ready"], 9)

                def claim():
                    wait(pe, sems["misc_free"], n.at("misc_free"))

                for b, odd, steps in batches(pe, n, layer):
                    for step in steps:
                        name, d, arg = step
                        par = (odd + d) % 2
                        if name == "exp":
                            u, kt = divmod(arg, QT)
                            lo, hi = cols(kt)
                            if arg == 0:
                                wait(pe, sems["shift_in"], n.at("shift_in") - 64)
                            if arg == QT:
                                wait(pe, sems["shift_in"], n.at("shift_in"))
                            for g in range(2):
                                slot = 2 * u + g
                                wait(pe, sems["probs"], n.at("probs") + g - 1)
                                for j in range(2):
                                    o = ps_scores[:, 2 * g + j, 0:hi - lo]
                                    mm = pe.matmul(o, k_strip[par][:, NG * j + slot, kt * P:(kt + 1) * P],
                                                   q_strip[par][:, slot, lo:hi], start=True, stop=not causal)
                                    if causal:
                                        mm = pe.matmul(ps_scores[:, 2 * g + j, 0:P], ident_bf[:], const["mask_kq"][:],
                                                       start=False, stop=True)
                                mm.then_inc(sems["scores"], 1)
                        if name == "sum":
                            group, more = arg
                            u, kt = divmod(group, QT)
                            lo, hi = cols(kt)
                            wait(pe, sems["probs"], n.at("probs") - (2 if more else 0))
                            if kt == 0:
                                wait(pe, sems["taken"], n.at("taken"))
                            for c in range(4):
                                mm = pe.matmul(ps_sum[VW * c:VW * (c + 1), lo:hi], v_aug[par][:, kt, 4 * u + c, :],
                                               probs[group % 2][:, c, 0:hi - lo], start=kt == 0, stop=kt == QT - 1)
                            mm.then_inc(sems["summed"], 1)
                        if name == "norm":
                            wait(pe, sems["taken"], n.at("taken"))
                            claim()
                            for t in range(QT):
                                mm = pe.transpose(ps_misc[:, t * P:(t + 1) * P], o_strip[arg % 2][:, t * P:(t + 1) * P], ident[:])
                            mm.then_inc(sems["misc"], 1)
                        if name == "zT":
                            wait(pe, sems["z_in"], n.at("z_in"))
                            wait_apart(pe, sems["misc_free"], n.at("misc_free"), sems["apart"])
                            if layer == 0:
                                for t in range(QT):
                                    pe.transpose(ps_misc[0:HALF, t * P:(t + 1) * P], z_in[:, t, 0:HALF], ident[:])
                                for t in range(QT):
                                    mm = pe.matmul(ps_misc[HALF:P, t * P:S], z_in[:, t, 0:HALF],
                                                   const["holt"][:, holt_block(t, t) * P:(holt_block(t, QT - 1) + 1) * P],
                                                   start=t == 0, stop=t == QT - 1)
                            else:
                                for t in range(QT):
                                    mm = pe.transpose(ps_misc[:, t * P:(t + 1) * P], z_in[:, t, :], ident[:])
                            mm.then_inc(sems["misc"], 1)
                        if name in ("q", "k"):
                            claim()
                            pe.matmul(ps_misc[:], (wq if name == "q" else wk)[:], z_T[:], start=True, stop=True).then_inc(sems["misc"], 1)
                        if name in ("v", "z"):
                            claim()
                            for t in range(QT):
                                o, i = ps_misc[:, t * P:(t + 1) * P], z_T[:, t * P:(t + 1) * P]
                                mm = pe.matmul(o, i, wv[:], start=True, stop=True) if name == "v" else pe.transpose(o, i, ident[:])
                            mm.then_inc(sems["misc"], 1)
                        if name == "max":
                            if arg == 0:
                                wait(pe, sems["strips"], n.at("strips"))
                            half, j, slot, qt = head(arg)
                            slot += QT * half
                            wait(pe, sems["max_out"], n.at("max_out") - 1)
                            o = ps_max[:, arg % 2, 0:keys(qt)]
                            mm = pe.matmul(o, q_strip[par][:, slot, qt * P:(qt + 1) * P], k_strip[par][:, NG * j + slot, 0:keys(qt)],
                                           start=True, stop=not causal)
                            if causal:
                                mm = pe.matmul(ps_max[:, arg % 2, qt * P:(qt + 1) * P], ident_bf[:], const["mask_qk"][:],
                                               start=False, stop=True)
                            mm.then_inc(sems["max_in"], 1)
                        if name == "shift":
                            wait(pe, sems["max_out"], n.at("max_out"))
                            claim()
                            for t in range(QT):
                                mm = pe.transpose(ps_misc[0:NG, t * P:(t + 1) * P], neg_max[:, t, arg, :], ident[:])
                            mm.then_inc(sems["misc"], 1)
                        if name == "onT":
                            claim()
                            for t in range(QT):
                                mm = pe.transpose(ps_misc[:, t * P:(t + 1) * P], o_norm[par][:, t, :], ident[:])
                            mm.then_inc(sems["misc"], 1)
                        if name == "proj":
                            claim()
                            for t in range(QT):
                                mm = pe.matmul(ps_misc[:, t * P:(t + 1) * P], o_T[:, t * P:(t + 1) * P], wo[:], start=True, stop=True)
                            mm.then_inc(sems["misc"], 1)
                        if name == "yT":
                            wait(pe, sems["y"], n.at("y"))
                            claim()
                            for t in range(QT):
                                mm = pe.transpose(ps_misc[:, t * P:(t + 1) * P], y[:, t, :], ident[:])
                            mm.then_inc(sems["misc"], 1)
                        if name == "ff1":
                            claim()
                            pe.matmul(ps_misc[:], w_ff1[:, arg * P:(arg + 1) * P], y_T[:], start=True, stop=True).then_inc(sems["misc"], 1)
                        if name == "ff2":
                            claim()
                            for t in range(QT):
                                for c in range(FC0):
                                    mm = pe.matmul(ps_misc[:, t * P:(t + 1) * P], hid[:, c, t * P:(t + 1) * P], w_ff2[:, c, :],
                                                   start=c == 0, stop=c == FC0 - 1)
                            mm.then_inc(sems["misc"], 1)
                        if name == "x2T":
                            wait(pe, sems["xn2"], n.at("xn2"))
                            claim()
                            for t in range(QT):
                                mm = pe.transpose(ps_misc[:, t * P:(t + 1) * P], xn2[:, t, :], ident[:])
                            mm.then_inc(sems["misc"], 1)
                        if name == "logits":
                            claim()
                            for t in range(QT):
                                mm = pe.matmul(ps_misc[:, t * E1:(t + 1) * E1], xn2_T[:, t * P:(t + 1) * P], wg[:], start=True, stop=True)
                            mm.then_inc(sems["misc"], 1)
                        n.step(step)

            @block.scalar
            def _(act):
                n = Tally(adds(layer))
                wait(act, sems["weights"], 16 * n_loads)
                wait(act, sems["ready"], 9)
                for b, odd, steps in batches(act, n, layer):
                    for step in steps:
                        name, d, arg = step
                        if name == "exp":
                            lo, hi = cols(arg % QT)
                            wait(act, sems["summed"], n.at("summed"))
                            for g in range(2):
                                wait(act, sems["scores"], n.at("scores") + 1 + g)
                                act.activation(probs[arg % 2][:, 2 * g:2 * g + 2, 0:hi - lo], ps_scores[:, 2 * g:2 * g + 2, 0:hi - lo],
                                               ACT.Exp).then_inc(sems["probs"], 1)
                        if name in ("zT", "onT", "yT", "x2T"):
                            wait(act, sems["misc"], n.at("misc") + 1)
                            dst = {"zT": z_T, "onT": o_T}[name] if name in ("zT", "onT") else (y_T if name == "yT" else xn2_T)
                            act.activation(dst[:], ps_misc[:], ACT.Copy).then_inc(sems["misc_free"], 1)
                        if name in ("q", "k"):
                            wait(act, sems["misc"], n.at("misc") + 1)
                            wait(act, sems[f"{name}_out"], n.at(f"{name}_out"))
                            scale = SCALE if name == "q" else 1.0
                            bias = 0.0 if causal else (bqs if name == "q" else bk)[:, 0:1]
                            act.activation(parts[name][:, 0, :], ps_misc[:], ACT.Identity, bias=bias, scale=scale)
                            act.activation(whole[name][:], ps_misc[:], ACT.Identity, bias=bias, scale=scale).then_inc(sems["misc_free"], 1)
                        if name == "ff1":
                            wait(act, sems["misc"], n.at("misc") + 1)
                            act.activation(hid[:, arg, :], ps_misc[:], ACT.Relu, bias=b_ff1[:, arg:arg + 1]).then_inc(sems["misc_free"], 1)
                        if name == "proj" and layer == 1:
                            wait(act, sems["misc"], n.at("misc") + 1)
                            wait(act, sems["x2"], n.at("x2"))
                            act.activation(s_out[:].rearrange("p t d -> p (t d)"), ps_misc[:], ACT.Copy).then_inc(sems["misc_free"], 1)
                        if name == "gate":
                            wait(act, sems["gate_in"], n.at("gate_in") + 1)
                            act.activation(e[:], z[:], ACT.Exp, scale=-1.0).then_inc(sems["gate_exp"], 1)
                        n.step(step)

            @block.vector
            def _(dve):
                n = Tally(adds(layer))
                dve.memset(q_strip[0][:], 0.0).then_inc(sems["ready"], 1)
                dve.memset(q_strip[1][:], 0.0).then_inc(sems["ready"], 1)
                for i in range(2):
                    dve.memset(v_aug[i][:], 0.0).then_inc(sems["dve"], 1)
                wait(dve, sems["dve"], 2)
                for i in range(2):
                    dve.memset(v_aug[i][:, :, :, HD:HD + 1], 1.0).then_inc(sems["ready"], 1)
                dve.memset(fixed[:], 1.0).then_inc(sems["ready"], 1)
                wait(dve, sems["weights"], 16 * n_loads)
                if layer == 0:
                    dve.tensor_scalar(bqs[:], bq[:], SCALE, None, ALU.mult).then_inc(sems["ready"], 1)
                    n.n["dve"] = 2
                else:
                    dve.tensor_copy(pos_parts[:, 0, :], pos[:]).then_inc(sems["dve"], 1)
                    wait(dve, sems["dve"], 3)
                    dve.tensor_tensor(pos_rest[:], pos[:], pos_parts[:, 0, :], ALU.subtract).then_inc(sems["dve"], 1)
                    wait(dve, sems["dve"], 4)
                    dve.tensor_copy(pos_parts[:, 1, :], pos_rest[:]).then_inc(sems["dve"], 1)
                    wait(dve, sems["dve"], 5)
                    dve.tensor_tensor(pos_parts[:, 2, :], pos_rest[:], pos_parts[:, 1, :], ALU.subtract).then_inc(sems["ready"], 1)
                    n.n["dve"] = 5
                wait(dve, sems["ready"], 9)
                linked = [0]

                def link(op):
                    linked[0] += 1
                    op.then_inc(sems["dve"], 1)
                    wait_apart(dve, sems["dve"], n.at("dve") + linked[0], sems["apart"])

                def moments_of(src, width, count):
                    v = src[:].rearrange("p t d -> p (t d)")
                    for i in range(count):
                        op = dve.bn_stats(stats[:, i, :], v[:, i * width:(i + 1) * width])
                    link(op)
                    for i in range(count):
                        op = dve.bn_aggr(moments[:, i, :], stats[:, i, :])
                    op.then_inc(sems["moments"], 1)

                for b, odd, steps in batches(dve, n, layer):
                    for step in steps:
                        name, d, arg = step
                        par = (odd + d) % 2
                        linked[0] = 0
                        if name == "max":
                            half, j, slot, qt = head(arg)
                            wait(dve, sems["max_in"], n.at("max_in") + 1)
                            dve.tensor_reduce(neg_max[:, qt, half, j * QT + slot:j * QT + slot + 1], ps_max[:, arg % 2, 0:keys(qt)],
                                              AX.X, ALU.max, negate=True).then_inc(sems["max_out"], 1)
                        if name == "shift":
                            wait(dve, sems["misc"], n.at("misc") + 1)
                            wait(dve, sems["shift_in"], n.at("shift_in"))
                            link(dve.tensor_copy(shift[:, 0, :], ps_misc[0:NG, :]))
                            dve.tensor_tensor(shift[:, 1, :], ps_misc[0:NG, :], shift[:, 0, :], ALU.subtract).then_inc(sems["misc_free"], 1)
                        if name == "take":
                            wait(dve, sems["summed"], n.at("summed"))
                            dve.tensor_copy(o_strip[arg % 2][:], ps_sum[:]).then_inc(sems["taken"], 1)
                        if name == "norm":
                            wait(dve, sems["misc"], n.at("misc") + 1)
                            v = ps_misc[:].rearrange("p (t c v) -> p t c v", t=QT, c=4)
                            link(dve.reciprocal(o_den[:], v[:, :, :, HD]))
                            o = o_norm[par][:, :, 4 * HD * arg:4 * HD * (arg + 1)].rearrange("p t (c v) -> p t c v", c=4)
                            dve.tensor_tensor(o, v[:, :, :, 0:HD], o_den[:].unsqueeze(3).broadcast_to([P, QT, 4, HD]),
                                              ALU.mult).then_inc(sems["misc_free"], 1)
                        if name == "v":
                            wait(dve, sems["misc"], n.at("misc") + 1)
                            wait(dve, sems["summed"], n.at("summed"))
                            dst = v_aug[par][:, :, :, 0:HD]
                            src = ps_misc[:].rearrange("p (t h v) -> p t h v", t=QT, h=H)
                            if layer == 0:
                                for t in range(QT):
                                    op = dve.tensor_tensor(dst[:, t], src[:, t], bv[:].rearrange("p (h v) -> p h v", h=H), ALU.add)
                            else:
                                op = dve.tensor_copy(dst, src)
                            op.then_inc(sems["misc_free"], 1)
                        if name == "z":
                            wait(dve, sems["misc"], n.at("misc") + 1)
                            dve.tensor_tensor(resid[par][:], ps_misc[:].rearrange("p (t d) -> p t d", t=QT),
                                              bo[:].unsqueeze(1).broadcast_to([P, QT, D]), ALU.add).then_inc(sems["misc_free"], 1)
                        if name == "proj" and layer == 0:
                            wait(dve, sems["misc"], n.at("misc") + 1)
                            dve.tensor_tensor(y0[:], ps_misc[:].rearrange("p (t d) -> p t d", t=QT), resid[par][:],
                                              ALU.add).then_inc(sems["misc_free"], 1)
                            wait(dve, sems["misc_free"], n.at("misc_free") + 1)
                            moments_of(y0, HALF, 2 * QT)
                        if name == "ln1":
                            wait(dve, sems["rstd"], n.at("rstd"))
                            halves = "p t (a d) -> p (t a) d"
                            link(dve.tensor_tensor(y1[:].rearrange(halves, a=2), y0[:].rearrange(halves, a=2),
                                                   moments[:, :, 0:1].broadcast_to([P, 2 * QT, HALF]), ALU.subtract))
                            dve.tensor_tensor(y2[:].rearrange(halves, a=2), y1[:].rearrange(halves, a=2),
                                              rstd[:].unsqueeze(2).broadcast_to([P, 2 * QT, HALF]), ALU.mult).then_inc(sems["centred"], 1)
                        if name == "ff2":
                            wait(dve, sems["misc"], n.at("misc") + 1)
                            wait(dve, sems["yb"], n.at("yb"))
                            dve.tensor_tensor(t0[:], ps_misc[:].rearrange("p (t d) -> p t d", t=QT), yb[:],
                                              ALU.add).then_inc(sems["misc_free"], 1)
                            wait(dve, sems["misc_free"], n.at("misc_free") + 1)
                            moments_of(t0, D, QT)
                        if name == "ln2":
                            wait(dve, sems["rstd"], n.at("rstd"))
                            for t in range(QT):
                                op = dve.tensor_scalar(t1[:, t, :], t0[:, t, :], moments[:, t, 0:1], rstd[:, t:t + 1], ALU.subtract, ALU.mult)
                            op.then_inc(sems["normed"], 1)
                        if name == "gather":
                            wait(dve, sems["rows"], n.at("rows"))
                            wait(dve, sems["gate_in"], n.at("gate_in"))
                            at = slice(QT * (b + d), QT * (b + d + 1)) if isinstance(b, int) else bass.ds((b + d) * QT, QT)
                            for i in range(len(rows)):
                                dve.tensor_copy(row_at[i][:], route["at"][i][:, at])
                                op = dve.tensor_copy(row_w[i][:], route["weight"][i][:, at])
                            op.then_inc(sems["picks"], 1)
                        if name == "mix":
                            wait(dve, sems["gate_den"], n.at("gate_den"))
                            link(dve.reciprocal(e[:], den[:]))
                            dve.tensor_tensor(gz[:], z[:], e[:], ALU.mult).then_inc(sems["gate_out"], 1)
                        if name == "ln3a":
                            wait(dve, sems["x2"], n.at("x2"))
                            moments_of(x2, D, QT)
                        if name == "ln3b":
                            wait(dve, sems["rstd"], n.at("rstd"))
                            wait(dve, sems["xn2_out"], n.at("xn2_out"))
                            for t in range(QT):
                                op = dve.tensor_scalar(xn2[:, t, :], x2[:, t, :], moments[:, t, 0:1], rstd[:, t:t + 1], ALU.subtract, ALU.mult)
                            op.then_inc(sems["xn2"], 1)
                        if name == "logits":
                            wait(dve, sems["misc"], n.at("misc") + 1)
                            at = slice(QT * (b + d), QT * (b + d + 1)) if isinstance(b, int) else bass.ds((b + d) * QT, QT)
                            dve.tensor_tensor(route["logits"][:, at, :], ps_misc[:, 0:QT * E1].rearrange("p (t e) -> p t e", t=QT),
                                              bg[:].unsqueeze(1).broadcast_to([P, QT, E1]), ALU.add).then_inc(sems["misc_free"], 1)
                        assert linked[0] == n.adds(step).get("dve", 0), (step, linked[0])
                        n.step(step)

            @block.gpsimd
            def _(pool):
                n = Tally(adds(layer))
                pool.memset(k_strip[0][:], 0.0).then_inc(sems["ready"], 1)
                pool.memset(k_strip[1][:], 0.0).then_inc(sems["ready"], 1)
                pool.memset(zeros[:], 0.0).then_inc(sems["ready"], 1)
                wait(pool, sems["weights"], 16 * n_loads)
                linked = [0]

                def link(op):
                    linked[0] += 1
                    op.then_inc(sems["pool"], 1)
                    wait_apart(pool, sems["pool"], n.at("pool") + linked[0], sems["apart"])

                def inverse_deviation(count):
                    wait_apart(pool, sems["moments"], n.at("moments") + 1, sems["apart"])
                    link(pool.tensor_scalar(veps[:, 0:count], moments[:, 0:count, 1], EPS, None, ALU.add))
                    pool.tensor_tensor(rstd[:, 0:count], veps[:, 0:count], const["minus_half"][:, 0:count], ALU.pow).then_inc(sems["rstd"], 1)

                def bcast(t):
                    return t[:].unsqueeze(1).broadcast_to([P, QT, D])

                for b, odd, steps in batches(pool, n, layer):
                    for step in steps:
                        name, d, arg = step
                        linked[0] = 0
                        if name in ("q", "k"):
                            wait(pool, sems["misc_free"], n.at("misc_free") + 1)
                            a, full, r = parts[name], whole[name], rest[name]
                            link(pool.tensor_tensor(r[:], full[:], a[:, 0, :], ALU.subtract))
                            link(pool.tensor_copy(a[:, 1, :], r[:]))
                            pool.tensor_tensor(a[:, 2, :], r[:], a[:, 1, :], ALU.subtract).then_inc(sems["split"], 1)
                        if name in LN_TILES and layer == 0:
                            inverse_deviation(LN_TILES[name])
                        if name == "ln1":
                            wait(pool, sems["centred"], n.at("centred") + 1)
                            link(pool.tensor_tensor(y3[:], y2[:], bcast(g12), ALU.mult))
                            pool.tensor_tensor(y[:], y3[:], bcast(be12), ALU.add).then_inc(sems["y"], 1)
                            wait(pool, sems["y"], n.at("y") + 1)
                            pool.tensor_tensor(yb[:], y[:], bcast(b_ff2), ALU.add).then_inc(sems["yb"], 1)
                        if name == "ln2":
                            wait(pool, sems["normed"], n.at("normed") + 1)
                            link(pool.tensor_tensor(t2[:], t1[:], bcast(g_ff), ALU.mult))
                            pool.tensor_tensor(s_out[:], t2[:], bcast(be_ff), ALU.add).then_inc(sems["s"], 1)
                        if name == "gather":
                            if layer == 1:
                                wait(pool, sems["x2"], n.at("x2"))
                            wait_apart(pool, sems["picks"], n.at("picks") + 1, sems["apart"])
                            for i in range(len(rows)):
                                for t in range(QT):
                                    pool.indirect_dma_start(rows[i][:, t, :], None, dram["moe"],
                                                            bass.IndirectOffsetOnAxis(ap=row_at[i][:, t:t + 1], axis=0)
                                                            ).then_inc(sems["rows"], 16)
                        if name == "gate":
                            wait(pool, sems["rows"], n.at("rows"))
                            per = lambda i: row_w[i][:].unsqueeze(2).broadcast_to([P, QT, D])
                            if layer == 0:
                                pool.tensor_tensor(z[:], rows[0][:], per(0), ALU.mult).then_inc(sems["gate_in"], 1)
                            else:
                                pool.tensor_tensor(den[:], rows[0][:], per(0), ALU.mult)
                                link(pool.tensor_tensor(gz[:], rows[1][:], per(1), ALU.mult))
                                pool.tensor_tensor(z[:], den[:], gz[:], ALU.add).then_inc(sems["gate_in"], 1)
                            wait_apart(pool, sems["gate_exp"], n.at("gate_exp") + 1, sems["apart"])
                            pool.tensor_scalar(den[:], e[:], 1.0, None, ALU.add).then_inc(sems["gate_den"], 1)
                        if name == "mix":
                            wait(pool, sems["gate_out"], n.at("gate_out") + 1)
                            wait(pool, sems["x_in"], n.at("x_in"))
                            wait(pool, sems["x2_out"], n.at("x2_out"))
                            if layer == 0:
                                wait(pool, sems["s"], n.at("s"))
                            else:
                                wait(pool, sems["misc_free"], n.at("misc_free"))
                            link(pool.tensor_tensor(t1[:] if layer == 0 else rows[0][:], gz[:], s_out[:], ALU.mult))
                            pool.tensor_tensor(x2[:], t1[:] if layer == 0 else rows[0][:], x_in[:], ALU.add).then_inc(sems["x2"], 1)
                        assert linked[0] == n.adds(step).get("pool", 0), (step, linked[0])
                        n.step(step)


def first_best(dve, link, logits, experts, number, best, flag, first, onehot):
    def per(t):
        return t[:].unsqueeze(2).broadcast_to([P, NT, experts])
    numbers = number.unsqueeze(1).broadcast_to([P, NT, experts])
    link(dve.tensor_reduce(best[:], logits, AX.X, ALU.max))
    link(dve.tensor_tensor(flag[:], logits, per(best), ALU.is_ge))
    link(dve.tensor_tensor(flag[:], flag[:], numbers, ALU.mult))
    link(dve.tensor_reduce(first[:], flag[:], AX.X, ALU.min))
    link(dve.tensor_tensor(onehot[:], numbers, per(first), ALU.is_equal))


def places(dve, link, before, totals, run, pos):
    link(dve.tensor_copy(run[0][:], totals))
    a, b, k = 0, 1, 1
    while k < NT:
        dve.tensor_copy(run[b][:, 0:k, :], run[a][:, 0:k, :])
        link(dve.tensor_tensor(run[b][:, k:NT, :], run[a][:, k:NT, :], run[a][:, 0:NT - k, :], ALU.add))
        a, b, k = b, a, 2 * k
    link(dve.tensor_tensor(pos[:], run[a][:], totals, ALU.subtract))
    link(dve.tensor_tensor(pos[:], pos[:], before, ALU.add))
    return run[a]


def experts0(nc, const, psum, dram, w, route):
    with ExitStack() as ctx:
        def sb(name, shape, dt=F32):
            return ctx.enter_context(nc.sbuf_tensor(f"m0_{name}", shape, dt))

        names = ("consts", "const", "x_in0", "x_in1", "moments", "rstd", "xn", "xn_out0", "xn_out1", "xT", "xnT", "scored", "logits",
                 "zeroed", "chosen", "counted", "shifted", "exped", "slots", "all_in", "sent", "w_in0", "w_in1", "rows_in0",
                 "rows_in1", "rowsT", "rowsT_out", "hidden", "hidden_out", "made", "made_out", "stored0", "stored1", "dve", "pool", "apart")
        sems = {k: ctx.enter_context(nc.semaphore(f"m0_{k}")) for k in names}
        ps_scores, ps_max, ps_sum, ps_misc = psum
        x_in = [sb(f"x_in{i}", [P, QT, D]) for i in range(2)]
        xn = [sb(f"xn{i}", [P, QT, D]) for i in range(2)]
        xn_T = [sb(f"xn_T{i}", [P, S]) for i in range(2)]
        stats, moments = sb("stats", [P, QT, 6]), [sb(f"moments{i}", [P, QT, 2]) for i in range(2)]
        veps, rstd = sb("veps", [P, QT]), [sb(f"rstd{i}", [P, QT]) for i in range(2)]
        wg = sb("wg", [P, E0])
        logits, shifted, exped, flag, onehot, pos = (sb(k, [P, NT, E0]) for k in ("logits", "shifted", "exped", "flag", "onehot", "pos"))
        run = [sb(f"run{i}", [P, NT, E0]) for i in range(2)]
        onehot_bf = sb("onehot_bf", [P, NT, E0], BF16)
        best, first, loc, start, valid, slot, send = (sb(k, [P, NT]) for k in ("best", "first", "loc", "start", "valid", "slot", "send"))
        send_at = sb("send_at", [P, NT], U32)
        xn_all = sb("xn_all", [P, NT, D])
        zero = sb("zero", [P, 1024])
        w1 = [sb(f"w1{i}", [P, F0]) for i in range(2)]
        w2 = [sb(f"w2{i}", [P, FC0, D]) for i in range(2)]
        CT = CAP // P
        rows = [sb(f"rows{i}", [P, CT, D]) for i in range(2)]
        rows_T = [sb(f"rows_T{i}", [P, CAP]) for i in range(2)]
        hid = [sb(f"hid{i}", [P, FC0, CAP]) for i in range(2)]
        made = [sb(f"made{i}", [P, CT, D]) for i in range(2)]

        tiles = "(b t p) d -> b p t d"
        x_src = dram["x"].rearrange(tiles, b=NB, p=P)
        xn_dst = dram["xn"].rearrange(tiles, b=NB, p=P)
        rows_src = dram["sent0"][0:E0 * CAP, :].rearrange("(e t p) d -> e p t d", e=E0, p=P)
        made_dst = dram["made0"].rearrange("(e t p) d -> e p t d", e=E0, p=P)
        zero_dmas = [(dram[k][0:r, :], r) for k, r in (("sent0", E0 * CAP), ("sent1", TILES1 * P))]
        n_zero = sum(r // 1024 for _, r in zero_dmas)

        def one(ap, e):
            return ap[e] if isinstance(e, int) else ap[bass.ds(e, 1)].rearrange("o p t d -> (o p) t d")

        def one2(ap, e):
            return ap[e] if isinstance(e, int) else ap[bass.ds(e, 1)].rearrange("o p f -> (o p) f")

        with nc.Block() as block:

            @block.sync
            def _(sp):
                sp.dma_start(const["all"][:], w["consts"]).then_inc(sems["consts"], 16)
                for b in range(2):
                    sp.dma_start(x_in[b][:], x_src[b]).then_inc(sems[f"x_in{b}"], 16)
                sp.dma_start(wg[:], w["gate_w0"]).then_inc(sems["consts"], 16)

                def weights(e, par):
                    sp.dma_start(w1[par][:], one2(w["w1_0"], e)).then_inc(sems[f"w_in{par}"], 16)
                    sp.dma_start(w2[par][:], one(w["w2_0"].rearrange("e (c p) d -> e p c d", p=P), e)).then_inc(sems[f"w_in{par}"], 16)

                def store_xn(b, par):
                    sp.wait_ge(sems["xn"], b + 1)
                    sp.dma_start(of_batch(xn_dst, b), xn[par][:]).then_inc(sems[f"xn_out{par}"], 16)

                with sp.Fori(1, NB // 2) as i:
                    for par in range(2):
                        store_xn(i * 2 + par - 2, par)
                        sp.dma_start(x_in[par][:], of_batch(x_src, i * 2 + par)).then_inc(sems[f"x_in{par}"], 16)
                for par in range(2):
                    store_xn(NB - 2 + par, par)
                for e in range(2):
                    weights(e, e)
                sp.wait_ge(sems["const"], 3)
                for dst, r in zero_dmas:
                    v = dst.rearrange("(n p r) d -> n p (r d)", p=P, r=1024 // D)
                    for k in range(r // 1024):
                        sp.dma_start(v[k], zero[:]).then_inc(sems["zeroed"], 16)
                for par in range(2):
                    sp.wait_ge(sems[f"xn_out{par}"], 16 * (NB // 2 + 1))
                sp.dma_start(xn_all[:], dram["xn"].rearrange("(t p) d -> p t d", p=P)).then_inc(sems["all_in"], 16)
                sp.wait_ge(sems["sent"], 16 * NT)
                for e in range(2):
                    sp.dma_start(rows[e][:], rows_src[e]).then_inc(sems[f"rows_in{e}"], 16)
                def store_made(e, par):
                    sp.wait_ge(sems["made_out"], e + 3)
                    sp.dma_start(one(made_dst, e), made[par][:]).then_inc(sems[f"stored{par}"], 16)

                with sp.Fori(1, E0 // 2) as i:
                    for par in range(2):
                        store_made(i * 2 + par - 2, par)
                        weights(i * 2 + par, par)
                        sp.dma_start(rows[par][:], one(rows_src, i * 2 + par)).then_inc(sems[f"rows_in{par}"], 16)
                for par in range(2):
                    store_made(E0 - 2 + par, par)
                for par in range(2):
                    sp.wait_ge(sems[f"stored{par}"], 16 * (E0 // 2 + 1))

            @block.tensor
            def _(pe):
                pe.wait_ge(sems["consts"], 32)
                pe.wait_ge(sems["const"], 3)
                with pe.Fori(0, NB // 2) as i:
                    for par in range(2):
                        b = i * 2 + par
                        pe.wait_ge(sems["xn"], b + 1)
                        for t in range(QT):
                            mm = pe.transpose(ps_max[:, par, t * P:(t + 1) * P], xn[par][:, t, :], const["ident"])
                        mm.then_inc(sems["xT"], 1)
                        pe.wait_ge(sems["xnT"], b + 1)
                        for t in range(QT):
                            mm = pe.matmul(ps_scores[:, par, t * E0:(t + 1) * E0], xn_T[par][:, t * P:(t + 1) * P], wg[:], start=True, stop=True)
                        mm.then_inc(sems["scored"], 1)
                pe.wait_ge(sems["chosen"], 1)
                v = onehot_bf[:].rearrange("p t e -> p (t e)")
                pe.matmul(ps_sum[:], const["before"][:], v, start=True, stop=True)
                pe.matmul(ps_misc[:], const["ones"][:], v, start=True, stop=True).then_inc(sems["counted"], 1)
                pe.wait_ge(sems["slots"], 1)
                with pe.Fori(0, E0 // 2) as i:
                    for par in range(2):
                        e = i * 2 + par
                        pe.wait_ge(sems[f"rows_in{par}"], i * 16 + 16)
                        for t in range(CT):
                            mm = pe.transpose(ps_max[:, par, t * P:(t + 1) * P], rows[par][:, t, :], const["ident"])
                        mm.then_inc(sems["rowsT"], 1)
                        pe.wait_ge(sems[f"w_in{par}"], i * 32 + 32)
                        pe.wait_ge(sems["rowsT_out"], e + 1)
                        for c in range(FC0):
                            mm = pe.matmul(ps_scores[:, c, 0:CAP], w1[par][:, c * P:(c + 1) * P], rows_T[par][:], start=True, stop=True)
                            if c % 2 == 1:
                                mm.then_inc(sems["hidden"], 1)
                        pe.wait_ge(sems["hidden_out"], e * 2 + 2)
                        pe.wait_ge(sems["made_out"], e + 1)
                        bank = ps_sum if par == 0 else ps_misc
                        for t in range(CT):
                            for c in range(FC0):
                                mm = pe.matmul(bank[:, t * D:(t + 1) * D], hid[par][:, c, t * P:(t + 1) * P], w2[par][:, c, :],
                                               start=c == 0, stop=c == FC0 - 1)
                        mm.then_inc(sems["made"], 1)

            @block.scalar
            def _(act):
                with act.Fori(0, NB // 2) as i:
                    for par in range(2):
                        act.wait_ge(sems["xT"], i * 2 + par + 1)
                        act.activation(xn_T[par][:], ps_max[:, par, :], ACT.Copy).then_inc(sems["xnT"], 1)
                act.wait_ge(sems["shifted"], 1)
                act.activation(exped[:], shifted[:], ACT.Exp).then_inc(sems["exped"], 1)
                with act.Fori(0, E0 // 2) as i:
                    for par in range(2):
                        e = i * 2 + par
                        act.wait_ge(sems["rowsT"], e + 1)
                        act.activation(rows_T[par][:], ps_max[:, par, 0:CAP], ACT.Copy).then_inc(sems["rowsT_out"], 1)
                        act.wait_ge(sems["hidden"], e * 2 + 1)
                        act.activation(hid[par][:, 0:2, :], ps_scores[:, 0:2, 0:CAP], ACT.Relu).then_inc(sems["hidden_out"], 1)

            @block.vector
            def _(dve):
                linked = [0]

                def link(op):
                    linked[0] += 1
                    op.then_inc(sems["dve"], 1)
                    dve.wait_ge(sems["dve"], linked[0])

                dve.memset(zero[:], 0.0).then_inc(sems["const"], 1)
                link(dve.memset(const["ones"][:], 1.0))
                dve.memset(const["minus_half"][:], -0.5).then_inc(sems["const"], 1)
                dve.wait_ge(sems["consts"], 32)
                for k, at in (("ident_bf", C_IDENT), ("before", C_BEFORE), ("mask_qk", C_MASK_QK), ("mask_kq", C_MASK_KQ)):
                    op = dve.tensor_copy(const[k][:], const["all"][:, at:at + P])
                op.then_inc(sems["const"], 1)
                dve.sem_inc(sems["xn_out0"], 16)
                dve.sem_inc(sems["xn_out1"], 16)
                dve.sem_inc(sems["made_out"], 2)
                dve.sem_inc(sems["stored0"], 16)
                dve.sem_inc(sems["stored1"], 16)
                base = linked[0]
                with dve.Fori(0, NB // 2) as i:
                    for par in range(2):
                        b = i * 2 + par
                        dve.wait_ge(sems[f"x_in{par}"], i * 16 + 16)
                        for t in range(QT):
                            op = dve.bn_stats(stats[:, t, :], x_in[par][:, t, :])
                        op.then_inc(sems["dve"], 1)
                        wait_apart(dve, sems["dve"], b + base + 1, sems["apart"])
                        for t in range(QT):
                            op = dve.bn_aggr(moments[par][:, t, :], stats[:, t, :])
                        op.then_inc(sems["moments"], 1)
                        dve.wait_ge(sems["rstd"], b + 1)
                        dve.wait_ge(sems[f"xn_out{par}"], i * 16 + 16)
                        for t in range(QT):
                            op = dve.tensor_scalar(xn[par][:, t, :], x_in[par][:, t, :], moments[par][:, t, 0:1],
                                                   rstd[par][:, t:t + 1], ALU.subtract, ALU.mult)
                        op.then_inc(sems["xn"], 1)
                        dve.wait_ge(sems["scored"], b + 1)
                        dve.tensor_copy(logits[:, bass.ds(b * QT, QT), :],
                                        ps_scores[:, par, 0:QT * E0].rearrange("p (t e) -> p t e", t=QT)).then_inc(sems["logits"], 1)
                linked[0] += NB
                dve.wait_ge(sems["logits"], NB)
                number = const["all"][:, C_EXP0:C_EXP0 + E0]
                first_best(dve, link, logits[:], E0, number, best, flag, first, onehot)
                dve.tensor_copy(onehot_bf[:], onehot[:]).then_inc(sems["chosen"], 1)
                dve.tensor_tensor(shifted[:], logits[:], best[:].unsqueeze(2).broadcast_to([P, NT, E0]), ALU.subtract).then_inc(sems["shifted"], 1)
                dve.wait_ge(sems["counted"], 1)
                by = "p (t e) -> p t e"
                places(dve, link, ps_sum[:].rearrange(by, e=E0), ps_misc[:].rearrange(by, e=E0), run, pos)
                link(dve.tensor_tensor(pos[:], pos[:], onehot[:], ALU.mult))
                link(dve.tensor_reduce(loc[:], pos[:], AX.X, ALU.add))
                link(dve.tensor_scalar(start[:], first[:], float(E0), float(CAP), ALU.add, ALU.mult))
                link(dve.tensor_scalar(valid[:], loc[:], float(CAP), None, ALU.is_lt))
                link(dve.tensor_tensor(slot[:], start[:], loc[:], ALU.add))
                dump = const["all"][:, C_DUMP:C_DUMP + NT]
                link(dve.tensor_tensor(send[:], slot[:], dump, ALU.subtract))
                link(dve.tensor_tensor(send[:], send[:], valid[:], ALU.mult))
                link(dve.tensor_tensor(send[:], send[:], dump, ALU.add))
                dve.tensor_copy(send_at[:], send[:]).then_inc(sems["slots"], 1)
                link(dve.tensor_scalar(loc[:], loc[:], float(CAP - 1), None, ALU.min))
                link(dve.tensor_tensor(slot[:], start[:], loc[:], ALU.add))
                dve.tensor_copy(route["at"][0][:], slot[:])
                dve.wait_ge(sems["exped"], 1)
                link(dve.tensor_reduce(best[:], exped[:], AX.X, ALU.add))
                link(dve.reciprocal(first[:], best[:]))
                dve.tensor_tensor(route["weight"][0][:], first[:], valid[:], ALU.mult)
                with dve.Fori(0, E0 // 2) as i:
                    for par in range(2):
                        e = i * 2 + par
                        dve.wait_ge(sems["hidden"], e * 2 + 2)
                        dve.tensor_scalar(hid[par][:, 2:4, :], ps_scores[:, 2:4, 0:CAP], 0.0, None, ALU.max).then_inc(sems["hidden_out"], 1)
                        dve.wait_ge(sems["made"], e + 1)
                        dve.wait_ge(sems[f"stored{par}"], i * 16 + 16)
                        bank = ps_sum if par == 0 else ps_misc
                        dve.tensor_copy(made[par][:], bank[:, 0:CT * D].rearrange("p (t d) -> p t d", t=CT)).then_inc(sems["made_out"], 1)

            @block.gpsimd
            def _(pool):
                pool.wait_ge(sems["const"], 3)
                with pool.Fori(0, NB // 2) as i:
                    for par in range(2):
                        b = i * 2 + par
                        wait_apart(pool, sems["moments"], b + 1, sems["apart"])
                        pool.tensor_scalar(veps[:], moments[par][:, :, 1], EPS, None, ALU.add).then_inc(sems["pool"], 1)
                        pool.wait_ge(sems["pool"], b + 1)
                        pool.tensor_tensor(rstd[par][:], veps[:], const["minus_half"][:, 0:QT], ALU.pow).then_inc(sems["rstd"], 1)
                pool.wait_ge(sems["zeroed"], 16 * n_zero)
                pool.wait_ge(sems["all_in"], 16)
                pool.wait_ge(sems["slots"], 1)
                for t in range(NT):
                    pool.indirect_dma_start(dram["sent0"], bass.IndirectOffsetOnAxis(ap=send_at[:, t:t + 1], axis=0),
                                            xn_all[:, t, :], None).then_inc(sems["sent"], 16)


def experts1(nc, const, psum, dram, w, route):
    with ExitStack() as ctx:
        def sb(name, shape, dt=F32):
            return ctx.enter_context(nc.sbuf_tensor(f"m1_{name}", shape, dt))

        names = ("chosen", "counted", "gap", "gap_exp", "slots", "tiles", "all_in", "sent", "pack_in0", "pack_in1", "rows_in0", "rows_in1",
                 "rowsT", "rowsT_out", "hidden", "silu", "hidden_out", "made", "made_out", "stored0", "stored1", "dve")
        sems = {k: ctx.enter_context(nc.semaphore(f"m1_{k}")) for k in names}
        ps_scores, ps_max, ps_sum, ps_misc = psum
        logits, weight, at = route["logits"], route["weight"], route["at"]
        rest, flag, pos = (sb(k, [P, NT, E1]) for k in ("rest", "flag", "pos"))
        onehot = [sb(f"onehot{i}", [P, NT, E1]) for i in range(TOP + 1)]
        onehot_bf = sb("onehot_bf", [P, NT, E1], BF16)
        run = [sb(f"run{i}", [P, NT, E1]) for i in range(2)]
        best = [sb(f"best{i}", [P, NT]) for i in range(2)]
        first, gap, gap_exp, slot = (sb(k, [P, NT]) for k in ("first", "gap", "gap_exp", "slot"))
        filled = sb("filled", [P, E1, NT])
        used, ends = sb("used", [P, E1]), [sb(f"ends{i}", [P, E1]) for i in range(2)]
        past, tile_e = sb("past", [1, TILES1, E1]), sb("tile_e", [1, TILES1])
        tile_expert = sb("tile_expert", [1, TILES1], I32)
        xn_all = sb("xn_all", [P, NT, D])
        pack = [sb(f"pack{i}", [P, PACK1]) for i in range(2)]
        rows = [sb(f"rows{i}", [P, D]) for i in range(2)]
        rows_T = [sb(f"rows_T{i}", [P, P]) for i in range(2)]
        silu = [sb(f"silu{i}", [P, FC1, P]) for i in range(2)]
        hid = [sb(f"hid{i}", [P, FC1, P]) for i in range(2)]
        made = [sb(f"made{i}", [P, D]) for i in range(2)]
        W2_AT, B_AT, B2_AT = 2 * F1, 2 * F1 + FC1 * D, 2 * F1 + FC1 * D + 2 * FC1
        sent = dram["sent1"].rearrange("(n p) d -> n p d", p=P)
        made_dst = dram["made1"].rearrange("(n p) d -> n p d", p=P)

        def one(ap, k):
            return ap[k] if isinstance(k, int) else ap[bass.ds(k, 1)].rearrange("o p d -> (o p) d")

        with nc.Block() as block:

            @block.sync
            def _(sp):
                sp.dma_start(xn_all[:], dram["xn2"].rearrange("(t p) d -> p t d", p=P)).then_inc(sems["all_in"], 16)
                sp.wait_ge(sems["tiles"], 1)

                def load(k, par):
                    e = sp.value_load(tile_expert[0:1, k:k + 1] if isinstance(k, int) else tile_expert[0:1, bass.ds(k, 1)],
                                      min_val=0, max_val=E1 - 1)
                    sp.dma_start(pack[par][:], one(w["pack1"], e)).then_inc(sems[f"pack_in{par}"], 16)
                    sp.dma_start(rows[par][:], one(sent, k)).then_inc(sems[f"rows_in{par}"], 16)

                def store(k, par):
                    sp.wait_ge(sems["made_out"], k + 3)
                    sp.dma_start(one(made_dst, k), made[par][:]).then_inc(sems[f"stored{par}"], 16)

                sp.wait_ge(sems["sent"], 16 * NT * TOP)
                for k in range(2):
                    load(k, k)
                with sp.Fori(1, TILES1 // 2) as i:
                    for par in range(2):
                        store(i * 2 + par - 2, par)
                        load(i * 2 + par, par)
                for par in range(2):
                    store(TILES1 - 2 + par, par)
                for par in range(2):
                    sp.wait_ge(sems[f"stored{par}"], 16 * (TILES1 // 2 + 1))

            @block.tensor
            def _(pe):
                pe.wait_ge(sems["chosen"], 1)
                v = onehot_bf[:].rearrange("p t e -> p (t e)")
                pe.matmul(ps_sum[:, 0:NT * E1], const["before"][:], v, start=True, stop=True)
                pe.matmul(ps_misc[:, 0:NT * E1], const["ones"][:], v, start=True, stop=True).then_inc(sems["counted"], 1)
                pe.wait_ge(sems["slots"], 1)
                with pe.Fori(0, TILES1 // 2) as i:
                    for par in range(2):
                        k = i * 2 + par
                        pe.wait_ge(sems[f"rows_in{par}"], i * 16 + 16)
                        pe.transpose(ps_max[:, par, 0:P], rows[par][:], const["ident"]).then_inc(sems["rowsT"], 1)
                        pe.wait_ge(sems[f"pack_in{par}"], i * 16 + 16)
                        pe.wait_ge(sems["rowsT_out"], k + 1)
                        for c in range(2 * FC1):
                            mm = pe.matmul(ps_scores[:, par, c * P:(c + 1) * P], pack[par][:, c * P:(c + 1) * P], rows_T[par][:], start=True, stop=True)
                        mm.then_inc(sems["hidden"], 1)
                        pe.wait_ge(sems["hidden_out"], k + 1)
                        pe.wait_ge(sems["made_out"], k + 1)
                        bank = ps_sum if par == 0 else ps_misc
                        for c in range(FC1):
                            mm = pe.matmul(bank[:, 0:D], hid[par][:, c, :], pack[par][:, W2_AT + c * D:W2_AT + (c + 1) * D],
                                           start=c == 0, stop=c == FC1 - 1)
                        mm.then_inc(sems["made"], 1)

            @block.scalar
            def _(act):
                act.wait_ge(sems["gap"], 1)
                act.activation(gap_exp[:], gap[:], ACT.Exp).then_inc(sems["gap_exp"], 1)
                with act.Fori(0, TILES1 // 2) as i:
                    for par in range(2):
                        k = i * 2 + par
                        act.wait_ge(sems["rowsT"], k + 1)
                        act.activation(rows_T[par][:], ps_max[:, par, 0:P], ACT.Copy).then_inc(sems["rowsT_out"], 1)
                        act.wait_ge(sems["hidden"], k + 1)
                        for c in range(FC1):
                            op = act.activation(silu[par][:, c, :], ps_scores[:, par, (FC1 + c) * P:(FC1 + c + 1) * P], ACT.Silu,
                                                bias=pack[par][:, B_AT + FC1 + c:B_AT + FC1 + c + 1])
                        op.then_inc(sems["silu"], 1)

            @block.vector
            def _(dve):
                linked = [0]

                def link(op):
                    linked[0] += 1
                    op.then_inc(sems["dve"], 1)
                    dve.wait_ge(sems["dve"], linked[0])

                dve.sem_inc(sems["made_out"], 2)
                dve.sem_inc(sems["stored0"], 16)
                dve.sem_inc(sems["stored1"], 16)
                number = const["all"][:, C_EXP1:C_EXP1 + E1]
                first_best(dve, link, logits[:], E1, number, best[0], flag, first, onehot[0])
                link(dve.scalar_tensor_tensor(rest[:], onehot[0][:], MASK, logits[:], ALU.mult, ALU.add))
                first_best(dve, link, rest[:], E1, number, best[1], flag, first, onehot[1])
                link(dve.tensor_tensor(onehot[2][:], onehot[0][:], onehot[1][:], ALU.add))
                dve.tensor_copy(onehot_bf[:], onehot[2][:]).then_inc(sems["chosen"], 1)
                dve.tensor_tensor(gap[:], best[1][:], best[0][:], ALU.subtract).then_inc(sems["gap"], 1)
                dve.wait_ge(sems["counted"], 1)
                by = "p (t e) -> p t e"
                total = places(dve, link, ps_sum[:, 0:NT * E1].rearrange(by, e=E1), ps_misc[:, 0:NT * E1].rearrange(by, e=E1), run, pos)
                link(dve.tensor_tensor(filled[:], total[:, NT - 1, :].unsqueeze(2).broadcast_to([P, E1, NT]),
                                       const["all"][:, C_FILL:C_FILL + NT].unsqueeze(1).broadcast_to([P, E1, NT]), ALU.is_gt))
                link(dve.tensor_reduce(used[:], filled[:], AX.X, ALU.add))
                link(dve.tensor_copy(ends[0][:], used[:]))
                a, b, k = 0, 1, 1
                while k < E1:
                    dve.tensor_copy(ends[b][:, 0:k], ends[a][:, 0:k])
                    link(dve.tensor_tensor(ends[b][:, k:E1], ends[a][:, k:E1], ends[a][:, 0:E1 - k], ALU.add))
                    a, b, k = b, a, 2 * k
                link(dve.tensor_tensor(past[:], const["all"][0:1, C_TILE:C_TILE + TILES1].unsqueeze(2).broadcast_to([1, TILES1, E1]),
                                       ends[a][0:1, :].unsqueeze(1).broadcast_to([1, TILES1, E1]), ALU.is_ge))
                link(dve.tensor_reduce(tile_e[:], past[:], AX.X, ALU.add))
                link(dve.tensor_scalar(tile_e[:], tile_e[:], float(E1 - 1), None, ALU.min))
                dve.tensor_copy(tile_expert[:], tile_e[:]).then_inc(sems["tiles"], 1)
                link(dve.tensor_tensor(ends[b][:], ends[a][:], used[:], ALU.subtract))
                link(dve.tensor_scalar(ends[b][:], ends[b][:], float(P), None, ALU.mult))
                link(dve.tensor_tensor(pos[:], pos[:], ends[b][:].unsqueeze(1).broadcast_to([P, NT, E1]), ALU.add))
                for i in range(TOP):
                    link(dve.tensor_tensor(flag[:], pos[:], onehot[i][:], ALU.mult))
                    link(dve.tensor_reduce(slot[:], flag[:], AX.X, ALU.add))
                    op = dve.tensor_copy(at[i][:], slot[:])
                    if i == 0:
                        link(op)
                op.then_inc(sems["slots"], 1)
                dve.wait_ge(sems["gap_exp"], 1)
                link(dve.tensor_scalar(first[:], gap_exp[:], 1.0, None, ALU.add))
                link(dve.reciprocal(weight[0][:], first[:]))
                dve.tensor_tensor(weight[1][:], gap_exp[:], weight[0][:], ALU.mult)
                with dve.Fori(0, TILES1 // 2) as i:
                    for par in range(2):
                        k = i * 2 + par
                        dve.wait_ge(sems["silu"], k + 1)
                        for c in range(FC1):
                            op = dve.scalar_tensor_tensor(hid[par][:, c, :], ps_scores[:, par, c * P:(c + 1) * P],
                                                          pack[par][:, B_AT + c:B_AT + c + 1], silu[par][:, c, :], ALU.add, ALU.mult)
                        op.then_inc(sems["hidden_out"], 1)
                        dve.wait_ge(sems["made"], k + 1)
                        dve.wait_ge(sems[f"stored{par}"], i * 16 + 16)
                        bank = ps_sum if par == 0 else ps_misc
                        dve.tensor_tensor(made[par][:], bank[:, 0:D], pack[par][:, B2_AT:B2_AT + D], ALU.add).then_inc(sems["made_out"], 1)

            @block.gpsimd
            def _(pool):
                pool.wait_ge(sems["all_in"], 16)
                pool.wait_ge(sems["slots"], 1)
                for t in range(NT):
                    for i in range(TOP):
                        pool.indirect_dma_start(dram["sent1"], bass.IndirectOffsetOnAxis(ap=at[i][:, t:t + 1], axis=0),
                                                xn_all[:, t, :], None).then_inc(sems["sent"], 16)


def build(nc, w, out):
    with ExitStack() as ctx:
        def sb(name, shape, dt=F32):
            return ctx.enter_context(nc.sbuf_tensor(name, shape, dt))

        def ps(name, shape):
            return ctx.enter_context(nc.psum_tensor(name, shape, F32))

        def scratch(name, shape, dt=F32):
            return nc.dram_tensor(name, shape, dt, kind="Internal").ap()

        psum = (ps("ps_scores", [P, 4, S]), ps("ps_max", [P, 2, S]), ps("ps_sum", [P, S]), ps("ps_misc", [P, S]))
        dram = {
            "x": w["x"], "xn": scratch("xn", [NB * S, D]), "x2": scratch("x2", [NB * S, D]), "xn2": scratch("xn2", [NB * S, D]),
            "q": scratch("q_parts", [3, P, S], BF16), "k": scratch("k_parts", [3, P, S], BF16),
            "sent0": scratch("sent0", [E0 * CAP + NB * S, D]), "made0": scratch("made0", [E0 * CAP, D]),
            "sent1": scratch("sent1", [TILES1 * P, D]), "made1": scratch("made1", [TILES1 * P, D]),
        }
        every = sb("consts", [P, C_END])
        const = {
            "all": every, "ident": every[:, C_IDENT:C_IDENT + P], "holt": every[:, C_HOLT:C_END],
            "minus_half": sb("minus_half", [P, 2 * QT]), "ones": sb("ones", [P, P], BF16),
            **{k: sb(k, [P, P], BF16) for k in ("ident_bf", "before", "mask_qk", "mask_kq")},
        }
        routes = [{"at": [sb(f"at{n}{i}", [P, NT], U32) for i in range(k)], "weight": [sb(f"weight{n}{i}", [P, NT]) for i in range(k)]}
                  for n, k in ((0, 1), (1, TOP))]
        routes[0]["logits"] = routes[1]["logits"] = sb("logits1", [P, NT, E1])
        experts0(nc, const, psum, dram, w, routes[0])
        attention(nc, 0, const, psum, {**dram, "moe": dram["made0"]}, w["attn0"], routes[0], out)
        experts1(nc, const, psum, dram, w, routes[1])
        attention(nc, 1, const, psum, {**dram, "moe": dram["made1"]}, w["attn1"], routes[1], out)


def layout(v):
    f = {k: np.asarray(a) for k, a in v.items()}

    def pair(name):
        m = np.zeros((P, P), np.float32)
        m[:HALF, :HALF], m[HALF:, HALF:] = f[f"L0_attn_{name}1"].T, f[f"L0_attn_{name}2"].T
        return m

    def both(name):
        return np.concatenate([f[f"L0_attn_{name}1"], f[f"L0_attn_{name}2"]])

    pack = np.concatenate([
        f["L1_ffn_w0"].transpose(0, 2, 1), f["L1_ffn_w1"].transpose(0, 2, 1),
        f["L1_ffn_w2"].transpose(0, 2, 1).reshape(E1, FC1, P, D).transpose(0, 2, 1, 3).reshape(E1, P, FC1 * D),
        f["L1_ffn_b0"].reshape(E1, FC1, P).transpose(0, 2, 1), f["L1_ffn_b1"].reshape(E1, FC1, P).transpose(0, 2, 1),
        np.repeat(f["L1_ffn_b2"][:, None, :], P, 1)], 2)
    return {
        "x": f["L0_attn_x"].reshape(NB * S, D), "consts": constants(), "alibi": alibi(),
        "gate_w0": f["L0_ffn_Wg"], "w1_0": f["L0_ffn_w1"], "w2_0": f["L0_ffn_w2"], "pack1": pack,
        **{f"a0_w{k}": pair(f"w{k}") for k in "qkvo"},
        **{f"a0_b{k}": both(f"b{k}").reshape(P, 1) if k in "qk" else both(f"b{k}") for k in "qkvo"},
        "a0_g12": both("g"), "a0_be12": both("be"),
        "a0_w_ff1": f["L0_attn_w_ff1"].T, "a0_b_ff1": f["L0_attn_b_ff1"].reshape(FC0, P).T,
        "a0_w_ff2": f["L0_attn_w_ff2"].T.reshape(FC0, P, D).transpose(1, 0, 2), "a0_b_ff2": f["L0_attn_b_ff2"],
        "a0_g_ff": f["L0_attn_g_ff"], "a0_be_ff": f["L0_attn_be_ff"],
        "a0_gate_w1": f["L1_ffn_gate_w"].T, "a0_gate_b1": f["L1_ffn_gate_b"],
        **{f"a1_w{k}": f[f"L1_attn_W{k}"].T for k in "qkvo"},
    }


def kernel(**inputs):
    import concourse.bacc as bacc
    from concourse.bass_utils import run_bass_kernel_spmd

    nc = bacc.Bacc("TRN2", target_bir_lowering=False, num_devices=1)
    arrays = {k: np.ascontiguousarray(a) for k, a in layout(inputs).items()}
    aps = {k: nc.dram_tensor(f"in_{k}", a.shape, mybir.dt.from_np(a.dtype), kind="ExternalInput").ap() for k, a in arrays.items()}
    w = {k: a for k, a in aps.items() if k[:2] not in ("a0", "a1")}
    w["attn0"] = {k[3:]: a for k, a in aps.items() if k.startswith("a0_")}
    w["attn1"] = {**{k[3:]: a for k, a in aps.items() if k.startswith("a1_")}, "alibi": aps["alibi"]}
    out = nc.dram_tensor("out", (NB * S, D), F32, kind="ExternalOutput").ap()
    build(nc, w, out)
    r = run_bass_kernel_spmd(nc, [{f"in_{k}": a for k, a in arrays.items()}], core_ids=[0])
    return r.results[0]["out"].reshape(NB, S, D)
```

```python
import math
from contextlib import ExitStack

import numpy as np

import concourse.bass as bass
from concourse import mybir

F32, BF16 = mybir.dt.float32, mybir.dt.bfloat16
U32, I32 = mybir.dt.uint32, mybir.dt.int32
ALU = mybir.AluOpType
ACT = mybir.ActivationFunctionType
AX = mybir.AxisListType

P = 128
NB, S, D = 8, 512, 128
QT = S // P
NT = NB * QT
HD, H = 8, 16
HALF = D // 2
NG = H // 2
STRIP = 64
PARTS = 6
ROW_SHIFT = PARTS * HD
ROW_ALIBI = ROW_SHIFT + 2
ROW_END = ROW_ALIBI + 3
VW = 32
SCALE = 1.0 / math.sqrt(HD)
EPS = 1e-5
MASK = -1.0e30

E0, F0 = 16, 512
CAP = NB * S // E0
FC0 = F0 // P
E1, F1, TOP = 8, 256, 2
FC1 = F1 // P
TILES1 = NB * S * TOP // P + E1
PACK1 = 2 * F1 + FC1 * D + 2 * FC1 + D

C_IDENT = 0
C_BEFORE = C_IDENT + P
C_MASK_QK = C_BEFORE + P
C_MASK_KQ = C_MASK_QK + P
C_EXP0 = C_MASK_KQ + P
C_EXP1 = C_EXP0 + E0
C_FILL = C_EXP1 + E1
C_DUMP = C_FILL + NT
C_TILE = C_DUMP + NT
C_HOLT = C_TILE + TILES1
N_HOLT = QT * (QT + 1) // 2
C_END = C_HOLT + N_HOLT * P


def holt_block(st, tt):
    return st * QT - st * (st - 1) // 2 + tt - st


def constants():
    c = np.zeros((P, C_END), np.float32)
    n = np.arange(P)
    c[:, C_IDENT:C_IDENT + P] = np.eye(P)
    c[:, C_BEFORE:C_BEFORE + P] = n[:, None] < n[None, :]
    c[:, C_MASK_QK:C_MASK_QK + P] = np.where(n[None, :] > n[:, None], MASK, 0)
    c[:, C_MASK_KQ:C_MASK_KQ + P] = np.where(n[:, None] > n[None, :], MASK, 0)
    c[:, C_EXP0:C_EXP0 + E0] = np.arange(E0) - E0
    c[:, C_EXP1:C_EXP1 + E1] = np.arange(E1) - E1
    c[:, C_FILL:C_FILL + NT] = P * np.arange(NT)
    c[:, C_DUMP:C_DUMP + NT] = E0 * CAP + P * np.arange(NT)[None, :] + n[:, None]
    c[:, C_TILE:C_TILE + TILES1] = np.arange(TILES1)
    alpha, beta = 0.1, 0.1
    level, trend = np.zeros(S), np.zeros(S)
    level[0] = 1.0
    rows = [level]
    for t in range(1, S):
        x = np.zeros(S)
        x[t] = 1.0
        new = alpha * x + (1 - alpha) * (level + trend)
        trend = beta * (new - level) + (1 - beta) * trend
        level = new
        rows.append(level)
    holt = np.stack(rows, 1)
    for st in range(QT):
        for tt in range(st, QT):
            at = C_HOLT + holt_block(st, tt) * P
            c[:, at:at + P] = holt[st * P:(st + 1) * P, tt * P:(tt + 1) * P]
    return c


def alibi():
    base = 2.0 ** (-8.0 / H)
    slopes = np.array([np.float32(base ** i) for i in range(1, H + 1)], np.float32)
    order = [2 * g + j for j in range(2) for g in range(NG)]
    return (slopes[order][:, None] * (np.arange(S) - S // 2)[None, :].astype(np.float32)).astype(np.float32)


class Tally:

    def __init__(self, adds):
        self.adds, self.n, self.trip, self.per = adds, {}, None, {}

    def at(self, name):
        v = self.n.get(name, 0)
        return v if self.trip is None else self.trip * self.per.get(name, 0) + v

    def step(self, step):
        for name, k in self.adds(step).items():
            self.n[name] = self.n.get(name, 0) + k

    def enter(self, trip, steps):
        self.trip, self.per = trip, {}
        for s in steps:
            for name, k in self.adds(s).items():
                self.per[name] = self.per.get(name, 0) + k

    def leave(self, trips):
        for name, k in self.per.items():
            self.n[name] = self.n.get(name, 0) + k * (trips - 1)
        self.trip = None


def wait(eng, sem, value):
    if isinstance(value, int) and value <= 0:
        return
    eng.wait_ge(sem, value)


def wait_apart(eng, sem, value, apart):
    wait(eng, sem, value)
    if not isinstance(value, int):
        eng.sem_inc(apart, 1)


GROUPS = H
READY = 9
MAX_TILES = H * QT
PER_GROUP = MAX_TILES // GROUPS
FIRST_MAX = 6

MISC = {
    0: {0: [("gather", -1), ("zT", 1), ("onT", -1)],
        1: [("q", 1), ("proj", -1)],
        2: [("k", 1)],
        3: [("ln1", -1), ("v", 1), ("fetch", 1)],
        4: [("z", 1)],
        5: [("yT", -1)],
        6: [("ff1", -1, 0), ("ff1", -1, 1)],
        7: [("ff1", -1, 2), ("ff1", -1, 3)],
        8: [("ff2", -1)],
        9: [("gate", -1)],
        10: [("ln2", -1)],
        11: [("mix", -1)],
        12: [("ln3a", -1)],
        13: [("ln3b", -1)],
        14: [("x2T", -1)],
        15: [("logits", -1)]},
    1: {0: [("gather", -1), ("zT", 1), ("onT", -1)],
        1: [("q", 1), ("proj", -1)],
        2: [("k", 1)],
        3: [("v", 1), ("fetch", 1)],
        5: [("gate", -1)],
        8: [("mix", -1)]},
}


def plan(layer, b):
    here, ahead, behind = 0 <= b < NB, 0 <= b + 1 < NB, b >= 1
    steps = []
    if ahead:
        steps.append(("load", 1, 0))
    if behind:
        steps.append(("loadx", -1, 0))
    for n in range(GROUPS):
        if here:
            steps.append(("exp", 0, n))
        if n == 0 and behind:
            steps += [("sum", -1, (GROUPS - 1, here)), ("take", -1, QT - 1), ("norm", -1, QT - 1)]
        elif n > 0 and here:
            steps.append(("sum", 0, (n - 1, True)))
            if n % QT == 0:
                steps.append(("take", 0, n // QT - 1))
            if n % QT == 1 and n > 1:
                steps.append(("norm", 0, n // QT - 1))
        d = 1 if n >= FIRST_MAX else 0
        first = PER_GROUP * ((n - FIRST_MAX) % GROUPS)
        tiles = [("max", d, m) for m in range(first, first + PER_GROUP)] if (ahead if d else here) else []
        steps += tiles[:PER_GROUP // 2]
        for name, at, *arg in MISC[layer].get(n, []):
            if ahead if at == 1 else behind:
                steps.append((name, at, *(arg or [0])))
        steps += tiles[PER_GROUP // 2:]
        half, last = divmod(first + PER_GROUP, MAX_TILES // 2)
        if tiles and last == 0:
            steps.append(("shift", d, half - 1))
    return steps


FETCHES = 2 * 2
LN_TILES = {"proj": 2 * QT, "ff2": QT, "ln3a": QT}


def adds(layer):
    both = {"misc": 1, "misc_free": 1}
    table = {
        "load": {"z_in": 16}, "loadx": {"x_in": 16},
        "exp": {"scores": 2, "probs": 2}, "sum": {"summed": 1}, "take": {"taken": 1},
        "norm": {**both, "dve": 1},
        "zT": both, "q": {**both, "split": 1, "pool": 2, "q_out": 16 * PARTS}, "k": {**both, "split": 1, "pool": 2, "k_out": 16 * PARTS},
        "v": both, "z": both, "fetch": {"strips": 16 * FETCHES},
        "max": {"max_in": 1, "max_out": 1}, "shift": {**both, "dve": 1, "shift_in": 64},
        "onT": both, "yT": {**both}, "ff1": both, "x2T": both, "logits": both,
        "proj": {**both, "dve": 1, "moments": 1, "rstd": 1, "pool": 1} if layer == 0 else both,
        "ln1": {"dve": 1, "centred": 1, "pool": 1, "y": 1, "yb": 1},
        "ff2": {**both, "dve": 1, "moments": 1, "rstd": 1, "pool": 1},
        "ln2": {"normed": 1, "pool": 1, "s": 1},
        "gather": {"picks": 1, "rows": 16 * QT * (1 if layer == 0 else TOP)},
        "gate": {"gate_in": 1, "gate_tanh": 1, "pool": 0 if layer == 0 else 1},
        "mix": {"gate_out": 1, "pool": 1, "x2": 1, "x2_out": 16},
        "ln3a": {"dve": 1, "moments": 1, "rstd": 1, "pool": 1},
        "ln3b": {"xn2": 1, "xn2_out": 16},
    }
    return lambda step: table[step[0]]


def batches(eng, n, layer):
    for b in (-1, 0):
        yield b, b % 2, plan(layer, b)
    trips = (NB - 2) // 2
    with eng.Fori(0, trips) as trip:
        n.enter(trip, plan(layer, 1) + plan(layer, 2))
        for half in range(2):
            yield trip * 2 + 1 + half, (1 + half) % 2, plan(layer, 1 + half)
        n.leave(trips)
    for b in (NB - 1, NB):
        yield b, b % 2, plan(layer, b)


def of_batch(ap, b):
    if isinstance(b, int):
        return ap[b]
    return ap[bass.ds(b, 1)].rearrange("o p t d -> (o p) t d")


def attention(nc, layer, const, psum, dram, w, route, out):
    causal = layer == 1
    with ExitStack() as ctx:
        def sb(name, shape, dt=F32):
            return ctx.enter_context(nc.sbuf_tensor(f"a{layer}_{name}", shape, dt))

        sems = {k: ctx.enter_context(nc.semaphore(f"a{layer}_{k}")) for k in (
            "weights", "ready", "z_in", "x_in", "scores", "probs", "summed", "taken", "misc", "misc_free", "split",
            "q_out", "k_out", "strips", "max_in", "max_out", "shift_in", "moments", "rstd", "centred",
            "y", "yb", "normed", "s", "picks", "rows", "gate_in", "gate_tanh", "gate_out",
            "x2", "x2_out", "xn2", "xn2_out", "dve", "pool", "apart")}
        ps_scores, ps_max, ps_sum, ps_misc = psum

        q_strip = [sb(f"q_strip{i}", [P, NG, S], BF16) for i in range(2)]
        k_strip = [sb(f"k_strip{i}", [P, H, S], BF16) for i in range(2)]
        v_aug = [sb(f"v_aug{i}", [P, QT, H, VW]) for i in range(2)]
        probs = [sb(f"probs{i}", [P, 4, S]) for i in range(2)]
        z_in, z_T = sb("z_in", [P, QT, D]), sb("z_T", [P, S])
        whole = {k: sb(f"{k}_whole", [P, S]) for k in "qk"}
        parts = {k: sb(f"{k}_parts", [P, 3, S], BF16) for k in "qk"}
        rest = {k: sb(f"{k}_rest", [P, S]) for k in "qk"}
        neg_max = sb("neg_max", [P, QT, 2, NG])
        shift = sb("shift", [NG, 2, S], BF16)
        rows_of = {"q": sb("zeros", [P, S], BF16), "k": sb("ones", [P, S], BF16)}
        o_strip = [sb(f"o_strip{i}", [P, S]) for i in range(2)]
        o_norm = [sb(f"o_norm{i}", [P, QT, D]) for i in range(2)]
        o_den = sb("o_den", [P, QT, 4])
        o_T = sb("o_T", [P, S])
        x_in, x2 = sb("x_in", [P, QT, D]), sb("x2", [P, QT, D])
        rows = [sb(f"rows{i}", [P, QT, D]) for i in range(1 if layer == 0 else TOP)]
        row_at = [sb(f"row_at{i}", [P, QT], U32) for i in range(len(rows))]
        row_w = [sb(f"row_w{i}", [P, QT]) for i in range(len(rows))]
        z, e, gz, s_out = (sb(k, [P, QT, D]) for k in ("z", "e", "gz", "s_out"))
        sg = sb("sg", [P, QT, D])
        wq, wk, wv, wo = (sb(k, [P, D]) for k in ("wq", "wk", "wv", "wo"))
        loads = [(wq, w["wq"]), (wk, w["wk"]), (wv, w["wv"]), (wo, w["wo"])]
        if layer == 0:
            resid = [sb(f"resid{i}", [P, QT, D]) for i in range(2)]
            y0, y1, y2, y3, y, yb, t0, t1, t2 = (sb(k, [P, QT, D]) for k in (
                "y0", "y1", "y2", "y3", "y", "yb", "t0", "t1", "t2"))
            y_T, hid = sb("y_T", [P, S]), sb("hid", [P, FC0, S])
            xn2, xn2_T = sb("xn2", [P, QT, D]), sb("xn2_T", [P, S])
            stats, moments = sb("stats", [P, 2 * QT, 6]), sb("moments", [P, 2 * QT, 2])
            veps, rstd = sb("veps", [P, 2 * QT]), sb("rstd", [P, 2 * QT])
            bq, bk, bqs = sb("bq", [P, 1]), sb("bk", [P, 1]), sb("bqs", [P, 1])
            w_ff1, w_ff2, b_ff1 = sb("w_ff1", [P, F0]), sb("w_ff2", [P, FC0, D]), sb("b_ff1", [P, FC0])
            bv, bo, g12, be12, b_ff2, g_ff, be_ff = (sb(k, [P, D]) for k in (
                "bv", "bo", "g12", "be12", "b_ff2", "g_ff", "be_ff"))
            wg, bg = sb("wg", [P, E1]), sb("bg", [P, E1])
            loads += [(bq, w["bq"]), (bk, w["bk"]), (w_ff1, w["w_ff1"]), (w_ff2, w["w_ff2"]), (b_ff1, w["b_ff1"]),
                      (wg, w["gate_w1"]), (bg, w["gate_b1"].partition_broadcast(P))]
            loads += [(t, w[k].partition_broadcast(P)) for t, k in (
                (bv, "bv"), (bo, "bo"), (g12, "g12"), (be12, "be12"), (b_ff2, "b_ff2"), (g_ff, "g_ff"), (be_ff, "be_ff"))]
        else:
            pos = sb("pos", [H, S])
            pos_parts, pos_rest = sb("pos_parts", [H, 3, S], BF16), sb("pos_rest", [H, S])
            z_both = [sb(f"z_both{i}", [P, QT, D]) for i in range(TOP)]
            loads.append((pos, w["alibi"]))
        n_loads = len(loads)
        fixed_dmas = 2 + (1 if causal else 0)
        strip_rows = {"q": ROW_ALIBI, "k": ROW_END if causal else ROW_ALIBI}

        ident, ident_bf = const["ident"], const["ident_bf"]
        tiles = "(b t p) d -> b p t d"
        z_src = (dram["xn"] if layer == 0 else dram["xn2"]).rearrange(tiles, b=NB, p=P)
        x_src = (dram["x"] if layer == 0 else dram["x2"]).rearrange(tiles, b=NB, p=P)
        x_dst = (dram["x2"] if layer == 0 else out).rearrange(tiles, b=NB, p=P)
        xn_dst = dram["xn2"].rearrange(tiles, b=NB, p=P)

        def cols(kt):
            return (kt * P if causal else 0), S

        def keys(qt):
            return (qt + 1) * P if causal else S

        def head(m):
            half, r = divmod(m, MAX_TILES // 2)
            hd, qt = divmod(r, QT)
            return half, hd % 2, hd // 2, qt

        with nc.Block() as block:

            @block.sync
            def _(sp):
                n = Tally(adds(layer))
                for dst, src in loads:
                    sp.dma_start(dst[:], src).then_inc(sems["weights"], 16)
                wait(sp, sems["ready"], READY)
                for k in "qk":
                    sp.dma_start(dram[k][:, ROW_SHIFT:ROW_ALIBI], rows_of[k][0:2 * H, :]).then_inc(sems["weights"], 16)
                if causal:
                    sp.dma_start(dram["k"][:, ROW_ALIBI:ROW_END], pos_parts[:]).then_inc(sems["weights"], 16)
                for b, odd, steps in batches(sp, n, layer):
                    for step in steps:
                        name, d, arg = step
                        par = (odd + d) % 2
                        if name == "load":
                            sp.dma_start(z_in[:], of_batch(z_src, b + d)).then_inc(sems["z_in"], 16)
                        if name == "loadx":
                            sp.dma_start(x_in[:], of_batch(x_src, b + d)).then_inc(sems["x_in"], 16)
                        if name in ("q", "k"):
                            wait(sp, sems["split"], n.at("split") + 1)
                            order = (0, 0, 0, 1, 1, 2) if name == "q" else (0, 1, 2, 0, 1, 0)
                            for a in range(PARTS):
                                sp.dma_start(dram[name][:, HD * a:HD * (a + 1)],
                                             parts[name][:, order[a], :]).then_inc(sems[f"{name}_out"], 16)
                        if name == "fetch":
                            wait_apart(sp, sems["q_out"], n.at("q_out"), sems["apart"])
                            wait_apart(sp, sems["k_out"], n.at("k_out"), sems["apart"])
                            wait(sp, sems["scores"], n.at("scores"))
                            for j in range(2):
                                for k, strip, slots in (("q", q_strip, slice(0, NG)), ("k", k_strip, slice(NG * j, NG * (j + 1)))):
                                    sp.dma_start(strip[par][STRIP * j:STRIP * j + strip_rows[k], slots, :],
                                                 dram[k][NG * j:NG * (j + 1), 0:strip_rows[k]].rearrange("g r n -> r g n")).then_inc(sems["strips"], 16)
                        if name == "shift":
                            wait(sp, sems["misc_free"], n.at("misc_free") + 1)
                            for j in range(2):
                                for a in range(2):
                                    r = STRIP * j + ROW_SHIFT + a
                                    sp.dma_start(q_strip[par][r:r + 1, arg * QT:(arg + 1) * QT, :],
                                                 shift[j * QT:(j + 1) * QT, a, :]).then_inc(sems["shift_in"], 16)
                        if name == "mix":
                            wait(sp, sems["x2"], n.at("x2") + 1)
                            sp.dma_start(of_batch(x_dst, b + d), x2[:]).then_inc(sems["x2_out"], 16)
                        if name == "ln3b":
                            wait(sp, sems["xn2"], n.at("xn2") + 1)
                            sp.dma_start(of_batch(xn_dst, b + d), xn2[:]).then_inc(sems["xn2_out"], 16)
                        n.step(step)
                wait(sp, sems["x2_out"], n.at("x2_out"))
                wait(sp, sems["xn2_out"], n.at("xn2_out"))

            @block.tensor
            def _(pe):
                n = Tally(adds(layer))
                wait(pe, sems["weights"], 16 * (n_loads + fixed_dmas))
                wait(pe, sems["ready"], READY)

                def claim():
                    wait(pe, sems["misc_free"], n.at("misc_free"))

                for b, odd, steps in batches(pe, n, layer):
                    for step in steps:
                        name, d, arg = step
                        par = (odd + d) % 2
                        if name == "exp":
                            u, kt = divmod(arg, QT)
                            lo, hi = cols(kt)
                            if arg in (0, GROUPS // 2):
                                wait(pe, sems["shift_in"], n.at("shift_in"))
                            for g in range(2):
                                slot = 2 * u + g
                                wait(pe, sems["probs"], n.at("probs") + g - 1)
                                for j in range(2):
                                    o = ps_scores[:, 2 * g + j, 0:hi - lo]
                                    mm = pe.matmul(o, k_strip[par][:, NG * j + slot, kt * P:(kt + 1) * P],
                                                   q_strip[par][:, slot, lo:hi], start=True, stop=not causal)
                                    if causal:
                                        mm = pe.matmul(ps_scores[:, 2 * g + j, 0:P], ident_bf[:], const["mask_kq"][:],
                                                       start=False, stop=True)
                                mm.then_inc(sems["scores"], 1)
                        if name == "sum":
                            group, more = arg
                            u, kt = divmod(group, QT)
                            lo, hi = cols(kt)
                            wait(pe, sems["probs"], n.at("probs") - (2 if more else 0))
                            if kt == 0:
                                wait(pe, sems["taken"], n.at("taken"))
                            for c in range(4):
                                mm = pe.matmul(ps_sum[VW * c:VW * (c + 1), lo:hi], v_aug[par][:, kt, 4 * u + c, :],
                                               probs[group % 2][:, c, 0:hi - lo], start=kt == 0, stop=kt == QT - 1)
                            mm.then_inc(sems["summed"], 1)
                        if name == "norm":
                            wait(pe, sems["taken"], n.at("taken"))
                            claim()
                            for t in range(QT):
                                mm = pe.transpose(ps_misc[:, t * P:(t + 1) * P], o_strip[arg % 2][:, t * P:(t + 1) * P], ident[:])
                            mm.then_inc(sems["misc"], 1)
                        if name == "zT":
                            wait(pe, sems["z_in"], n.at("z_in"))
                            wait_apart(pe, sems["misc_free"], n.at("misc_free"), sems["apart"])
                            if layer == 0:
                                for t in range(QT):
                                    pe.transpose(ps_misc[0:HALF, t * P:(t + 1) * P], z_in[:, t, 0:HALF], ident[:])
                                for t in range(QT):
                                    mm = pe.matmul(ps_misc[HALF:P, t * P:S], z_in[:, t, 0:HALF],
                                                   const["holt"][:, holt_block(t, t) * P:(holt_block(t, QT - 1) + 1) * P],
                                                   start=t == 0, stop=t == QT - 1)
                            else:
                                for t in range(QT):
                                    mm = pe.transpose(ps_misc[:, t * P:(t + 1) * P], z_in[:, t, :], ident[:])
                            mm.then_inc(sems["misc"], 1)
                        if name in ("q", "k"):
                            claim()
                            pe.matmul(ps_misc[:], (wq if name == "q" else wk)[:], z_T[:], start=True, stop=True).then_inc(sems["misc"], 1)
                        if name in ("v", "z"):
                            claim()
                            for t in range(QT):
                                o, i = ps_misc[:, t * P:(t + 1) * P], z_T[:, t * P:(t + 1) * P]
                                mm = pe.matmul(o, i, wv[:], start=True, stop=True) if name == "v" else pe.transpose(o, i, ident[:])
                            mm.then_inc(sems["misc"], 1)
                        if name == "max":
                            if arg == 0:
                                wait(pe, sems["strips"], n.at("strips"))
                            half, j, slot, qt = head(arg)
                            slot += QT * half
                            wait(pe, sems["max_out"], n.at("max_out") - 1)
                            o = ps_max[:, arg % 2, 0:keys(qt)]
                            mm = pe.matmul(o, q_strip[par][:, slot, qt * P:(qt + 1) * P], k_strip[par][:, NG * j + slot, 0:keys(qt)],
                                           start=True, stop=not causal)
                            if causal:
                                mm = pe.matmul(ps_max[:, arg % 2, qt * P:(qt + 1) * P], ident_bf[:], const["mask_qk"][:],
                                               start=False, stop=True)
                            mm.then_inc(sems["max_in"], 1)
                        if name == "shift":
                            wait(pe, sems["max_out"], n.at("max_out"))
                            claim()
                            for t in range(QT):
                                mm = pe.transpose(ps_misc[0:NG, t * P:(t + 1) * P], neg_max[:, t, arg, :], ident[:])
                            mm.then_inc(sems["misc"], 1)
                        if name == "onT":
                            claim()
                            for t in range(QT):
                                mm = pe.transpose(ps_misc[:, t * P:(t + 1) * P], o_norm[par][:, t, :], ident[:])
                            mm.then_inc(sems["misc"], 1)
                        if name == "proj":
                            claim()
                            for t in range(QT):
                                mm = pe.matmul(ps_misc[:, t * P:(t + 1) * P], o_T[:, t * P:(t + 1) * P], wo[:], start=True, stop=True)
                            mm.then_inc(sems["misc"], 1)
                        if name == "yT":
                            wait(pe, sems["y"], n.at("y"))
                            claim()
                            for t in range(QT):
                                mm = pe.transpose(ps_misc[:, t * P:(t + 1) * P], y[:, t, :], ident[:])
                            mm.then_inc(sems["misc"], 1)
                        if name == "ff1":
                            claim()
                            pe.matmul(ps_misc[:], w_ff1[:, arg * P:(arg + 1) * P], y_T[:], start=True, stop=True).then_inc(sems["misc"], 1)
                        if name == "ff2":
                            claim()
                            for t in range(QT):
                                for c in range(FC0):
                                    mm = pe.matmul(ps_misc[:, t * P:(t + 1) * P], hid[:, c, t * P:(t + 1) * P], w_ff2[:, c, :],
                                                   start=c == 0, stop=c == FC0 - 1)
                            mm.then_inc(sems["misc"], 1)
                        if name == "x2T":
                            wait(pe, sems["xn2"], n.at("xn2"))
                            claim()
                            for t in range(QT):
                                mm = pe.transpose(ps_misc[:, t * P:(t + 1) * P], xn2[:, t, :], ident[:])
                            mm.then_inc(sems["misc"], 1)
                        if name == "logits":
                            claim()
                            for t in range(QT):
                                mm = pe.matmul(ps_misc[:, t * E1:(t + 1) * E1], xn2_T[:, t * P:(t + 1) * P], wg[:], start=True, stop=True)
                            mm.then_inc(sems["misc"], 1)
                        n.step(step)

            @block.scalar
            def _(act):
                n = Tally(adds(layer))
                wait(act, sems["weights"], 16 * n_loads)
                wait(act, sems["ready"], READY)
                for b, odd, steps in batches(act, n, layer):
                    for step in steps:
                        name, d, arg = step
                        if name == "exp":
                            lo, hi = cols(arg % QT)
                            wait(act, sems["summed"], n.at("summed"))
                            for g in range(2):
                                wait(act, sems["scores"], n.at("scores") + 1 + g)
                                act.activation(probs[arg % 2][:, 2 * g:2 * g + 2, 0:hi - lo], ps_scores[:, 2 * g:2 * g + 2, 0:hi - lo],
                                               ACT.Exp).then_inc(sems["probs"], 1)
                        if name == "take":
                            wait(act, sems["summed"], n.at("summed"))
                            act.activation(o_strip[arg % 2][:], ps_sum[:], ACT.Copy).then_inc(sems["taken"], 1)
                        if name in ("zT", "onT", "yT", "x2T"):
                            wait(act, sems["misc"], n.at("misc") + 1)
                            dst = {"zT": z_T, "onT": o_T}[name] if name in ("zT", "onT") else (y_T if name == "yT" else xn2_T)
                            act.activation(dst[:], ps_misc[:], ACT.Copy).then_inc(sems["misc_free"], 1)
                        if name in ("q", "k"):
                            wait(act, sems["misc"], n.at("misc") + 1)
                            wait(act, sems[f"{name}_out"], n.at(f"{name}_out"))
                            scale = SCALE if name == "q" else 1.0
                            bias = 0.0 if causal else (bqs if name == "q" else bk)[:, 0:1]
                            act.activation(parts[name][:, 0, :], ps_misc[:], ACT.Identity, bias=bias, scale=scale)
                            act.activation(whole[name][:], ps_misc[:], ACT.Identity, bias=bias, scale=scale).then_inc(sems["misc_free"], 1)
                        if name == "ff1":
                            wait(act, sems["misc"], n.at("misc") + 1)
                            act.activation(hid[:, arg, :], ps_misc[:], ACT.Relu, bias=b_ff1[:, arg:arg + 1]).then_inc(sems["misc_free"], 1)
                        if name == "proj" and layer == 1:
                            wait(act, sems["misc"], n.at("misc") + 1)
                            wait(act, sems["x2"], n.at("x2"))
                            act.activation(s_out[:].rearrange("p t d -> p (t d)"), ps_misc[:], ACT.Copy).then_inc(sems["misc_free"], 1)
                        if name == "gate":
                            wait(act, sems["gate_in"], n.at("gate_in") + 1)
                            act.activation(e[:], z[:], ACT.Tanh).then_inc(sems["gate_tanh"], 1)
                        n.step(step)

            @block.vector
            def _(dve):
                n = Tally(adds(layer))
                dve.memset(q_strip[0][:], 1.0).then_inc(sems["ready"], 1)
                dve.memset(q_strip[1][:], 1.0).then_inc(sems["ready"], 1)
                for i in range(2):
                    dve.memset(v_aug[i][:], 0.0).then_inc(sems["dve"], 1)
                wait(dve, sems["dve"], 2)
                for i in range(2):
                    dve.memset(v_aug[i][:, :, :, HD:HD + 1], 1.0).then_inc(sems["ready"], 1)
                dve.memset(rows_of["k"][:], 1.0).then_inc(sems["ready"], 1)
                wait(dve, sems["weights"], 16 * n_loads)
                if layer == 0:
                    dve.tensor_scalar(bqs[:], bq[:], SCALE, None, ALU.mult).then_inc(sems["ready"], 1)
                    n.n["dve"] = 2
                else:
                    dve.tensor_copy(pos_parts[:, 0, :], pos[:]).then_inc(sems["dve"], 1)
                    wait(dve, sems["dve"], 3)
                    dve.tensor_tensor(pos_rest[:], pos[:], pos_parts[:, 0, :], ALU.subtract).then_inc(sems["dve"], 1)
                    wait(dve, sems["dve"], 4)
                    dve.tensor_copy(pos_parts[:, 1, :], pos_rest[:]).then_inc(sems["dve"], 1)
                    wait(dve, sems["dve"], 5)
                    dve.tensor_tensor(pos_parts[:, 2, :], pos_rest[:], pos_parts[:, 1, :], ALU.subtract).then_inc(sems["ready"], 1)
                    n.n["dve"] = 5
                wait(dve, sems["ready"], READY)
                linked = [0]

                def link(op):
                    linked[0] += 1
                    op.then_inc(sems["dve"], 1)
                    wait_apart(dve, sems["dve"], n.at("dve") + linked[0], sems["apart"])

                def moments_of(src, width, count):
                    v = src[:].rearrange("p t d -> p (t d)")
                    for i in range(count):
                        op = dve.bn_stats(stats[:, i, :], v[:, i * width:(i + 1) * width])
                    link(op)
                    for i in range(count):
                        op = dve.bn_aggr(moments[:, i, :], stats[:, i, :])
                    op.then_inc(sems["moments"], 1)

                for b, odd, steps in batches(dve, n, layer):
                    for step in steps:
                        name, d, arg = step
                        par = (odd + d) % 2
                        linked[0] = 0
                        if name == "max":
                            half, j, slot, qt = head(arg)
                            wait(dve, sems["max_in"], n.at("max_in") + 1)
                            dve.tensor_reduce(neg_max[:, qt, half, j * QT + slot:j * QT + slot + 1], ps_max[:, arg % 2, 0:keys(qt)],
                                              AX.X, ALU.max, negate=True).then_inc(sems["max_out"], 1)
                        if name == "shift":
                            wait(dve, sems["misc"], n.at("misc") + 1)
                            wait(dve, sems["shift_in"], n.at("shift_in"))
                            link(dve.tensor_copy(shift[:, 0, :], ps_misc[0:NG, :]))
                            dve.tensor_tensor(shift[:, 1, :], ps_misc[0:NG, :], shift[:, 0, :], ALU.subtract).then_inc(sems["misc_free"], 1)
                        if name == "norm":
                            wait(dve, sems["misc"], n.at("misc") + 1)
                            v = ps_misc[:].rearrange("p (t c v) -> p t c v", t=QT, c=4)
                            link(dve.reciprocal(o_den[:], v[:, :, :, HD]))
                            o = o_norm[par][:, :, 4 * HD * arg:4 * HD * (arg + 1)].rearrange("p t (c v) -> p t c v", c=4)
                            dve.tensor_tensor(o, v[:, :, :, 0:HD], o_den[:].unsqueeze(3).broadcast_to([P, QT, 4, HD]),
                                              ALU.mult).then_inc(sems["misc_free"], 1)
                        if name == "v":
                            wait(dve, sems["misc"], n.at("misc") + 1)
                            wait(dve, sems["summed"], n.at("summed"))
                            dst = v_aug[par][:, :, :, 0:HD]
                            src = ps_misc[:].rearrange("p (t h v) -> p t h v", t=QT, h=H)
                            if layer == 0:
                                for t in range(QT):
                                    op = dve.tensor_tensor(dst[:, t], src[:, t], bv[:].rearrange("p (h v) -> p h v", h=H), ALU.add)
                            else:
                                op = dve.tensor_copy(dst, src)
                            op.then_inc(sems["misc_free"], 1)
                        if name == "z":
                            wait(dve, sems["misc"], n.at("misc") + 1)
                            dve.tensor_tensor(resid[par][:], ps_misc[:].rearrange("p (t d) -> p t d", t=QT),
                                              bo[:].unsqueeze(1).broadcast_to([P, QT, D]), ALU.add).then_inc(sems["misc_free"], 1)
                        if name == "proj" and layer == 0:
                            wait(dve, sems["misc"], n.at("misc") + 1)
                            dve.tensor_tensor(y0[:], ps_misc[:].rearrange("p (t d) -> p t d", t=QT), resid[par][:],
                                              ALU.add).then_inc(sems["misc_free"], 1)
                            wait(dve, sems["misc_free"], n.at("misc_free") + 1)
                            moments_of(y0, HALF, 2 * QT)
                        if name == "ln1":
                            wait(dve, sems["rstd"], n.at("rstd"))
                            halves = "p t (a d) -> p (t a) d"
                            link(dve.tensor_tensor(y1[:].rearrange(halves, a=2), y0[:].rearrange(halves, a=2),
                                                   moments[:, :, 0:1].broadcast_to([P, 2 * QT, HALF]), ALU.subtract))
                            dve.tensor_tensor(y2[:].rearrange(halves, a=2), y1[:].rearrange(halves, a=2),
                                              rstd[:].unsqueeze(2).broadcast_to([P, 2 * QT, HALF]), ALU.mult).then_inc(sems["centred"], 1)
                        if name == "ff2":
                            wait(dve, sems["misc"], n.at("misc") + 1)
                            wait(dve, sems["yb"], n.at("yb"))
                            dve.tensor_tensor(t0[:], ps_misc[:].rearrange("p (t d) -> p t d", t=QT), yb[:],
                                              ALU.add).then_inc(sems["misc_free"], 1)
                            wait(dve, sems["misc_free"], n.at("misc_free") + 1)
                            moments_of(t0, D, QT)
                        if name == "ln2":
                            wait(dve, sems["rstd"], n.at("rstd"))
                            for t in range(QT):
                                op = dve.tensor_scalar(t1[:, t, :], t0[:, t, :], moments[:, t, 0:1], rstd[:, t:t + 1], ALU.subtract, ALU.mult)
                            op.then_inc(sems["normed"], 1)
                        if name == "gather":
                            wait(dve, sems["rows"], n.at("rows"))
                            wait(dve, sems["gate_in"], n.at("gate_in"))
                            at = slice(QT * (b + d), QT * (b + d + 1)) if isinstance(b, int) else bass.ds((b + d) * QT, QT)
                            for i in range(len(rows)):
                                dve.tensor_copy(row_at[i][:], route["at"][i][:, at])
                                op = dve.tensor_copy(row_w[i][:], route["weight"][i][:, at])
                            op.then_inc(sems["picks"], 1)
                        if name == "mix":
                            wait(dve, sems["gate_tanh"], n.at("gate_tanh"))
                            dve.scalar_tensor_tensor(gz[:], e[:], 1.0, z[:], ALU.add, ALU.mult).then_inc(sems["gate_out"], 1)
                        if name == "ln3a":
                            wait(dve, sems["x2"], n.at("x2"))
                            moments_of(x2, D, QT)
                        if name == "ln3b":
                            wait(dve, sems["rstd"], n.at("rstd"))
                            wait(dve, sems["xn2_out"], n.at("xn2_out"))
                            for t in range(QT):
                                op = dve.tensor_scalar(xn2[:, t, :], x2[:, t, :], moments[:, t, 0:1], rstd[:, t:t + 1], ALU.subtract, ALU.mult)
                            op.then_inc(sems["xn2"], 1)
                        if name == "logits":
                            wait(dve, sems["misc"], n.at("misc") + 1)
                            at = slice(QT * (b + d), QT * (b + d + 1)) if isinstance(b, int) else bass.ds((b + d) * QT, QT)
                            dve.tensor_tensor(route["logits"][:, at, :], ps_misc[:, 0:QT * E1].rearrange("p (t e) -> p t e", t=QT),
                                              bg[:].unsqueeze(1).broadcast_to([P, QT, E1]), ALU.add).then_inc(sems["misc_free"], 1)
                        assert linked[0] == n.adds(step).get("dve", 0), (step, linked[0])
                        n.step(step)

            @block.gpsimd
            def _(pool):
                n = Tally(adds(layer))
                pool.memset(k_strip[0][:], 0.0).then_inc(sems["ready"], 1)
                pool.memset(k_strip[1][:], 0.0).then_inc(sems["ready"], 1)
                pool.memset(rows_of["q"][:], 0.0).then_inc(sems["ready"], 1)
                wait(pool, sems["weights"], 16 * n_loads)
                linked = [0]

                def link(op):
                    linked[0] += 1
                    op.then_inc(sems["pool"], 1)
                    wait_apart(pool, sems["pool"], n.at("pool") + linked[0], sems["apart"])

                def inverse_deviation(count):
                    wait_apart(pool, sems["moments"], n.at("moments") + 1, sems["apart"])
                    link(pool.tensor_scalar(veps[:, 0:count], moments[:, 0:count, 1], EPS, None, ALU.add))
                    pool.tensor_tensor(rstd[:, 0:count], veps[:, 0:count], const["minus_half"][:, 0:count], ALU.pow).then_inc(sems["rstd"], 1)

                def bcast(t):
                    return t[:].unsqueeze(1).broadcast_to([P, QT, D])

                for b, odd, steps in batches(pool, n, layer):
                    for step in steps:
                        name, d, arg = step
                        linked[0] = 0
                        if name in ("q", "k"):
                            wait(pool, sems["misc_free"], n.at("misc_free") + 1)
                            a, full, r = parts[name], whole[name], rest[name]
                            link(pool.tensor_tensor(r[:], full[:], a[:, 0, :], ALU.subtract))
                            link(pool.tensor_copy(a[:, 1, :], r[:]))
                            pool.tensor_tensor(a[:, 2, :], r[:], a[:, 1, :], ALU.subtract).then_inc(sems["split"], 1)
                        if name in LN_TILES and layer == 0:
                            inverse_deviation(LN_TILES[name])
                        if name == "ln1":
                            wait(pool, sems["centred"], n.at("centred") + 1)
                            link(pool.tensor_tensor(y3[:], y2[:], bcast(g12), ALU.mult))
                            pool.tensor_tensor(y[:], y3[:], bcast(be12), ALU.add).then_inc(sems["y"], 1)
                            wait(pool, sems["y"], n.at("y") + 1)
                            pool.tensor_tensor(yb[:], y[:], bcast(b_ff2), ALU.add).then_inc(sems["yb"], 1)
                        if name == "ln2":
                            wait(pool, sems["normed"], n.at("normed") + 1)
                            link(pool.tensor_tensor(t2[:], t1[:], bcast(g_ff), ALU.mult))
                            pool.tensor_tensor(s_out[:], t2[:], bcast(be_ff), ALU.add).then_inc(sems["s"], 1)
                        if name == "gather":
                            wait_apart(pool, sems["picks"], n.at("picks") + 1, sems["apart"])
                            for i in range(len(rows)):
                                for t in range(QT):
                                    pool.indirect_dma_start(rows[i][:, t, :], None, dram["moe"],
                                                            bass.IndirectOffsetOnAxis(ap=row_at[i][:, t:t + 1], axis=0)
                                                            ).then_inc(sems["rows"], 16)
                        if name == "gate":
                            wait(pool, sems["rows"], n.at("rows"))
                            per = lambda i: row_w[i][:].unsqueeze(2).broadcast_to([P, QT, D])
                            if layer == 0:
                                pool.tensor_tensor(z[:], rows[0][:], per(0), ALU.mult).then_inc(sems["gate_in"], 1)
                            else:
                                pool.tensor_tensor(z_both[0][:], rows[0][:], per(0), ALU.mult)
                                link(pool.tensor_tensor(z_both[1][:], rows[1][:], per(1), ALU.mult))
                                pool.tensor_tensor(z[:], z_both[0][:], z_both[1][:], ALU.add).then_inc(sems["gate_in"], 1)
                        if name == "mix":
                            wait(pool, sems["gate_out"], n.at("gate_out") + 1)
                            wait(pool, sems["x_in"], n.at("x_in"))
                            wait(pool, sems["x2_out"], n.at("x2_out"))
                            if layer == 0:
                                wait(pool, sems["s"], n.at("s"))
                            else:
                                wait(pool, sems["misc_free"], n.at("misc_free"))
                            link(pool.tensor_tensor(sg[:], gz[:], s_out[:], ALU.mult))
                            pool.tensor_tensor(x2[:], sg[:], x_in[:], ALU.add).then_inc(sems["x2"], 1)
                        assert linked[0] == n.adds(step).get("pool", 0), (step, linked[0])
                        n.step(step)


def first_best(dve, link, logits, experts, number, best, flag, first, onehot):
    def per(t):
        return t[:].unsqueeze(2).broadcast_to([P, NT, experts])
    numbers = number.unsqueeze(1).broadcast_to([P, NT, experts])
    link(dve.tensor_reduce(best[:], logits, AX.X, ALU.max))
    link(dve.tensor_tensor(flag[:], logits, per(best), ALU.is_ge))
    link(dve.tensor_tensor(flag[:], flag[:], numbers, ALU.mult))
    link(dve.tensor_reduce(first[:], flag[:], AX.X, ALU.min))
    link(dve.tensor_tensor(onehot[:], numbers, per(first), ALU.is_equal))


def places(dve, link, before, totals, run, pos):
    link(dve.tensor_copy(run[0][:], totals))
    a, b, k = 0, 1, 1
    while k < NT:
        dve.tensor_copy(run[b][:, 0:k, :], run[a][:, 0:k, :])
        link(dve.tensor_tensor(run[b][:, k:NT, :], run[a][:, k:NT, :], run[a][:, 0:NT - k, :], ALU.add))
        a, b, k = b, a, 2 * k
    link(dve.tensor_tensor(pos[:], run[a][:], totals, ALU.subtract))
    link(dve.tensor_tensor(pos[:], pos[:], before, ALU.add))
    return run[a]


def pipelined(eng, count, lead):
    first = 5
    trips = (count - lead - first) // 4
    for k in range(first):
        yield k, k % 4, k
    with eng.Fori(0, trips) as trip:
        for u in range(4):
            yield trip * 4 + first + u, (first + u) % 4, None
    for k in range(first + 4 * trips, count + 1):
        yield k, k % 4, k


def uses(k, par, adds):
    return (k - par) * (adds // 4)


def experts0(nc, const, psum, dram, w, route):
    with ExitStack() as ctx:
        def sb(name, shape, dt=F32):
            return ctx.enter_context(nc.sbuf_tensor(f"m0_{name}", shape, dt))

        names = ("consts", "const", "moments", "rstd", "xn", "xn_out", "xT", "xnT", "scored", "logits",
                 "zeroed0", "zeroed1", "chosen", "counted", "shifted", "exped", "slots", "sent",
                 *(f"{k}{i}" for k in ("x_in", "w_in", "rows_in", "stored") for i in range(4)),
                 "rowsT", "rowsT_out", "hidden", "hidden_act", "hidden_dve", "made", "made_out", "dve", "pool")
        sems = {k: ctx.enter_context(nc.semaphore(f"m0_{k}")) for k in names}
        ps_scores, ps_max, ps_sum, ps_misc = psum
        x_all, xn_all = sb("x_all", [P, NT, D]), sb("xn_all", [P, NT, D])
        xn_T = [sb(f"xn_T{i}", [P, S]) for i in range(2)]
        stats, moments = sb("stats", [P, NT, 6]), sb("moments", [P, NT, 2])
        veps, rstd = sb("veps", [P, NT]), sb("rstd", [P, NT])
        wg = sb("wg", [P, E0])
        logits, shifted, exped, flag, onehot, pos = (sb(k, [P, NT, E0]) for k in ("logits", "shifted", "exped", "flag", "onehot", "pos"))
        run = [sb(f"run{i}", [P, NT, E0]) for i in range(2)]
        onehot_bf = sb("onehot_bf", [P, NT, E0], BF16)
        best, first, loc, start, valid, slot, send = (sb(k, [P, NT]) for k in ("best", "first", "loc", "start", "valid", "slot", "send"))
        send_at = sb("send_at", [P, NT], U32)
        w1 = [sb(f"w1{i}", [P, F0]) for i in range(4)]
        w2 = [sb(f"w2{i}", [P, FC0, D]) for i in range(4)]
        CT = CAP // P
        rows = [sb(f"rows{i}", [P, CT, D]) for i in range(4)]
        rows_T = [sb(f"rows_T{i}", [P, CAP]) for i in range(4)]
        hid = [sb(f"hid{i}", [P, FC0, CAP]) for i in range(2)]
        made = [sb(f"made{i}", [P, CT, D]) for i in range(4)]
        LOADS = 4
        PER = NT // LOADS

        x_src = dram["x"].rearrange("(t p) d -> p t d", p=P)
        xn_dst = dram["xn"].rearrange("(t p) d -> p t d", p=P)
        rows_src = dram["sent0"][0:E0 * CAP, :].rearrange("(e t p) d -> e p t d", e=E0, p=P)
        made_dst = dram["made0"].rearrange("(e t p) d -> e p t d", e=E0, p=P)

        def zero_fill(sp, dst, rows, sem):
            v = dst[0:rows, :].rearrange("(n r) d -> n (r d)", r=w["zeros"].shape[0] * w["zeros"].shape[1] // D)
            zeros = w["zeros"].rearrange("a b -> (a b)")
            for k in range(v.shape[0]):
                sp.dma_start(v[k], zeros).then_inc(sem, 16)
            return 16 * v.shape[0]

        def one(ap, e):
            return ap[e] if isinstance(e, int) else ap[bass.ds(e, 1)].rearrange("o p t d -> (o p) t d")

        def one2(ap, e):
            return ap[e] if isinstance(e, int) else ap[bass.ds(e, 1)].rearrange("o p f -> (o p) f")

        filled0 = 16 * (E0 * CAP * D // w["zeros"].shape[0] // w["zeros"].shape[1])

        with nc.Block() as block:

            @block.sync
            def _(sp):
                for i in range(LOADS):
                    sp.dma_start(x_all[:, i * PER:(i + 1) * PER, :], x_src[:, i * PER:(i + 1) * PER, :]).then_inc(sems[f"x_in{i}"], 16)
                    if i == 0:
                        sp.dma_start(const["all"][:], w["consts"]).then_inc(sems["consts"], 16)
                        sp.dma_start(wg[:], w["gate_w0"]).then_inc(sems["consts"], 16)
                assert zero_fill(sp, dram["sent0"], E0 * CAP, sems["zeroed0"]) == filled0
                sp.wait_ge(sems["xn"], LOADS)
                sp.dma_start(xn_dst, xn_all[:]).then_inc(sems["xn_out"], 16)

                def weights(e, par):
                    sp.dma_start(w1[par][:], one2(w["w1_0"], e)).then_inc(sems[f"w_in{par}"], 16)
                    sp.dma_start(w2[par][:], one(w["w2_0"].rearrange("e (c p) d -> e p c d", p=P), e)).then_inc(sems[f"w_in{par}"], 16)

                def tokens(e, par):
                    sp.dma_start(rows[par][:], one(rows_src, e)).then_inc(sems[f"rows_in{par}"], 16)

                def store(e, par):
                    sp.wait_ge(sems["made_out"], e + 1)
                    sp.dma_start(one(made_dst, e), made[par][:]).then_inc(sems[f"stored{par}"], 16)

                for e in range(4):
                    weights(e, e)
                sp.wait_ge(sems["sent"], 16 * NT)
                for e in range(6):
                    if e >= 4:
                        sp.wait_ge(sems["rowsT"], e - 3)
                    tokens(e, e % 4)
                with sp.Fori(0, E0 // 4 - 2) as i:
                    for par in range(4):
                        e = i * 4 + par
                        store(e, par)
                        weights(e + 4, par)
                        tokens(e + 6, (par + 2) % 4)
                for e in range(E0 - 8, E0):
                    store(e, e % 4)
                    if e + 4 < E0:
                        weights(e + 4, e % 4)
                    if e + 6 < E0:
                        tokens(e + 6, (e + 2) % 4)
                filled1 = zero_fill(sp, dram["sent1"], TILES1 * P, sems["zeroed1"])
                for par in range(4):
                    sp.wait_ge(sems[f"stored{par}"], 16 * (E0 // 4))
                sp.wait_ge(sems["xn_out"], 16)
                sp.wait_ge(sems["zeroed1"], filled1)

            @block.tensor
            def _(pe):
                pe.wait_ge(sems["consts"], 32)
                for b in range(NB):
                    pe.wait_ge(sems["xn"], b * QT // PER + 1)
                    if b >= 2:
                        pe.wait_ge(sems["xnT"], b - 1)
                    for t in range(QT):
                        mm = pe.transpose(ps_max[:, b % 2, t * P:(t + 1) * P], xn_all[:, b * QT + t, :], const["ident"])
                    mm.then_inc(sems["xT"], 1)
                    for last in ([b - 1] if b else []) + ([b] if b == NB - 1 else []):
                        pe.wait_ge(sems["xnT"], last + 1)
                        for t in range(QT):
                            at = (last * QT + t) * E0
                            mm = pe.matmul(ps_scores[:, 0, at:at + E0], xn_T[last % 2][:, t * P:(t + 1) * P], wg[:], start=True, stop=True)
                        mm.then_inc(sems["scored"], 1)
                pe.wait_ge(sems["const"], 2)
                pe.wait_ge(sems["chosen"], 1)
                v = onehot_bf[:].rearrange("p t e -> p (t e)")
                pe.matmul(ps_sum[:], const["before"][:], v, start=True, stop=True)
                pe.matmul(ps_misc[:], const["ones"][:], v, start=True, stop=True).then_inc(sems["counted"], 1)
                pe.wait_ge(sems["slots"], 1)

                def rows_transposed(e, par, fixed):
                    pe.wait_ge(sems[f"rows_in{par}"], uses(e, par, 16) + 16)
                    if fixed is None or fixed >= 2:
                        pe.wait_ge(sems["rowsT_out"], e - 1)
                    for t in range(CT):
                        mm = pe.transpose(ps_max[:, par % 2, t * P:(t + 1) * P], rows[par][:, t, :], const["ident"])
                    mm.then_inc(sems["rowsT"], 1)

                for e in range(2):
                    rows_transposed(e, e, e)
                for k, par, fixed in pipelined(pe, E0, 2):
                    if fixed is None or fixed < E0:
                        pe.wait_ge(sems[f"w_in{par}"], uses(k, par, 32) + 32)
                        pe.wait_ge(sems["rowsT_out"], k + 1)
                        for c in range(FC0):
                            bank, at = 2 * (par % 2) + c // 2, CAP * (c % 2)
                            mm = pe.matmul(ps_scores[:, bank, at:at + CAP], w1[par][:, c * P:(c + 1) * P], rows_T[par][:], start=True, stop=True)
                            if c % 2 == 1:
                                mm.then_inc(sems["hidden"], 1)
                    if fixed is None or fixed < E0 - 2:
                        rows_transposed(k + 2, (par + 2) % 4, None if fixed is None else fixed + 2)
                    if fixed != 0:
                        pe.wait_ge(sems["hidden_act"], k)
                        pe.wait_ge(sems["hidden_dve"], k)
                        if fixed is None or fixed > 2:
                            pe.wait_ge(sems["made_out"], k - 2)
                        last = (par + 3) % 4
                        for t in range(CT):
                            for c in range(FC0):
                                mm = pe.matmul((ps_sum, ps_misc)[last % 2][:, t * D:(t + 1) * D], hid[last % 2][:, c, t * P:(t + 1) * P],
                                               w2[last][:, c, :], start=c == 0, stop=c == FC0 - 1)
                        mm.then_inc(sems["made"], 1)

            @block.scalar
            def _(act):
                for b in range(NB):
                    act.wait_ge(sems["xT"], b + 1)
                    if b >= 2:
                        act.wait_ge(sems["scored"], b - 1)
                    act.activation(xn_T[b % 2][:], ps_max[:, b % 2, :], ACT.Copy).then_inc(sems["xnT"], 1)
                act.wait_ge(sems["shifted"], 1)
                act.activation(exped[:], shifted[:], ACT.Exp).then_inc(sems["exped"], 1)

                def rows_out(e, par):
                    act.wait_ge(sems["rowsT"], e + 1)
                    act.activation(rows_T[par][:], ps_max[:, par % 2, 0:CAP], ACT.Copy).then_inc(sems["rowsT_out"], 1)

                for e in range(2):
                    rows_out(e, e)
                for k, par, fixed in pipelined(act, E0, 2):
                    if fixed is None or fixed < E0:
                        act.wait_ge(sems["hidden"], k * 2 + 1)
                        if fixed is None or fixed > 1:
                            act.wait_ge(sems["made"], k - 1)
                        act.activation(hid[par % 2][:, 0:2, :], ps_scores[:, 2 * (par % 2), :].rearrange("p (c n) -> p c n", c=2),
                                       ACT.Relu).then_inc(sems["hidden_act"], 1)
                    if fixed is None or fixed < E0 - 2:
                        rows_out(k + 2, (par + 2) % 4)

            @block.vector
            def _(dve):
                linked = [0]

                def link(op):
                    linked[0] += 1
                    op.then_inc(sems["dve"], 1)
                    dve.wait_ge(sems["dve"], linked[0])

                link(dve.memset(const["ones"][:], 1.0))
                dve.memset(const["minus_half"][:], -0.5).then_inc(sems["const"], 1)
                for i in range(LOADS):
                    at = slice(i * PER, (i + 1) * PER)
                    dve.wait_ge(sems[f"x_in{i}"], 16)
                    for t in range(i * PER, (i + 1) * PER):
                        op = dve.bn_stats(stats[:, t, :], x_all[:, t, :])
                    link(op)
                    for t in range(i * PER, (i + 1) * PER):
                        op = dve.bn_aggr(moments[:, t, :], stats[:, t, :])
                    op.then_inc(sems["moments"], 1)
                    for last in ([i - 1] if i else []) + ([i] if i == LOADS - 1 else []):
                        dve.wait_ge(sems["rstd"], last + 1)
                        for t in range(last * PER, (last + 1) * PER):
                            op = dve.tensor_scalar(xn_all[:, t, :], x_all[:, t, :], moments[:, t, 0:1], rstd[:, t:t + 1], ALU.subtract, ALU.mult)
                        op.then_inc(sems["xn"], 1)
                dve.wait_ge(sems["consts"], 32)
                for k, at in (("ident_bf", C_IDENT), ("before", C_BEFORE), ("mask_qk", C_MASK_QK), ("mask_kq", C_MASK_KQ)):
                    op = dve.tensor_copy(const[k][:], const["all"][:, at:at + P])
                op.then_inc(sems["const"], 1)
                dve.wait_ge(sems["scored"], NB)
                link(dve.tensor_copy(logits[:], ps_scores[:, 0, :].rearrange("p (t e) -> p t e", t=NT)))
                number = const["all"][:, C_EXP0:C_EXP0 + E0]
                first_best(dve, link, logits[:], E0, number, best, flag, first, onehot)
                dve.tensor_copy(onehot_bf[:], onehot[:]).then_inc(sems["chosen"], 1)
                dve.tensor_tensor(shifted[:], logits[:], best[:].unsqueeze(2).broadcast_to([P, NT, E0]), ALU.subtract).then_inc(sems["shifted"], 1)
                dve.wait_ge(sems["counted"], 1)
                by = "p (t e) -> p t e"
                places(dve, link, ps_sum[:].rearrange(by, e=E0), ps_misc[:].rearrange(by, e=E0), run, pos)
                link(dve.tensor_tensor(pos[:], pos[:], onehot[:], ALU.mult))
                link(dve.tensor_reduce(loc[:], pos[:], AX.X, ALU.add))
                link(dve.tensor_scalar(start[:], first[:], float(E0), float(CAP), ALU.add, ALU.mult))
                link(dve.tensor_scalar(valid[:], loc[:], float(CAP), None, ALU.is_lt))
                link(dve.tensor_tensor(slot[:], start[:], loc[:], ALU.add))
                dump = const["all"][:, C_DUMP:C_DUMP + NT]
                link(dve.tensor_tensor(send[:], slot[:], dump, ALU.subtract))
                link(dve.tensor_tensor(send[:], send[:], valid[:], ALU.mult))
                link(dve.tensor_tensor(send[:], send[:], dump, ALU.add))
                dve.tensor_copy(send_at[:], send[:]).then_inc(sems["slots"], 1)
                link(dve.tensor_scalar(loc[:], loc[:], float(CAP - 1), None, ALU.min))
                link(dve.tensor_tensor(slot[:], start[:], loc[:], ALU.add))
                dve.tensor_copy(route["at"][0][:], slot[:])
                dve.wait_ge(sems["exped"], 1)
                link(dve.tensor_reduce(best[:], exped[:], AX.X, ALU.add))
                link(dve.reciprocal(first[:], best[:]))
                dve.scalar_tensor_tensor(route["weight"][0][:], first[:], 0.5, valid[:], ALU.mult, ALU.mult)
                for k, par, fixed in pipelined(dve, E0, 2):
                    if fixed is None or fixed < E0:
                        dve.wait_ge(sems["hidden"], k * 2 + 2)
                        dve.tensor_scalar(hid[par % 2][:, 2:4, :], ps_scores[:, 2 * (par % 2) + 1, :].rearrange("p (c n) -> p c n", c=2), 0.0, None,
                                          ALU.max).then_inc(sems["hidden_dve"], 1)
                    if fixed != 0:
                        dve.wait_ge(sems["made"], k)
                        last = (par + 3) % 4
                        if fixed is None or fixed > 4:
                            dve.wait_ge(sems[f"stored{last}"], uses(k - 1, last, 16))
                        dve.tensor_copy(made[last][:], (ps_sum, ps_misc)[last % 2][:, 0:CT * D].rearrange("p (t d) -> p t d", t=CT)
                                        ).then_inc(sems["made_out"], 1)

            @block.gpsimd
            def _(pool):
                pool.wait_ge(sems["const"], 1)
                half = const["minus_half"]
                for i in range(LOADS):
                    at = slice(i * PER, (i + 1) * PER)
                    pool.wait_ge(sems["moments"], i + 1)
                    pool.tensor_scalar(veps[:, at], moments[:, at, 1], EPS, None, ALU.add).then_inc(sems["pool"], 1)
                    pool.wait_ge(sems["pool"], i + 1)
                    pool.tensor_tensor(rstd[:, at], veps[:, at], half[:, 0:PER], ALU.pow).then_inc(sems["rstd"], 1)
                pool.wait_ge(sems["zeroed0"], filled0)
                pool.wait_ge(sems["slots"], 1)
                for t in range(NT):
                    pool.indirect_dma_start(dram["sent0"], bass.IndirectOffsetOnAxis(ap=send_at[:, t:t + 1], axis=0),
                                            xn_all[:, t, :], None).then_inc(sems["sent"], 16)


def experts1(nc, const, psum, dram, w, route):
    with ExitStack() as ctx:
        def sb(name, shape, dt=F32):
            return ctx.enter_context(nc.sbuf_tensor(f"m1_{name}", shape, dt))

        names = ("chosen", "counted", "gap", "gap_exp", "slots", "tiles", "all_in", "sent",
                 *(f"{k}{i}" for k in ("pack_in", "rows_in", "stored") for i in range(4)),
                 "rowsT", "rowsT_out", "hidden", "silu", "hidden_out", "made", "made_out", "dve")
        sems = {k: ctx.enter_context(nc.semaphore(f"m1_{k}")) for k in names}
        ps_scores, ps_max, ps_sum, ps_misc = psum
        logits, weight, at = route["logits"], route["weight"], route["at"]
        rest, flag, pos = (sb(k, [P, NT, E1]) for k in ("rest", "flag", "pos"))
        onehot = [sb(f"onehot{i}", [P, NT, E1]) for i in range(TOP + 1)]
        onehot_bf = sb("onehot_bf", [P, NT, E1], BF16)
        run = [sb(f"run{i}", [P, NT, E1]) for i in range(2)]
        best = [sb(f"best{i}", [P, NT]) for i in range(2)]
        first, gap, gap_exp, slot = (sb(k, [P, NT]) for k in ("first", "gap", "gap_exp", "slot"))
        filled = sb("filled", [P, E1, NT])
        used, ends = sb("used", [P, E1]), [sb(f"ends{i}", [P, E1]) for i in range(2)]
        past, tile_e = sb("past", [1, TILES1, E1]), sb("tile_e", [1, TILES1])
        tile_expert = sb("tile_expert", [1, TILES1], I32)
        xn_all = sb("xn_all", [P, NT, D])
        pack = [sb(f"pack{i}", [P, PACK1]) for i in range(4)]
        rows = [sb(f"rows{i}", [P, D]) for i in range(4)]
        rows_T = [sb(f"rows_T{i}", [P, P]) for i in range(4)]
        silu = [sb(f"silu{i}", [P, FC1, P]) for i in range(2)]
        hid = [sb(f"hid{i}", [P, FC1, P]) for i in range(2)]
        made = [sb(f"made{i}", [P, D]) for i in range(4)]
        W2_AT, B_AT, B2_AT = 2 * F1, 2 * F1 + FC1 * D, 2 * F1 + FC1 * D + 2 * FC1
        sent = dram["sent1"].rearrange("(n p) d -> n p d", p=P)
        made_dst = dram["made1"].rearrange("(n p) d -> n p d", p=P)

        def one(ap, k):
            return ap[k] if isinstance(k, int) else ap[bass.ds(k, 1)].rearrange("o p d -> (o p) d")

        with nc.Block() as block:

            @block.sync
            def _(sp):
                sp.dma_start(xn_all[:], dram["xn2"].rearrange("(t p) d -> p t d", p=P)).then_inc(sems["all_in"], 16)
                sp.wait_ge(sems["tiles"], 1)

                def weights(k, par):
                    e = sp.value_load(tile_expert[0:1, k:k + 1] if isinstance(k, int) else tile_expert[0:1, bass.ds(k, 1)],
                                      min_val=0, max_val=E1 - 1)
                    sp.dma_start(pack[par][:], one(w["pack1"], e)).then_inc(sems[f"pack_in{par}"], 16)

                def tokens(k, par):
                    sp.dma_start(rows[par][:], one(sent, k)).then_inc(sems[f"rows_in{par}"], 16)

                def store(k, par):
                    sp.wait_ge(sems["made_out"], k + 1)
                    sp.dma_start(one(made_dst, k), made[par][:]).then_inc(sems[f"stored{par}"], 16)

                for k in range(4):
                    weights(k, k)
                sp.wait_ge(sems["sent"], 16 * NT * TOP)
                for k in range(6):
                    if k >= 4:
                        sp.wait_ge(sems["rowsT"], k - 3)
                    tokens(k, k % 4)
                with sp.Fori(0, TILES1 // 4 - 2) as i:
                    for par in range(4):
                        k = i * 4 + par
                        store(k, par)
                        weights(k + 4, par)
                        tokens(k + 6, (par + 2) % 4)
                for k in range(TILES1 - 8, TILES1):
                    store(k, k % 4)
                    if k + 4 < TILES1:
                        weights(k + 4, k % 4)
                    if k + 6 < TILES1:
                        tokens(k + 6, (k + 2) % 4)
                for par in range(4):
                    sp.wait_ge(sems[f"stored{par}"], 16 * (TILES1 // 4))

            @block.tensor
            def _(pe):
                pe.wait_ge(sems["chosen"], 1)
                v = onehot_bf[:].rearrange("p t e -> p (t e)")
                pe.matmul(ps_sum[:, 0:NT * E1], const["before"][:], v, start=True, stop=True)
                pe.matmul(ps_misc[:, 0:NT * E1], const["ones"][:], v, start=True, stop=True).then_inc(sems["counted"], 1)
                pe.wait_ge(sems["slots"], 1)

                def rows_transposed(k, par, fixed):
                    pe.wait_ge(sems[f"rows_in{par}"], uses(k, par, 16) + 16)
                    if fixed is None or fixed >= 2:
                        pe.wait_ge(sems["rowsT_out"], k - 1)
                    pe.transpose(ps_max[:, par % 2, 0:P], rows[par][:], const["ident"]).then_inc(sems["rowsT"], 1)

                for k in range(2):
                    rows_transposed(k, k, k)
                for k, par, fixed in pipelined(pe, TILES1, 2):
                    if fixed is None or fixed < TILES1:
                        pe.wait_ge(sems[f"pack_in{par}"], uses(k, par, 16) + 16)
                        pe.wait_ge(sems["rowsT_out"], k + 1)
                        for c in range(2 * FC1):
                            mm = pe.matmul(ps_scores[:, par, c * P:(c + 1) * P], pack[par][:, c * P:(c + 1) * P], rows_T[par][:], start=True, stop=True)
                        mm.then_inc(sems["hidden"], 1)
                    if fixed is None or fixed < TILES1 - 2:
                        rows_transposed(k + 2, (par + 2) % 4, None if fixed is None else fixed + 2)
                    if fixed != 0:
                        last = (par + 3) % 4
                        pe.wait_ge(sems["hidden_out"], k)
                        if fixed is None or fixed > 2:
                            pe.wait_ge(sems["made_out"], k - 2)
                        for c in range(FC1):
                            mm = pe.matmul((ps_sum, ps_misc)[last % 2][:, 0:D], hid[last % 2][:, c, :],
                                           pack[last][:, W2_AT + c * D:W2_AT + (c + 1) * D], start=c == 0, stop=c == FC1 - 1)
                        mm.then_inc(sems["made"], 1)

            @block.scalar
            def _(act):
                act.wait_ge(sems["gap"], 1)
                act.activation(gap_exp[:], gap[:], ACT.Exp).then_inc(sems["gap_exp"], 1)
                for k, par, fixed in pipelined(act, TILES1, 2):
                    if fixed == TILES1:
                        continue
                    act.wait_ge(sems["hidden"], k + 1)
                    if fixed is None or fixed > 1:
                        act.wait_ge(sems["hidden_out"], k - 1)
                    for c in range(FC1):
                        op = act.activation(silu[par % 2][:, c, :], ps_scores[:, par, (FC1 + c) * P:(FC1 + c + 1) * P], ACT.Silu,
                                            bias=pack[par][:, B_AT + FC1 + c:B_AT + FC1 + c + 1])
                    op.then_inc(sems["silu"], 1)

            @block.vector
            def _(dve):
                linked = [0]

                def link(op):
                    linked[0] += 1
                    op.then_inc(sems["dve"], 1)
                    dve.wait_ge(sems["dve"], linked[0])

                number = const["all"][:, C_EXP1:C_EXP1 + E1]
                first_best(dve, link, logits[:], E1, number, best[0], flag, first, onehot[0])
                link(dve.scalar_tensor_tensor(rest[:], onehot[0][:], MASK, logits[:], ALU.mult, ALU.add))
                first_best(dve, link, rest[:], E1, number, best[1], flag, first, onehot[1])
                link(dve.tensor_tensor(onehot[2][:], onehot[0][:], onehot[1][:], ALU.add))
                dve.tensor_copy(onehot_bf[:], onehot[2][:]).then_inc(sems["chosen"], 1)
                dve.tensor_tensor(gap[:], best[1][:], best[0][:], ALU.subtract).then_inc(sems["gap"], 1)
                dve.wait_ge(sems["counted"], 1)
                by = "p (t e) -> p t e"
                total = places(dve, link, ps_sum[:, 0:NT * E1].rearrange(by, e=E1), ps_misc[:, 0:NT * E1].rearrange(by, e=E1), run, pos)
                link(dve.tensor_tensor(filled[:], total[:, NT - 1, :].unsqueeze(2).broadcast_to([P, E1, NT]),
                                       const["all"][:, C_FILL:C_FILL + NT].unsqueeze(1).broadcast_to([P, E1, NT]), ALU.is_gt))
                link(dve.tensor_reduce(used[:], filled[:], AX.X, ALU.add))
                link(dve.tensor_copy(ends[0][:], used[:]))
                a, b, k = 0, 1, 1
                while k < E1:
                    dve.tensor_copy(ends[b][:, 0:k], ends[a][:, 0:k])
                    link(dve.tensor_tensor(ends[b][:, k:E1], ends[a][:, k:E1], ends[a][:, 0:E1 - k], ALU.add))
                    a, b, k = b, a, 2 * k
                link(dve.tensor_tensor(past[:], const["all"][0:1, C_TILE:C_TILE + TILES1].unsqueeze(2).broadcast_to([1, TILES1, E1]),
                                       ends[a][0:1, :].unsqueeze(1).broadcast_to([1, TILES1, E1]), ALU.is_ge))
                link(dve.tensor_reduce(tile_e[:], past[:], AX.X, ALU.add))
                link(dve.tensor_scalar(tile_e[:], tile_e[:], float(E1 - 1), None, ALU.min))
                dve.tensor_copy(tile_expert[:], tile_e[:]).then_inc(sems["tiles"], 1)
                link(dve.tensor_tensor(ends[b][:], ends[a][:], used[:], ALU.subtract))
                link(dve.tensor_scalar(ends[b][:], ends[b][:], float(P), None, ALU.mult))
                link(dve.tensor_tensor(pos[:], pos[:], ends[b][:].unsqueeze(1).broadcast_to([P, NT, E1]), ALU.add))
                for i in range(TOP):
                    link(dve.tensor_tensor(flag[:], pos[:], onehot[i][:], ALU.mult))
                    link(dve.tensor_reduce(slot[:], flag[:], AX.X, ALU.add))
                    op = dve.tensor_copy(at[i][:], slot[:])
                    if i == 0:
                        link(op)
                op.then_inc(sems["slots"], 1)
                dve.wait_ge(sems["gap_exp"], 1)
                link(dve.tensor_scalar(first[:], gap_exp[:], 1.0, 2.0, ALU.add, ALU.mult))
                link(dve.reciprocal(weight[0][:], first[:]))
                dve.tensor_tensor(weight[1][:], gap_exp[:], weight[0][:], ALU.mult)

                def rows_out(k, par):
                    dve.wait_ge(sems["rowsT"], k + 1)
                    dve.tensor_copy(rows_T[par][:], ps_max[:, par % 2, 0:P]).then_inc(sems["rowsT_out"], 1)

                for k in range(2):
                    rows_out(k, k)
                for k, par, fixed in pipelined(dve, TILES1, 2):
                    if fixed is None or fixed < TILES1:
                        dve.wait_ge(sems["silu"], k + 1)
                        for c in range(FC1):
                            op = dve.scalar_tensor_tensor(hid[par % 2][:, c, :], ps_scores[:, par, c * P:(c + 1) * P],
                                                          pack[par][:, B_AT + c:B_AT + c + 1], silu[par % 2][:, c, :], ALU.add, ALU.mult)
                        op.then_inc(sems["hidden_out"], 1)
                    if fixed is None or fixed < TILES1 - 2:
                        rows_out(k + 2, (par + 2) % 4)
                    if fixed != 0:
                        last = (par + 3) % 4
                        dve.wait_ge(sems["made"], k)
                        if fixed is None or fixed > 4:
                            dve.wait_ge(sems[f"stored{last}"], uses(k - 1, last, 16))
                        dve.tensor_tensor(made[last][:], (ps_sum, ps_misc)[last % 2][:, 0:D], pack[last][:, B2_AT:B2_AT + D],
                                          ALU.add).then_inc(sems["made_out"], 1)

            @block.gpsimd
            def _(pool):
                pool.wait_ge(sems["all_in"], 16)
                pool.wait_ge(sems["slots"], 1)
                for t in range(NT):
                    for i in range(TOP):
                        pool.indirect_dma_start(dram["sent1"], bass.IndirectOffsetOnAxis(ap=at[i][:, t:t + 1], axis=0),
                                                xn_all[:, t, :], None).then_inc(sems["sent"], 16)


def build(nc, w, out):
    with ExitStack() as ctx:
        def sb(name, shape, dt=F32):
            return ctx.enter_context(nc.sbuf_tensor(name, shape, dt))

        def ps(name, shape):
            return ctx.enter_context(nc.psum_tensor(name, shape, F32))

        def scratch(name, shape, dt=F32):
            return nc.dram_tensor(name, shape, dt, kind="Internal").ap()

        psum = (ps("ps_scores", [P, 4, S]), ps("ps_max", [P, 2, S]), ps("ps_sum", [P, S]), ps("ps_misc", [P, S]))
        dram = {
            "x": w["x"], "xn": scratch("xn", [NB * S, D]), "x2": scratch("x2", [NB * S, D]), "xn2": scratch("xn2", [NB * S, D]),
            "q": scratch("q_rows", [H, ROW_END, S], BF16), "k": scratch("k_rows", [H, ROW_END, S], BF16),
            "sent0": scratch("sent0", [E0 * CAP + NB * S, D]), "made0": scratch("made0", [E0 * CAP, D]),
            "sent1": scratch("sent1", [TILES1 * P, D]), "made1": scratch("made1", [TILES1 * P, D]),
        }
        every = sb("consts", [P, C_END])
        const = {
            "all": every, "ident": every[:, C_IDENT:C_IDENT + P], "holt": every[:, C_HOLT:C_END],
            "minus_half": sb("minus_half", [P, 2 * QT]), "ones": sb("ones", [P, P], BF16),
            **{k: sb(k, [P, P], BF16) for k in ("ident_bf", "before", "mask_qk", "mask_kq")},
        }
        routes = [{"at": [sb(f"at{n}{i}", [P, NT], U32) for i in range(k)], "weight": [sb(f"weight{n}{i}", [P, NT]) for i in range(k)]}
                  for n, k in ((0, 1), (1, TOP))]
        routes[0]["logits"] = routes[1]["logits"] = sb("logits1", [P, NT, E1])
        experts0(nc, const, psum, dram, w, routes[0])
        attention(nc, 0, const, psum, {**dram, "moe": dram["made0"]}, w["attn0"], routes[0], out)
        experts1(nc, const, psum, dram, w, routes[1])
        attention(nc, 1, const, psum, {**dram, "moe": dram["made1"]}, w["attn1"], routes[1], out)


def layout(v):
    f = {k: np.asarray(a) for k, a in v.items()}

    order = np.arange(P).reshape(NG, 2, HD).transpose(1, 0, 2).reshape(P)

    def pair(name):
        m = np.zeros((P, P), np.float32)
        m[:HALF, :HALF], m[HALF:, HALF:] = f[f"L0_attn_{name}1"].T, f[f"L0_attn_{name}2"].T
        return m[:, order] if name in ("wq", "wk") else m

    def both(name):
        return np.concatenate([f[f"L0_attn_{name}1"], f[f"L0_attn_{name}2"]])

    pack = np.concatenate([
        f["L1_ffn_w0"].transpose(0, 2, 1), f["L1_ffn_w1"].transpose(0, 2, 1),
        f["L1_ffn_w2"].transpose(0, 2, 1).reshape(E1, FC1, P, D).transpose(0, 2, 1, 3).reshape(E1, P, FC1 * D),
        f["L1_ffn_b0"].reshape(E1, FC1, P).transpose(0, 2, 1), f["L1_ffn_b1"].reshape(E1, FC1, P).transpose(0, 2, 1),
        np.repeat(f["L1_ffn_b2"][:, None, :], P, 1)], 2)
    return {
        "x": f["L0_attn_x"].reshape(NB * S, D), "zeros": np.zeros((P, 1024), np.float32), "consts": constants(), "alibi": alibi(),
        "gate_w0": f["L0_ffn_Wg"], "w1_0": f["L0_ffn_w1"], "w2_0": f["L0_ffn_w2"], "pack1": pack,
        **{f"a0_w{k}": pair(f"w{k}") for k in "qkvo"},
        **{f"a0_b{k}": both(f"b{k}")[order].reshape(P, 1) if k in "qk" else both(f"b{k}") for k in "qkvo"},
        "a0_g12": both("g"), "a0_be12": both("be"),
        "a0_w_ff1": f["L0_attn_w_ff1"].T, "a0_b_ff1": f["L0_attn_b_ff1"].reshape(FC0, P).T,
        "a0_w_ff2": f["L0_attn_w_ff2"].T.reshape(FC0, P, D).transpose(1, 0, 2), "a0_b_ff2": f["L0_attn_b_ff2"],
        "a0_g_ff": f["L0_attn_g_ff"], "a0_be_ff": f["L0_attn_be_ff"],
        "a0_gate_w1": f["L1_ffn_gate_w"].T, "a0_gate_b1": f["L1_ffn_gate_b"],
        **{f"a1_w{k}": f[f"L1_attn_W{k}"].T[:, order if k in "qk" else slice(None)] for k in "qkvo"},
    }


def kernel(**inputs):
    import concourse.bacc as bacc
    from concourse.bass_utils import run_bass_kernel_spmd

    nc = bacc.Bacc("TRN2", target_bir_lowering=False, num_devices=1)
    arrays = {k: np.ascontiguousarray(a) for k, a in layout(inputs).items()}
    aps = {k: nc.dram_tensor(f"in_{k}", a.shape, mybir.dt.from_np(a.dtype), kind="ExternalInput").ap() for k, a in arrays.items()}
    w = {k: a for k, a in aps.items() if k[:2] not in ("a0", "a1")}
    w["attn0"] = {k[3:]: a for k, a in aps.items() if k.startswith("a0_")}
    w["attn1"] = {**{k[3:]: a for k, a in aps.items() if k.startswith("a1_")}, "alibi": aps["alibi"]}
    out = nc.dram_tensor("out", (NB * S, D), F32, kind="ExternalOutput").ap()
    build(nc, w, out)
    r = run_bass_kernel_spmd(nc, [{f"in_{k}": a for k, a in arrays.items()}], core_ids=[0])
    return r.results[0]["out"].reshape(NB, S, D)
```

```python
import math
from contextlib import ExitStack

import numpy as np

import concourse.bass as bass
from concourse import mybir

F32, BF16 = mybir.dt.float32, mybir.dt.bfloat16
U32, I32 = mybir.dt.uint32, mybir.dt.int32
ALU = mybir.AluOpType
ACT = mybir.ActivationFunctionType
AX = mybir.AxisListType

P = 128
NB, S, D = 8, 512, 128
QT = S // P
NT = NB * QT
HD, H = 8, 16
HALF = D // 2
NG = H // 2
STRIP = 64
PARTS = 6
ROW_SHIFT = PARTS * HD
ROW_ALIBI = ROW_SHIFT + 2
ROW_END = ROW_ALIBI + 3
VW = 32
SCALE = 1.0 / math.sqrt(HD)
EPS = 1e-5
MASK = -1.0e30

E0, F0 = 16, 512
CAP = NB * S // E0
FC0 = F0 // P
E1, F1, TOP = 8, 256, 2
FC1 = F1 // P
SLOTS1 = 2 * P
CT1 = SLOTS1 // P
TILES1 = NB * S * TOP // SLOTS1 + E1
FILLS = NB * S // SLOTS1
PACK1 = 2 * F1 + FC1 * D + 2 * FC1 + D

C_IDENT = 0
C_BEFORE = C_IDENT + P
C_MASK_QK = C_BEFORE + P
C_MASK_KQ = C_MASK_QK + P
C_EXP0 = C_MASK_KQ + P
C_EXP1 = C_EXP0 + E0
C_FILL = C_EXP1 + E1
C_DUMP = C_FILL + FILLS
C_TILE = C_DUMP + NT
C_HOLT = C_TILE + TILES1
N_HOLT = QT * (QT + 1) // 2
C_END = C_HOLT + N_HOLT * P


def holt_block(st, tt):
    return st * QT - st * (st - 1) // 2 + tt - st


def constants():
    c = np.zeros((P, C_END), np.float32)
    n = np.arange(P)
    c[:, C_IDENT:C_IDENT + P] = np.eye(P)
    c[:, C_BEFORE:C_BEFORE + P] = n[:, None] < n[None, :]
    c[:, C_MASK_QK:C_MASK_QK + P] = np.where(n[None, :] > n[:, None], MASK, 0)
    c[:, C_MASK_KQ:C_MASK_KQ + P] = np.where(n[:, None] > n[None, :], MASK, 0)
    c[:, C_EXP0:C_EXP0 + E0] = np.arange(E0) - E0
    c[:, C_EXP1:C_EXP1 + E1] = np.arange(E1) - E1
    c[:, C_FILL:C_FILL + FILLS] = SLOTS1 * np.arange(FILLS)
    c[:, C_DUMP:C_DUMP + NT] = E0 * CAP + P * np.arange(NT)[None, :] + n[:, None]
    c[:, C_TILE:C_TILE + TILES1] = np.arange(TILES1)
    alpha, beta = 0.1, 0.1
    level, trend = np.zeros(S), np.zeros(S)
    level[0] = 1.0
    rows = [level]
    for t in range(1, S):
        x = np.zeros(S)
        x[t] = 1.0
        new = alpha * x + (1 - alpha) * (level + trend)
        trend = beta * (new - level) + (1 - beta) * trend
        level = new
        rows.append(level)
    holt = np.stack(rows, 1)
    for st in range(QT):
        for tt in range(st, QT):
            at = C_HOLT + holt_block(st, tt) * P
            c[:, at:at + P] = holt[st * P:(st + 1) * P, tt * P:(tt + 1) * P]
    return c


def alibi():
    base = 2.0 ** (-8.0 / H)
    slopes = np.array([np.float32(base ** i) for i in range(1, H + 1)], np.float32)
    order = [2 * g + j for j in range(2) for g in range(NG)]
    return (slopes[order][:, None] * (np.arange(S) - S // 2)[None, :].astype(np.float32)).astype(np.float32)


class Tally:

    def __init__(self, adds):
        self.adds, self.n, self.trip, self.per = adds, {}, None, {}

    def at(self, name):
        v = self.n.get(name, 0)
        return v if self.trip is None else self.trip * self.per.get(name, 0) + v

    def step(self, step):
        for name, k in self.adds(step).items():
            self.n[name] = self.n.get(name, 0) + k

    def enter(self, trip, steps):
        self.trip, self.per = trip, {}
        for s in steps:
            for name, k in self.adds(s).items():
                self.per[name] = self.per.get(name, 0) + k

    def leave(self, trips):
        for name, k in self.per.items():
            self.n[name] = self.n.get(name, 0) + k * (trips - 1)
        self.trip = None


def wait(eng, sem, value):
    if isinstance(value, int) and value <= 0:
        return
    eng.wait_ge(sem, value)


def wait_apart(eng, sem, value, apart):
    wait(eng, sem, value)
    if not isinstance(value, int):
        eng.sem_inc(apart, 1)


STREAM = 2 * NB
ROUTE1 = NB + 1
MIX1 = NB + 3
GROUPS = H
MAX_TILES = H * QT
PER_GROUP = MAX_TILES // GROUPS
FIRST_MAX = 3

MISC = {
    0: {0: [("gather", -1)], 2: [("norm", -1, QT - 1)], 3: [("v", 1)], 4: [("onT", -1)],
        6: [("proj", -1)], 7: [("z", 1)], 8: [("shift", 0, 1)], 9: [("ln1", -1), ("zT", 2)],
        10: [("norm", 0, 0)], 11: [("q", 2)], 12: [("yT", -1)], 13: [("ff1", -1, 0)],
        14: [("ff1", -1, 1)], 15: [("ff1", -1, 2)], 17: [("ff1", -1, 3), ("k", 2)],
        18: [("norm", 0, 1)], 19: [("gate", -1)], 20: [("ff2", -1)], 22: [("shift", 1, 0)],
        23: [("ln2", -1)], 25: [("mix", -1)], 26: [("norm", 0, 2)], 27: [("ln3a", -1)],
        28: [("ln3b", -1)], 30: [("x2T", -1)], 31: [("logits", -1)]},
    1: {2: [("norm", -1, QT - 1)], 3: [("v", 1)], 4: [("onT", -1)], 8: [("shift", 0, 1)],
        9: [("zT", 2)], 11: [("q", 2)], 12: [("norm", 0, 0)], 15: [("k", 2)], 17: [("proj", -1)],
        18: [("norm", 0, 1)], 22: [("shift", 1, 0)], 26: [("norm", 0, 2)]},
}

EXTRA = {
    ROUTE1: {0: [("choose", 0)], 5: [("count", 0)], 6: [("send", 0, 0)], 15: [("weigh", 0)]},
    ROUTE1 + 1: {0: [("send", 0, 1)], 17: [("send", 0, 2)]},
    MIX1: {0: [("loadx", -3), ("gather", -3)], 10: [("gate", -3)], 14: [("mix", -3)],
           15: [("loadx", -2), ("gather", -2)], 26: [("gate", -2)], 30: [("mix", -2)]},
    MIX1 + 1: {0: [("loadx", -2), ("gather", -2)], 10: [("gate", -2)], 14: [("mix", -2)],
               17: [("loadx", -1), ("gather", -1)], 26: [("gate", -1)], 30: [("mix", -1)]},
    **{b: {0: [("loadx", -1), ("gather", -1)], 24: [("gate", -1)], 30: [("mix", -1)]} for b in range(MIX1 + 2, STREAM + 1)},
}


def plan(b):
    def live(d):
        return 0 <= b + d < STREAM

    def layer(d):
        return min(b + d, STREAM - 1) // NB

    steps = []

    def add(name, d, arg=0):
        steps.append((name, d, arg, layer(d)))

    def misc(place):
        for k in range(2):
            for step in MISC[k].get(place, []):
                if live(step[1]) and layer(step[1]) == k:
                    name, d, *arg = step
                    if name == "shift":
                        arg = [(*arg, since(d, *arg))]
                    add(name, d, *arg)
        for step in EXTRA.get(b, {}).get(place, []):
            add(*step)

    def since(d, half):
        taken = [(at, arg) for name, at, arg, _ in steps if name == "max"]
        return len(taken) - 1 - taken.index((d, (half + 1) * MAX_TILES // 2 - 1))

    def maxima(d, first, count):
        for m in range(first, first + count):
            if live(d):
                add("max", d, m)

    if live(1):
        add("fetch", 1)
    if live(2):
        add("load", 2)
    if live(-1) and layer(-1) == 0:
        add("loadx", -1)
    for n in range(GROUPS):
        d = 1 if n >= FIRST_MAX else 0
        first, part = PER_GROUP * ((n - FIRST_MAX) % GROUPS), PER_GROUP // 2
        if live(0):
            add("exp", 0, n)
        maxima(d, first, part)
        misc(2 * n)
        if n == 0 and live(-1):
            add("sum", -1, (GROUPS - 1, live(0)))
            add("take", -1, QT - 1)
        elif n > 0 and live(0):
            add("sum", 0, (n - 1, True))
            if n % QT == 0:
                add("take", 0, n // QT - 1)
        maxima(d, first + part, PER_GROUP - part)
        misc(2 * n + 1)
    return steps


WORK = 18 * S
FETCHES = 2 * 2
LN_TILES = {"proj": 2 * QT, "ff2": QT, "ln3a": QT}


def adds(step):
    name, d, arg, layer = step
    both = {"misc": 1, "misc_free": 1}
    table = {
        "load": {"z_in": 16}, "loadx": {"x_in": 16},
        "exp": {"scores": 2, "probs": 2}, "sum": {"summed": 1}, "take": {"taken": 1},
        "norm": {**both, "dve": 1},
        "zT": both, "q": {**both, "split": 1, "pool": 2, "q_out": 16 * PARTS}, "k": {**both, "split": 1, "pool": 2, "k_out": 16 * PARTS},
        "v": both, "z": both, "fetch": {"strips": 16 * FETCHES},
        "max": {"max_in": 1, "max_out": 1}, "shift": {**both, "dve": 1, "shift_in": 64},
        "onT": both, "yT": {**both}, "ff1": both, "x2T": both, "logits": both,
        "proj": {**both, "dve": 1, "moments": 1, "rstd": 1, "pool": 1} if layer == 0 else both,
        "ln1": {"dve": 1, "centred": 1, "pool": 1, "y": 1, "yb": 1},
        "ff2": {**both, "dve": 1, "moments": 1, "rstd": 1, "pool": 1},
        "ln2": {"normed": 1, "pool": 1, "s": 1},
        "gather": {"picks": 1, "rows": 16 * QT * (1 if layer == 0 else TOP)},
        "gate": {"gate_in": 1, "gate_tanh": 1, "pool": 0 if layer == 0 else 1},
        "mix": {"gate_out": 1, "pool": 1, "x2": 1, "x2_out": 16},
        "ln3a": {"dve": 1, "moments": 1, "rstd": 1, "pool": 1},
        "ln3b": {"xn2": 1, "xn2_out": 16},
        "choose": {}, "count": both, "weigh": {}, "send": {},
    }
    return table[name]


def batches(eng, n):
    for b in (-2, -1, 0, 1):
        yield b, b % 2, plan(b)
    trips = (NB - 4) // 2
    with eng.Fori(0, trips) as trip:
        n.enter(trip, plan(2) + plan(3))
        for half in range(2):
            yield trip * 2 + 2 + half, half, plan(2 + half)
        n.leave(trips)
    for b in range(2 + 2 * trips, STREAM + 1):
        yield b, b % 2, plan(b)


def is_iteration(b, k):
    return isinstance(b, int) and b == k


def of_batch(ap, b):
    if isinstance(b, int):
        return ap[b]
    return ap[bass.ds(b, 1)].rearrange("o p t d -> (o p) t d")


def columns(buf):
    at = [0]

    def take(n):
        at[0] += n
        return buf[:, at[0] - n:at[0]]
    return take


def attention(nc, const, psum, strips, late, work, dram, weights, routes, out, experts_of):
    with ExitStack() as ctx:
        def sb(name, shape, dt=F32):
            return ctx.enter_context(nc.sbuf_tensor(f"a_{name}", shape, dt))

        sems = {k: ctx.enter_context(nc.semaphore(f"a_{k}")) for k in (
            "z_in", "x_in", "scores", "probs", "summed", "taken", "misc", "misc_free", "split",
            "q_out", "k_out", "strips", "max_in", "max_out", "shift_in", "moments", "rstd", "centred",
            "y", "yb", "normed", "s", "picks", "rows", "gate_in", "gate_tanh", "gate_out",
            "x2", "x2_out", "xn2", "xn2_out", "dve", "pool", "apart")}
        ps_scores, ps_max, ps_sum, ps_misc = psum

        q_strip, k_strip, v_aug = strips["q"], strips["k"], strips["v"]
        probs = [sb(f"probs{i}", [P, 4, S]) for i in range(2)]
        z_in, z_T = sb("z_in", [P, QT, D]), sb("z_T", [P, S])
        whole = {k: sb(f"{k}_whole", [P, S]) for k in "qk"}
        parts = {k: sb(f"{k}_parts", [P, 3, S], BF16) for k in "qk"}
        rest = sb("rest", [P, S])
        neg_max = sb("neg_max", [P, QT, 2, NG])
        shift = sb("shift", [NG, 2, S], BF16)
        o_strip = [sb(f"o_strip{i}", [P, S]) for i in range(2)]
        o_norm = [sb(f"o_norm{i}", [P, QT, D]) for i in range(2)]
        o_den = sb("o_den", [P, QT, 4])
        o_T = sb("o_T", [P, S])
        resid = [sb(f"resid{i}", [P, QT, D]) for i in range(2)]
        z, e, gz, sg, *others = (late[:, QT * i:QT * (i + 1), :] for i in range(NB))
        gathered = (others[:1], others[:TOP])
        y0, y1, y2 = others[1:]
        z_both = others[TOP:]
        take = columns(work)
        x_in, x2, s0_out, xn2, y3, y, yb, t0, t1, t2 = (take(S).rearrange("p (t d) -> p t d", t=QT) for _ in range(10))
        y_T, xn2_T, hid = take(S), take(S), take(FC0 * S).rearrange("p (c n) -> p c n", c=FC0)
        s1_out = resid
        row_at = [sb(f"row_at{i}", [P, QT], U32) for i in range(TOP)]
        row_w = [sb(f"row_w{i}", [P, QT]) for i in range(TOP)]
        stats, moments = sb("stats", [P, 2 * QT, 6]), sb("moments", [P, 2 * QT, 2])
        veps, rstd = sb("veps", [P, 2 * QT]), sb("rstd", [P, 2 * QT])
        w_of = weights["by_layer"]
        w_ff1, w_ff2, b_ff1, bv, bo, g12, be12, b_ff2, g_ff, be_ff, wg, bg = (weights[k] for k in (
            "w_ff1", "w_ff2", "b_ff1", "bv", "bo", "g12", "be12", "b_ff2", "g_ff", "be_ff", "gate_w1", "gate_b1"))
        bqk = {"q": weights["bqs"], "k": weights["bk"]}
        strip_rows = ({"q": ROW_ALIBI, "k": ROW_ALIBI}, {"q": ROW_ALIBI, "k": ROW_END})

        ident, ident_bf = const["ident"], const["ident_bf"]

        def by_batch(ap):
            return ap.rearrange("(b t p) d -> b p t d", b=NB, p=P)
        z_src = (by_batch(dram["xn"]), by_batch(dram["xn2"]))
        x_src = (by_batch(dram["x"]), by_batch(dram["x2"]))
        x_dst = (by_batch(dram["x2"]), by_batch(out))
        xn_dst = by_batch(dram["xn2"])
        moe = (dram["made0"], dram["made1"])

        def cols(kt, causal):
            return (kt * P if causal else 0), S

        def keys(qt, causal):
            return (qt + 1) * P if causal else S

        def head(m):
            half, r = divmod(m, MAX_TILES // 2)
            hd, qt = divmod(r, QT)
            return half, hd % 2, hd // 2, qt

        (experts0_sems, experts0), (experts1_sems, experts1) = experts_of(ctx, probs)

        with nc.Block() as block:

            @block.sync
            def _(sp):
                n = Tally(adds)
                for b, odd, steps in batches(sp, n):
                    if is_iteration(b, 1):
                        experts0["tiles_sync"](sp)
                    if is_iteration(b, MIX1):
                        experts1["tiles_sync"](sp)
                    for step in steps:
                        name, d, arg, layer = step
                        at = b + d - NB * layer
                        par = (odd + d) % 2
                        if name == "load":
                            if layer == 1:
                                wait(sp, sems["xn2_out"], 16 * (at + 1))
                            sp.dma_start(z_in[:], of_batch(z_src[layer], at)).then_inc(sems["z_in"], 16)
                        if name == "loadx":
                            if layer == 1:
                                wait(sp, sems["x2_out"], 16 * (at + 1))
                            sp.dma_start(x_in[:], of_batch(x_src[layer], at)).then_inc(sems["x_in"], 16)
                        if name in ("q", "k"):
                            wait_apart(sp, sems["strips"], n.at("strips"), sems["apart"])
                            wait(sp, sems["split"], n.at("split") + 1)
                            order = (0, 0, 0, 1, 1, 2) if name == "q" else (0, 1, 2, 0, 1, 0)
                            for a in range(PARTS):
                                sp.dma_start(dram[name][:, HD * a:HD * (a + 1)],
                                             parts[name][:, order[a], :]).then_inc(sems[f"{name}_out"], 16)
                        if name == "fetch":
                            wait_apart(sp, sems["q_out"], n.at("q_out"), sems["apart"])
                            wait_apart(sp, sems["k_out"], n.at("k_out"), sems["apart"])
                            wait(sp, sems["scores"], n.at("scores"))
                            for j in range(2):
                                for k, strip, slots in (("q", q_strip, slice(0, NG)), ("k", k_strip, slice(NG * j, NG * (j + 1)))):
                                    sp.dma_start(strip[par][STRIP * j:STRIP * j + strip_rows[layer][k], slots, :],
                                                 dram[k][NG * j:NG * (j + 1), 0:strip_rows[layer][k]].rearrange("g r n -> r g n")).then_inc(sems["strips"], 16)
                        if name == "shift":
                            wait(sp, sems["misc_free"], n.at("misc_free") + 1)
                            half, _ = arg
                            for j in range(2):
                                for a in range(2):
                                    r = STRIP * j + ROW_SHIFT + a
                                    sp.dma_start(q_strip[par][r:r + 1, half * QT:(half + 1) * QT, :],
                                                 shift[j * QT:(j + 1) * QT, a, :]).then_inc(sems["shift_in"], 16)
                        if name == "mix":
                            wait(sp, sems["x2"], n.at("x2") + 1)
                            sp.dma_start(of_batch(x_dst[layer], at), x2[:]).then_inc(sems["x2_out"], 16)
                        if name == "choose":
                            wait(sp, sems["xn2_out"], n.at("xn2_out"))
                            experts1["route_sync"](sp)
                        if name == "ln3b":
                            wait(sp, sems["xn2"], n.at("xn2") + 1)
                            sp.dma_start(of_batch(xn_dst, at), xn2[:]).then_inc(sems["xn2_out"], 16)
                        n.step(step)
                wait(sp, sems["x2_out"], n.at("x2_out"))
                wait(sp, sems["xn2_out"], n.at("xn2_out"))

            @block.tensor
            def _(pe):
                n = Tally(adds)

                def claim():
                    wait(pe, sems["misc_free"], n.at("misc_free"))

                for b, odd, steps in batches(pe, n):
                    if is_iteration(b, -2):
                        experts0["route_tensor"](pe)
                    if is_iteration(b, -1):
                        wait(pe, experts0_sems["slots"], 1)
                    if is_iteration(b, 1) or is_iteration(b, MIX1):
                        wait(pe, sems["probs"], n.at("probs"))
                        wait(pe, sems["max_out"], n.at("max_out"))
                        claim()
                        (experts0 if b == 1 else experts1)["tiles_tensor"](pe)
                    for step in steps:
                        name, d, arg, layer = step
                        causal = layer == 1
                        par = (odd + d) % 2
                        if name == "exp":
                            u, kt = divmod(arg, QT)
                            lo, hi = cols(kt, causal)
                            if arg in (0, GROUPS // 2):
                                wait(pe, sems["shift_in"], n.at("shift_in"))
                            for g in range(2):
                                slot = 2 * u + g
                                wait(pe, sems["probs"], n.at("probs") + g - 1)
                                for j in range(2):
                                    o = ps_scores[:, 2 * g + j, 0:hi - lo]
                                    mm = pe.matmul(o, k_strip[par][:, NG * j + slot, kt * P:(kt + 1) * P],
                                                   q_strip[par][:, slot, lo:hi], start=True, stop=not causal)
                                    if causal:
                                        mm = pe.matmul(ps_scores[:, 2 * g + j, 0:P], ident_bf[:], const["mask_kq"][:],
                                                       start=False, stop=True)
                                mm.then_inc(sems["scores"], 1)
                        if name == "sum":
                            group, more = arg
                            u, kt = divmod(group, QT)
                            lo, hi = cols(kt, causal)
                            wait(pe, sems["probs"], n.at("probs") - (2 if more else 0))
                            if kt == 0:
                                wait(pe, sems["taken"], n.at("taken"))
                            for c in range(4):
                                mm = pe.matmul(ps_sum[VW * c:VW * (c + 1), lo:hi], v_aug[par][:, kt, 4 * u + c, :],
                                               probs[group % 2][:, c, 0:hi - lo], start=kt == 0, stop=kt == QT - 1)
                            mm.then_inc(sems["summed"], 1)
                        if name == "norm":
                            wait(pe, sems["taken"], n.at("taken"))
                            claim()
                            for t in range(QT):
                                mm = pe.transpose(ps_misc[:, t * P:(t + 1) * P], o_strip[arg % 2][:, t * P:(t + 1) * P], ident[:])
                            mm.then_inc(sems["misc"], 1)
                        if name == "zT":
                            wait(pe, sems["z_in"], n.at("z_in"))
                            wait_apart(pe, sems["misc_free"], n.at("misc_free"), sems["apart"])
                            if layer == 0:
                                for t in range(QT):
                                    pe.transpose(ps_misc[0:HALF, t * P:(t + 1) * P], z_in[:, t, 0:HALF], ident[:])
                                for t in range(QT):
                                    mm = pe.matmul(ps_misc[HALF:P, t * P:S], z_in[:, t, 0:HALF],
                                                   const["holt"][:, holt_block(t, t) * P:(holt_block(t, QT - 1) + 1) * P],
                                                   start=t == 0, stop=t == QT - 1)
                            else:
                                for t in range(QT):
                                    mm = pe.transpose(ps_misc[:, t * P:(t + 1) * P], z_in[:, t, :], ident[:])
                            mm.then_inc(sems["misc"], 1)
                        if name in ("q", "k"):
                            claim()
                            pe.matmul(ps_misc[:], w_of[layer][name][:], z_T[:], start=True, stop=True).then_inc(sems["misc"], 1)
                        if name in ("v", "z"):
                            claim()
                            for t in range(QT):
                                o, i = ps_misc[:, t * P:(t + 1) * P], z_T[:, t * P:(t + 1) * P]
                                mm = pe.matmul(o, i, w_of[layer]["v"][:], start=True, stop=True) if name == "v" else pe.transpose(o, i, ident[:])
                            mm.then_inc(sems["misc"], 1)
                        if name == "max":
                            if arg == 0:
                                wait(pe, sems["strips"], n.at("strips"))
                            half, j, slot, qt = head(arg)
                            slot += QT * half
                            wait(pe, sems["max_out"], n.at("max_out") - 1)
                            o = ps_max[:, arg % 2, 0:keys(qt, causal)]
                            mm = pe.matmul(o, q_strip[par][:, slot, qt * P:(qt + 1) * P], k_strip[par][:, NG * j + slot, 0:keys(qt, causal)],
                                           start=True, stop=not causal)
                            if causal:
                                mm = pe.matmul(ps_max[:, arg % 2, qt * P:(qt + 1) * P], ident_bf[:], const["mask_qk"][:],
                                               start=False, stop=True)
                            mm.then_inc(sems["max_in"], 1)
                        if name == "shift":
                            half, since = arg
                            wait(pe, sems["max_out"], n.at("max_out") - since)
                            claim()
                            for t in range(QT):
                                mm = pe.transpose(ps_misc[0:NG, t * P:(t + 1) * P], neg_max[:, t, half, :], ident[:])
                            mm.then_inc(sems["misc"], 1)
                        if name == "onT":
                            claim()
                            for t in range(QT):
                                mm = pe.transpose(ps_misc[:, t * P:(t + 1) * P], o_norm[par][:, t, :], ident[:])
                            mm.then_inc(sems["misc"], 1)
                        if name == "proj":
                            claim()
                            for t in range(QT):
                                mm = pe.matmul(ps_misc[:, t * P:(t + 1) * P], o_T[:, t * P:(t + 1) * P], w_of[layer]["o"][:], start=True, stop=True)
                            mm.then_inc(sems["misc"], 1)
                        if name == "yT":
                            wait(pe, sems["y"], n.at("y"))
                            claim()
                            for t in range(QT):
                                mm = pe.transpose(ps_misc[:, t * P:(t + 1) * P], y[:, t, :], ident[:])
                            mm.then_inc(sems["misc"], 1)
                        if name == "ff1":
                            claim()
                            pe.matmul(ps_misc[:], w_ff1[:, arg * P:(arg + 1) * P], y_T[:], start=True, stop=True).then_inc(sems["misc"], 1)
                        if name == "ff2":
                            claim()
                            for t in range(QT):
                                for c in range(FC0):
                                    mm = pe.matmul(ps_misc[:, t * P:(t + 1) * P], hid[:, c, t * P:(t + 1) * P], w_ff2[:, c, :],
                                                   start=c == 0, stop=c == FC0 - 1)
                            mm.then_inc(sems["misc"], 1)
                        if name == "count":
                            claim()
                            experts1["route_tensor"](pe).then_inc(sems["misc"], 1)
                        if name == "x2T":
                            wait(pe, sems["xn2"], n.at("xn2"))
                            claim()
                            for t in range(QT):
                                mm = pe.transpose(ps_misc[:, t * P:(t + 1) * P], xn2[:, t, :], ident[:])
                            mm.then_inc(sems["misc"], 1)
                        if name == "logits":
                            claim()
                            for t in range(QT):
                                mm = pe.matmul(ps_misc[:, t * E1:(t + 1) * E1], xn2_T[:, t * P:(t + 1) * P], wg[:], start=True, stop=True)
                            mm.then_inc(sems["misc"], 1)
                        n.step(step)

            @block.scalar
            def _(act):
                n = Tally(adds)
                for b, odd, steps in batches(act, n):
                    if is_iteration(b, -1):
                        experts0["route_scalar"](act)
                    if is_iteration(b, 1):
                        experts0["tiles_scalar"](act)
                    if is_iteration(b, MIX1):
                        experts1["tiles_scalar"](act)
                    for step in steps:
                        name, d, arg, layer = step
                        causal, par = layer == 1, (odd + d) % 2
                        if name == "exp":
                            lo, hi = cols(arg % QT, causal)
                            wait(act, sems["summed"], n.at("summed"))
                            for g in range(2):
                                wait(act, sems["scores"], n.at("scores") + 1 + g)
                                act.activation(probs[arg % 2][:, 2 * g:2 * g + 2, 0:hi - lo], ps_scores[:, 2 * g:2 * g + 2, 0:hi - lo],
                                               ACT.Exp).then_inc(sems["probs"], 1)
                        if name == "take":
                            wait(act, sems["summed"], n.at("summed"))
                            act.activation(o_strip[arg % 2][:], ps_sum[:], ACT.Copy).then_inc(sems["taken"], 1)
                        if name in ("zT", "onT", "yT", "x2T"):
                            wait(act, sems["misc"], n.at("misc") + 1)
                            dst = {"zT": z_T, "onT": o_T}[name] if name in ("zT", "onT") else (y_T if name == "yT" else xn2_T)
                            act.activation(dst[:], ps_misc[:], ACT.Copy).then_inc(sems["misc_free"], 1)
                        if name in ("q", "k"):
                            wait(act, sems["misc"], n.at("misc") + 1)
                            wait(act, sems[f"{name}_out"], n.at(f"{name}_out"))
                            scale = SCALE if name == "q" else 1.0
                            bias = 0.0 if causal else bqk[name][:, 0:1]
                            act.activation(parts[name][:, 0, :], ps_misc[:], ACT.Identity, bias=bias, scale=scale)
                            act.activation(whole[name][:], ps_misc[:], ACT.Identity, bias=bias, scale=scale).then_inc(sems["misc_free"], 1)
                        if name == "ff1":
                            wait(act, sems["misc"], n.at("misc") + 1)
                            act.activation(hid[:, arg, :], ps_misc[:], ACT.Relu, bias=b_ff1[:, arg:arg + 1]).then_inc(sems["misc_free"], 1)
                        if name == "proj" and layer == 1:
                            wait(act, sems["misc"], n.at("misc") + 1)
                            wait(act, sems["x2"], n.at("x2"))
                            act.activation(s1_out[par][:].rearrange("p t d -> p (t d)"), ps_misc[:], ACT.Copy).then_inc(sems["misc_free"], 1)
                        if name == "count":
                            experts1["route_scalar"](act)
                        if name == "gate":
                            wait(act, sems["gate_in"], n.at("gate_in") + 1)
                            act.activation(e[:], z[:], ACT.Tanh).then_inc(sems["gate_tanh"], 1)
                        n.step(step)

            @block.vector
            def _(dve):
                n = Tally(adds)
                linked = [0]

                def link(op):
                    linked[0] += 1
                    op.then_inc(sems["dve"], 1)
                    wait_apart(dve, sems["dve"], n.at("dve") + linked[0], sems["apart"])

                def moments_of(src, width, count):
                    v = src[:].rearrange("p t d -> p (t d)")
                    for i in range(count):
                        op = dve.bn_stats(stats[:, i, :], v[:, i * width:(i + 1) * width])
                    link(op)
                    for i in range(count):
                        op = dve.bn_aggr(moments[:, i, :], stats[:, i, :])
                    op.then_inc(sems["moments"], 1)

                for b, odd, steps in batches(dve, n):
                    if is_iteration(b, -2):
                        experts0["route_vector"](dve)
                    if is_iteration(b, -1):
                        experts0["weigh_vector"](dve)
                    if is_iteration(b, 1):
                        experts0["tiles_vector"](dve)
                    if is_iteration(b, MIX1):
                        experts1["tiles_vector"](dve)
                    for step in steps:
                        name, d, arg, layer = step
                        causal, at = layer == 1, b + d - NB * layer
                        par = (odd + d) % 2
                        linked[0] = 0
                        if name == "max":
                            half, j, slot, qt = head(arg)
                            wait(dve, sems["max_in"], n.at("max_in") + 1)
                            dve.tensor_reduce(neg_max[:, qt, half, j * QT + slot:j * QT + slot + 1], ps_max[:, arg % 2, 0:keys(qt, causal)],
                                              AX.X, ALU.max, negate=True).then_inc(sems["max_out"], 1)
                        if name == "shift":
                            wait(dve, sems["misc"], n.at("misc") + 1)
                            wait(dve, sems["shift_in"], n.at("shift_in"))
                            link(dve.tensor_copy(shift[:, 0, :], ps_misc[0:NG, :]))
                            dve.tensor_tensor(shift[:, 1, :], ps_misc[0:NG, :], shift[:, 0, :], ALU.subtract).then_inc(sems["misc_free"], 1)
                        if name == "norm":
                            wait(dve, sems["misc"], n.at("misc") + 1)
                            v = ps_misc[:].rearrange("p (t c v) -> p t c v", t=QT, c=4)
                            link(dve.reciprocal(o_den[:], v[:, :, :, HD]))
                            o = o_norm[par][:, :, 4 * HD * arg:4 * HD * (arg + 1)].rearrange("p t (c v) -> p t c v", c=4)
                            dve.tensor_tensor(o, v[:, :, :, 0:HD], o_den[:].unsqueeze(3).broadcast_to([P, QT, 4, HD]),
                                              ALU.mult).then_inc(sems["misc_free"], 1)
                        if name == "v":
                            wait(dve, sems["misc"], n.at("misc") + 1)
                            wait(dve, sems["summed"], n.at("summed"))
                            dst = v_aug[par][:, :, :, 0:HD]
                            src = ps_misc[:].rearrange("p (t h v) -> p t h v", t=QT, h=H)
                            if layer == 0:
                                for t in range(QT):
                                    op = dve.tensor_tensor(dst[:, t], src[:, t], bv[:].rearrange("p (h v) -> p h v", h=H), ALU.add)
                            else:
                                op = dve.tensor_copy(dst, src)
                            op.then_inc(sems["misc_free"], 1)
                        if name == "z":
                            wait(dve, sems["misc"], n.at("misc") + 1)
                            dve.tensor_tensor(resid[par][:], ps_misc[:].rearrange("p (t d) -> p t d", t=QT),
                                              bo[:].unsqueeze(1).broadcast_to([P, QT, D]), ALU.add).then_inc(sems["misc_free"], 1)
                        if name == "proj" and layer == 0:
                            wait(dve, sems["misc"], n.at("misc") + 1)
                            dve.tensor_tensor(y0[:], ps_misc[:].rearrange("p (t d) -> p t d", t=QT), resid[par][:],
                                              ALU.add).then_inc(sems["misc_free"], 1)
                            wait(dve, sems["misc_free"], n.at("misc_free") + 1)
                            moments_of(y0, HALF, 2 * QT)
                        if name == "ln1":
                            wait(dve, sems["rstd"], n.at("rstd"))
                            halves = "p t (a d) -> p (t a) d"
                            link(dve.tensor_tensor(y1[:].rearrange(halves, a=2), y0[:].rearrange(halves, a=2),
                                                   moments[:, :, 0:1].broadcast_to([P, 2 * QT, HALF]), ALU.subtract))
                            dve.tensor_tensor(y2[:].rearrange(halves, a=2), y1[:].rearrange(halves, a=2),
                                              rstd[:].unsqueeze(2).broadcast_to([P, 2 * QT, HALF]), ALU.mult).then_inc(sems["centred"], 1)
                        if name == "ff2":
                            wait(dve, sems["misc"], n.at("misc") + 1)
                            wait(dve, sems["yb"], n.at("yb"))
                            dve.tensor_tensor(t0[:], ps_misc[:].rearrange("p (t d) -> p t d", t=QT), yb[:],
                                              ALU.add).then_inc(sems["misc_free"], 1)
                            wait(dve, sems["misc_free"], n.at("misc_free") + 1)
                            moments_of(t0, D, QT)
                        if name == "ln2":
                            wait(dve, sems["rstd"], n.at("rstd"))
                            for t in range(QT):
                                op = dve.tensor_scalar(t1[:, t, :], t0[:, t, :], moments[:, t, 0:1], rstd[:, t:t + 1], ALU.subtract, ALU.mult)
                            op.then_inc(sems["normed"], 1)
                        if name == "gather":
                            wait(dve, sems["rows"], n.at("rows"))
                            wait(dve, sems["gate_in"], n.at("gate_in"))
                            tiles_of = slice(QT * at, QT * (at + 1)) if isinstance(b, int) else bass.ds(at * QT, QT)
                            for i in range(len(gathered[layer])):
                                dve.tensor_copy(row_at[i][:], routes[layer]["at"][i][:, tiles_of])
                                op = dve.tensor_copy(row_w[i][:], routes[layer]["weight"][i][:, tiles_of])
                            op.then_inc(sems["picks"], 1)
                        if name == "choose":
                            wait(dve, sems["misc_free"], n.at("misc_free"))
                            experts1["choose_vector"](dve)
                        if name == "count":
                            wait(dve, sems["misc"], n.at("misc") + 1)
                            experts1["place_vector"](dve, sems["misc_free"], n.at("misc_free") + 1)
                        if name == "weigh":
                            experts1["weigh_vector"](dve)
                        if name == "mix":
                            wait(dve, sems["gate_tanh"], n.at("gate_tanh"))
                            dve.scalar_tensor_tensor(gz[:], e[:], 1.0, z[:], ALU.add, ALU.mult).then_inc(sems["gate_out"], 1)
                        if name == "ln3a":
                            wait(dve, sems["x2"], n.at("x2"))
                            moments_of(x2, D, QT)
                        if name == "ln3b":
                            wait(dve, sems["rstd"], n.at("rstd"))
                            wait(dve, sems["xn2_out"], n.at("xn2_out"))
                            for t in range(QT):
                                op = dve.tensor_scalar(xn2[:, t, :], x2[:, t, :], moments[:, t, 0:1], rstd[:, t:t + 1], ALU.subtract, ALU.mult)
                            op.then_inc(sems["xn2"], 1)
                        if name == "logits":
                            wait(dve, sems["misc"], n.at("misc") + 1)
                            tiles_of = slice(QT * at, QT * (at + 1)) if isinstance(b, int) else bass.ds(at * QT, QT)
                            dve.tensor_tensor(routes[1]["logits"][:, tiles_of, :], ps_misc[:, 0:QT * E1].rearrange("p (t e) -> p t e", t=QT),
                                              bg[:].unsqueeze(1).broadcast_to([P, QT, E1]), ALU.add).then_inc(sems["misc_free"], 1)
                        assert linked[0] == n.adds(step).get("dve", 0), (step, linked[0])
                        n.step(step)

            @block.gpsimd
            def _(pool):
                n = Tally(adds)
                linked = [0]

                def link(op):
                    linked[0] += 1
                    op.then_inc(sems["pool"], 1)
                    wait_apart(pool, sems["pool"], n.at("pool") + linked[0], sems["apart"])

                def inverse_deviation(count):
                    wait_apart(pool, sems["moments"], n.at("moments") + 1, sems["apart"])
                    link(pool.tensor_scalar(veps[:, 0:count], moments[:, 0:count, 1], EPS, None, ALU.add))
                    pool.tensor_tensor(rstd[:, 0:count], veps[:, 0:count], const["minus_half"][:, 0:count], ALU.pow).then_inc(sems["rstd"], 1)

                def bcast(t):
                    return t[:].unsqueeze(1).broadcast_to([P, QT, D])

                for b, odd, steps in batches(pool, n):
                    if any(is_iteration(b, k) for k in (-1, 0, 1)):
                        experts0["send_pool"](pool, b + 1)
                    if is_iteration(b, MIX1):
                        experts1["done_pool"](pool)
                    for step in steps:
                        name, d, arg, layer = step
                        par = (odd + d) % 2
                        linked[0] = 0
                        if name in ("q", "k"):
                            wait(pool, sems["split"], n.at("split"))
                            wait(pool, sems["misc_free"], n.at("misc_free") + 1)
                            a, full, r = parts[name], whole[name], rest
                            link(pool.tensor_tensor(r[:], full[:], a[:, 0, :], ALU.subtract))
                            link(pool.tensor_copy(a[:, 1, :], r[:]))
                            pool.tensor_tensor(a[:, 2, :], r[:], a[:, 1, :], ALU.subtract).then_inc(sems["split"], 1)
                        if name in LN_TILES and layer == 0:
                            inverse_deviation(LN_TILES[name])
                        if name == "ln1":
                            wait(pool, sems["centred"], n.at("centred") + 1)
                            link(pool.tensor_tensor(y3[:], y2[:], bcast(g12), ALU.mult))
                            pool.tensor_tensor(y[:], y3[:], bcast(be12), ALU.add).then_inc(sems["y"], 1)
                            wait(pool, sems["y"], n.at("y") + 1)
                            pool.tensor_tensor(yb[:], y[:], bcast(b_ff2), ALU.add).then_inc(sems["yb"], 1)
                        if name == "ln2":
                            wait(pool, sems["normed"], n.at("normed") + 1)
                            link(pool.tensor_tensor(t2[:], t1[:], bcast(g_ff), ALU.mult))
                            pool.tensor_tensor(s0_out[:], t2[:], bcast(be_ff), ALU.add).then_inc(sems["s"], 1)
                        if name == "gather":
                            wait_apart(pool, sems["picks"], n.at("picks") + 1, sems["apart"])
                            for i, rows in enumerate(gathered[layer]):
                                for t in range(QT):
                                    pool.indirect_dma_start(rows[:, t, :], None, moe[layer],
                                                            bass.IndirectOffsetOnAxis(ap=row_at[i][:, t:t + 1], axis=0)
                                                            ).then_inc(sems["rows"], 16)
                        if name == "gate":
                            wait(pool, sems["rows"], n.at("rows"))
                            rows = gathered[layer]
                            per = lambda i: row_w[i][:].unsqueeze(2).broadcast_to([P, QT, D])
                            if layer == 0:
                                pool.tensor_tensor(z[:], rows[0][:], per(0), ALU.mult).then_inc(sems["gate_in"], 1)
                            else:
                                pool.tensor_tensor(z_both[0][:], rows[0][:], per(0), ALU.mult)
                                link(pool.tensor_tensor(z_both[1][:], rows[1][:], per(1), ALU.mult))
                                pool.tensor_tensor(z[:], z_both[0][:], z_both[1][:], ALU.add).then_inc(sems["gate_in"], 1)
                        if name == "send":
                            experts1["send_pool"](pool, arg)
                        if name == "mix":
                            wait(pool, sems["gate_out"], n.at("gate_out") + 1)
                            wait(pool, sems["x_in"], n.at("x_in"))
                            wait(pool, sems["x2_out"], n.at("x2_out"))
                            if layer == 0:
                                wait(pool, sems["s"], n.at("s"))
                            else:
                                wait(pool, sems["misc_free"], n.at("misc_free"))
                            link(pool.tensor_tensor(sg[:], gz[:], (s0_out if layer == 0 else s1_out[par])[:], ALU.mult))
                            pool.tensor_tensor(x2[:], sg[:], x_in[:], ALU.add).then_inc(sems["x2"], 1)
                        assert linked[0] == n.adds(step).get("pool", 0), (step, linked[0])
                        n.step(step)


def first_best(dve, link, logits, experts, number, best, flag, first, onehot):
    def per(t):
        return t[:].unsqueeze(2).broadcast_to([P, NT, experts])
    numbers = number.unsqueeze(1).broadcast_to([P, NT, experts])
    link(dve.tensor_reduce(best[:], logits, AX.X, ALU.max))
    link(dve.tensor_tensor(flag[:], logits, per(best), ALU.is_ge))
    link(dve.tensor_tensor(flag[:], flag[:], numbers, ALU.mult))
    link(dve.tensor_reduce(first[:], flag[:], AX.X, ALU.min))
    link(dve.tensor_tensor(onehot[:], numbers, per(first), ALU.is_equal))


def places(dve, link, read, before, totals, run, pos):
    link(dve.tensor_copy(run[0][:], totals))
    a, b, k = 0, 1, 1
    while k < NT:
        dve.tensor_copy(run[b][:, 0:k, :], run[a][:, 0:k, :])
        link(dve.tensor_tensor(run[b][:, k:NT, :], run[a][:, k:NT, :], run[a][:, 0:NT - k, :], ALU.add))
        a, b, k = b, a, 2 * k
    link(dve.tensor_tensor(pos[:], run[a][:], totals, ALU.subtract))
    read(dve.tensor_tensor(pos[:], pos[:], before, ALU.add))
    return run[a]


def pipelined(eng, count, lead):
    first = 5
    trips = (count - lead - first) // 4
    for k in range(first):
        yield k, k % 4, k
    with eng.Fori(0, trips) as trip:
        for u in range(4):
            yield trip * 4 + first + u, (first + u) % 4, None
    for k in range(first + 4 * trips, count + 1):
        yield k, k % 4, k


def uses(k, par, adds):
    return (k - par) * (adds // 4)


def zero_dmas(w, rows):
    return rows * D // (w["zeros"].shape[0] * w["zeros"].shape[1])


def zero_fill(sp, w, dst, rows, sem):
    n = zero_dmas(w, rows)
    v = dst[0:rows, :].rearrange("(n r) d -> n (r d)", n=n)
    for k in range(n):
        sp.dma_start(v[k], w["zeros"].rearrange("a b -> (a b)")).then_inc(sem, 16)


def normalise0(nc, const, psum, strips, dram, w, tokens, logits, weights, loads):
    with ExitStack() as ctx:
        def sb(name, shape, dt=F32):
            return ctx.enter_context(nc.sbuf_tensor(f"n0_{name}", shape, dt))

        names = ("consts", "const", "moments", "rstd", "xn", "xn_out", "xT", "xnT", "scored", "zeroed0",
                 *(f"x_in{i}" for i in range(4)), "row_fill", "rows_out", "strips", "weights", "positions", "dve", "pool")
        sems = {k: ctx.enter_context(nc.semaphore(f"n0_{k}")) for k in names}
        ps_scores, ps_max = psum[0:2]
        rows_of = {"q": sb("zeros", [P, S], BF16), "k": sb("ones", [P, S], BF16)}
        x_all, xn_all = sb("x_all", [P, NT, D]), tokens
        xn_T = [sb(f"xn_T{i}", [P, S]) for i in range(2)]
        stats, moments = sb("stats", [P, NT, 6]), sb("moments", [P, NT, 2])
        veps, rstd = sb("veps", [P, NT]), sb("rstd", [P, NT])
        wg = sb("wg", [P, E0])
        pos, pos_rest, pos_parts = sb("pos", [H, S]), sb("pos_rest", [H, S]), sb("pos_parts", [H, 3, S], BF16)
        LOADS = 4
        PER = NT // LOADS
        x_src = dram["x"].rearrange("(t p) d -> p t d", p=P)
        xn_dst = dram["xn"].rearrange("(t p) d -> p t d", p=P)
        filled0 = 16 * zero_dmas(w, E0 * CAP)

        with nc.Block() as block:

            @block.sync
            def _(sp):
                for i in range(LOADS):
                    sp.dma_start(x_all[:, i * PER:(i + 1) * PER, :], x_src[:, i * PER:(i + 1) * PER, :]).then_inc(sems[f"x_in{i}"], 16)
                    if i == 0:
                        sp.dma_start(const["all"][:], w["consts"]).then_inc(sems["consts"], 16)
                        sp.dma_start(wg[:], w["gate_w0"]).then_inc(sems["consts"], 16)
                for dst, src in loads + [(pos, w["alibi"])]:
                    sp.dma_start(dst[:], src).then_inc(sems["weights"], 16)
                sp.wait_ge(sems["row_fill"], 2)
                for k in "qk":
                    sp.dma_start(dram[k][:, ROW_SHIFT:ROW_ALIBI], rows_of[k][0:2 * H, :]).then_inc(sems["rows_out"], 16)
                for i in range(2):
                    for j in range(2):
                        sp.dma_start(strips["q"][i][STRIP * j + ROW_ALIBI:STRIP * (j + 1), :, :],
                                     rows_of["k"][0:(STRIP - ROW_ALIBI) * NG, :]).then_inc(sems["rows_out"], 16)
                zero_fill(sp, w, dram["sent0"], E0 * CAP, sems["zeroed0"])
                sp.wait_ge(sems["xn"], LOADS)
                sp.dma_start(xn_dst, xn_all[:]).then_inc(sems["xn_out"], 16)
                sp.wait_ge(sems["xn_out"], 16)
                sp.wait_ge(sems["zeroed0"], filled0)
                sp.wait_ge(sems["positions"], 1)
                sp.dma_start(dram["k"][:, ROW_ALIBI:ROW_END], pos_parts[:]).then_inc(sems["rows_out"], 16)
                sp.wait_ge(sems["rows_out"], 16 * 7)

            @block.tensor
            def _(pe):
                pe.wait_ge(sems["consts"], 32)
                for b in range(NB):
                    pe.wait_ge(sems["xn"], b * QT // PER + 1)
                    if b >= 2:
                        pe.wait_ge(sems["xnT"], b - 1)
                    for t in range(QT):
                        mm = pe.transpose(ps_max[:, b % 2, t * P:(t + 1) * P], xn_all[:, b * QT + t, :], const["ident"])
                    mm.then_inc(sems["xT"], 1)
                    for last in ([b - 1] if b else []) + ([b] if b == NB - 1 else []):
                        pe.wait_ge(sems["xnT"], last + 1)
                        for t in range(QT):
                            at = (last * QT + t) * E0
                            mm = pe.matmul(ps_scores[:, 0, at:at + E0], xn_T[last % 2][:, t * P:(t + 1) * P], wg[:], start=True, stop=True)
                        mm.then_inc(sems["scored"], 1)

            @block.scalar
            def _(act):
                for b in range(NB):
                    act.wait_ge(sems["xT"], b + 1)
                    if b >= 2:
                        act.wait_ge(sems["scored"], b - 1)
                    act.activation(xn_T[b % 2][:], ps_max[:, b % 2, :], ACT.Copy).then_inc(sems["xnT"], 1)

            @block.vector
            def _(dve):
                linked = [0]

                def link(op):
                    linked[0] += 1
                    op.then_inc(sems["dve"], 1)
                    dve.wait_ge(sems["dve"], linked[0])

                link(dve.memset(const["ones"][:], 1.0))
                dve.memset(const["minus_half"][:], -0.5).then_inc(sems["const"], 1)
                for i in range(LOADS):
                    at = slice(i * PER, (i + 1) * PER)
                    dve.wait_ge(sems[f"x_in{i}"], 16)
                    for t in range(i * PER, (i + 1) * PER):
                        op = dve.bn_stats(stats[:, t, :], x_all[:, t, :])
                    link(op)
                    for t in range(i * PER, (i + 1) * PER):
                        op = dve.bn_aggr(moments[:, t, :], stats[:, t, :])
                    op.then_inc(sems["moments"], 1)
                    for last in ([i - 1] if i else []) + ([i] if i == LOADS - 1 else []):
                        dve.wait_ge(sems["rstd"], last + 1)
                        for t in range(last * PER, (last + 1) * PER):
                            op = dve.tensor_scalar(xn_all[:, t, :], x_all[:, t, :], moments[:, t, 0:1], rstd[:, t:t + 1], ALU.subtract, ALU.mult)
                        op.then_inc(sems["xn"], 1)
                dve.wait_ge(sems["consts"], 32)
                for k, at in (("ident_bf", C_IDENT), ("before", C_BEFORE), ("mask_qk", C_MASK_QK), ("mask_kq", C_MASK_KQ)):
                    op = dve.tensor_copy(const[k][:], const["all"][:, at:at + P])
                op.then_inc(sems["const"], 1)
                dve.memset(strips["k"][1][:], 0.0)
                dve.wait_ge(sems["weights"], 16 * (len(loads) + 1))
                dve.tensor_scalar(weights["bqs"][:], weights["bq"][:], SCALE, None, ALU.mult)
                link(dve.tensor_copy(pos_parts[:, 0, :], pos[:]))
                link(dve.tensor_tensor(pos_rest[:], pos[:], pos_parts[:, 0, :], ALU.subtract))
                link(dve.tensor_copy(pos_parts[:, 1, :], pos_rest[:]))
                dve.tensor_tensor(pos_parts[:, 2, :], pos_rest[:], pos_parts[:, 1, :], ALU.subtract).then_inc(sems["positions"], 1)
                dve.wait_ge(sems["scored"], NB)
                dve.tensor_copy(logits, ps_scores[:, 0, :].rearrange("p (t e) -> p t e", t=NT))
                dve.wait_ge(sems["strips"], 2)
                for i in range(2):
                    dve.memset(strips["v"][i][:, :, :, HD:HD + 1], 1.0)

            @block.gpsimd
            def _(pool):
                pool.memset(rows_of["q"][:], 0.0).then_inc(sems["row_fill"], 1)
                pool.memset(rows_of["k"][:], 1.0).then_inc(sems["row_fill"], 1)
                pool.wait_ge(sems["const"], 1)
                half = const["minus_half"]
                for i in range(LOADS):
                    at = slice(i * PER, (i + 1) * PER)
                    pool.wait_ge(sems["moments"], i + 1)
                    pool.tensor_scalar(veps[:, at], moments[:, at, 1], EPS, None, ALU.add).then_inc(sems["pool"], 1)
                    pool.wait_ge(sems["pool"], i + 1)
                    pool.tensor_tensor(rstd[:, at], veps[:, at], half[:, 0:PER], ALU.pow).then_inc(sems["rstd"], 1)
                for i in range(2):
                    pool.memset(strips["v"][i][:], 0.0).then_inc(sems["strips"], 1)
                pool.memset(strips["k"][0][:], 0.0)


SEND = ((0, 12), (12, 22), (22, NT))


def made_of(work):
    return work[:, WORK - 4 * CAP * D // P:WORK]


def experts0(nc, ctx, xn_all, work, scratch, logits, send_at, const, psum, dram, w, route):
    def sb(name, shape, dt=F32):
        return ctx.enter_context(nc.sbuf_tensor(f"m0_{name}", shape, dt))

    names = ("zeroed1", "chosen", "counted", "shifted", "exped", "slots", "sent",
             *(f"{k}{i}" for k in ("w_in", "rows_in", "stored") for i in range(4)), "weighed",
             "rowsT", "rowsT_out", "hidden", "hidden_act", "hidden_dve", "made", "made_out", "dve")
    sems = {k: ctx.enter_context(nc.semaphore(f"m0_{k}")) for k in names}
    ps_scores, ps_max, ps_sum, ps_misc = psum
    made_bank = (ps_max[:, 1, :], ps_misc[:])
    shifted, exped, flag, onehot, pos, *run = (
        scratch[i][:, c, :].rearrange("p (t e) -> p t e", t=NT) for i in range(2) for c in range(4) if i + c < 4)
    onehot_bf = const["onehot_bf"][:].rearrange("p (t e) -> p t e", e=E0)
    CT = CAP // P
    take = columns(work)
    w1 = [take(F0) for i in range(4)]
    w2 = [take(FC0 * D).rearrange("p (c d) -> p c d", c=FC0) for i in range(4)]
    rows = [take(CT * D).rearrange("p (t d) -> p t d", t=CT) for i in range(4)]
    rows_T = [take(CAP) for i in range(4)]
    hid = [take(FC0 * CAP).rearrange("p (c n) -> p c n", c=FC0) for i in range(2)]
    made = [take(CT * D).rearrange("p (t d) -> p t d", t=CT) for i in range(4)]
    take = columns(made_of(work))
    best, first, loc, start, valid, slot, send = (take(NT) for _ in range(7))
    rows_src = dram["sent0"][0:E0 * CAP, :].rearrange("(e t p) d -> e p t d", e=E0, p=P)
    made_dst = dram["made0"].rearrange("(e t p) d -> e p t d", e=E0, p=P)

    def one(ap, e):
        return ap[e] if isinstance(e, int) else ap[bass.ds(e, 1)].rearrange("o p t d -> (o p) t d")

    def one2(ap, e):
        return ap[e] if isinstance(e, int) else ap[bass.ds(e, 1)].rearrange("o p f -> (o p) f")

    def tiles_sync(sp):
        def weights(e, par):
            sp.dma_start(w1[par][:], one2(w["w1_0"], e)).then_inc(sems[f"w_in{par}"], 16)
            sp.dma_start(w2[par][:], one(w["w2_0"].rearrange("e (c p) d -> e p c d", p=P), e)).then_inc(sems[f"w_in{par}"], 16)

        def tokens(e, par):
            sp.dma_start(rows[par][:], one(rows_src, e)).then_inc(sems[f"rows_in{par}"], 16)

        def store(e, par):
            sp.wait_ge(sems["made_out"], e + 1)
            sp.dma_start(one(made_dst, e), made[par][:]).then_inc(sems[f"stored{par}"], 16)

        for e in range(4):
            weights(e, e)
        sp.wait_ge(sems["sent"], 16 * NT)
        for e in range(6):
            if e >= 4:
                sp.wait_ge(sems["rowsT"], e - 3)
            tokens(e, e % 4)
        with sp.Fori(0, E0 // 4 - 2) as i:
            for par in range(4):
                e = i * 4 + par
                store(e, par)
                weights(e + 4, par)
                tokens(e + 6, (par + 2) % 4)
        for e in range(E0 - 8, E0):
            store(e, e % 4)
            if e + 4 < E0:
                weights(e + 4, e % 4)
            if e + 6 < E0:
                tokens(e + 6, (e + 2) % 4)
        zero_fill(sp, w, dram["sent1"], TILES1 * SLOTS1, sems["zeroed1"])

    def route_tensor(pe):
        pe.wait_ge(sems["chosen"], 1)
        v = onehot_bf[:].rearrange("p t e -> p (t e)")
        pe.matmul(ps_max[:, 0, :], const["before"][:], v, start=True, stop=True)
        pe.matmul(ps_max[:, 1, :], const["ones"][:], v, start=True, stop=True).then_inc(sems["counted"], 1)

    def tiles_tensor(pe):
        def rows_transposed(e, par, fixed):
            pe.wait_ge(sems[f"rows_in{par}"], uses(e, par, 16) + 16)
            if fixed is None or fixed >= 1:
                pe.wait_ge(sems["rowsT_out"], e)
            for t in range(CT):
                mm = pe.transpose(ps_max[:, 0, t * P:(t + 1) * P], rows[par][:, t, :], const["ident"])
            mm.then_inc(sems["rowsT"], 1)

        for e in range(2):
            rows_transposed(e, e, e)
        for k, par, fixed in pipelined(pe, E0, 2):
            if fixed is None or fixed < E0:
                pe.wait_ge(sems[f"w_in{par}"], uses(k, par, 32) + 32)
                pe.wait_ge(sems["rowsT_out"], k + 1)
                for c in range(FC0):
                    bank, at = 2 * (par % 2) + c // 2, CAP * (c % 2)
                    mm = pe.matmul(ps_scores[:, bank, at:at + CAP], w1[par][:, c * P:(c + 1) * P], rows_T[par][:], start=True, stop=True)
                    if c % 2 == 1:
                        mm.then_inc(sems["hidden"], 1)
            if fixed is None or fixed < E0 - 2:
                rows_transposed(k + 2, (par + 2) % 4, None if fixed is None else fixed + 2)
            if fixed != 0:
                pe.wait_ge(sems["hidden_act"], k)
                pe.wait_ge(sems["hidden_dve"], k)
                if fixed is None or fixed > 2:
                    pe.wait_ge(sems["made_out"], k - 2)
                last = (par + 3) % 4
                for t in range(CT):
                    for c in range(FC0):
                        mm = pe.matmul(made_bank[last % 2][:, t * D:(t + 1) * D], hid[last % 2][:, c, t * P:(t + 1) * P],
                                       w2[last][:, c, :], start=c == 0, stop=c == FC0 - 1)
                mm.then_inc(sems["made"], 1)
        pe.wait_ge(sems["made_out"], E0)

    def route_scalar(act):
        act.wait_ge(sems["shifted"], 1)
        act.activation(exped[:], shifted[:], ACT.Exp).then_inc(sems["exped"], 1)

    def tiles_scalar(act):
        def rows_out(e, par):
            act.wait_ge(sems["rowsT"], e + 1)
            act.activation(rows_T[par][:], ps_max[:, 0, 0:CAP], ACT.Copy).then_inc(sems["rowsT_out"], 1)

        for e in range(2):
            rows_out(e, e)
        for k, par, fixed in pipelined(act, E0, 2):
            if fixed is None or fixed < E0:
                act.wait_ge(sems["hidden"], k * 2 + 1)
                if fixed is None or fixed > 1:
                    act.wait_ge(sems["made"], k - 1)
                act.activation(hid[par % 2][:, 0:2, :], ps_scores[:, 2 * (par % 2), :].rearrange("p (c n) -> p c n", c=2),
                               ACT.Relu).then_inc(sems["hidden_act"], 1)
            if fixed is None or fixed < E0 - 2:
                rows_out(k + 2, (par + 2) % 4)

    def route_vector(dve):
        linked = [0]

        def link(op):
            linked[0] += 1
            op.then_inc(sems["dve"], 1)
            dve.wait_ge(sems["dve"], linked[0])

        number = const["all"][:, C_EXP0:C_EXP0 + E0]
        first_best(dve, link, logits, E0, number, best, flag, first, onehot)
        dve.tensor_copy(onehot_bf[:], onehot[:]).then_inc(sems["chosen"], 1)
        dve.tensor_tensor(shifted[:], logits, best[:].unsqueeze(2).broadcast_to([P, NT, E0]), ALU.subtract).then_inc(sems["shifted"], 1)
        dve.wait_ge(sems["counted"], 1)
        by = "p (t e) -> p t e"
        places(dve, link, link, ps_max[:, 0, :].rearrange(by, e=E0), ps_max[:, 1, :].rearrange(by, e=E0), run, pos)
        link(dve.tensor_tensor(pos[:], pos[:], onehot[:], ALU.mult))
        link(dve.tensor_reduce(loc[:], pos[:], AX.X, ALU.add))
        link(dve.tensor_scalar(start[:], first[:], float(E0), float(CAP), ALU.add, ALU.mult))
        link(dve.tensor_scalar(valid[:], loc[:], float(CAP), None, ALU.is_lt))
        link(dve.tensor_tensor(slot[:], start[:], loc[:], ALU.add))
        dump = const["all"][:, C_DUMP:C_DUMP + NT]
        link(dve.tensor_tensor(send[:], slot[:], dump, ALU.subtract))
        link(dve.tensor_tensor(send[:], send[:], valid[:], ALU.mult))
        link(dve.tensor_tensor(send[:], send[:], dump, ALU.add))
        dve.tensor_copy(send_at[:], send[:]).then_inc(sems["slots"], 1)
        link(dve.tensor_scalar(loc[:], loc[:], float(CAP - 1), None, ALU.min))
        link(dve.tensor_tensor(slot[:], start[:], loc[:], ALU.add))
        dve.tensor_copy(route["at"][0][:], slot[:])

    def weigh_vector(dve):
        dve.wait_ge(sems["exped"], 1)
        dve.tensor_reduce(best[:], exped[:], AX.X, ALU.add).then_inc(sems["weighed"], 1)
        dve.wait_ge(sems["weighed"], 1)
        dve.reciprocal(first[:], best[:]).then_inc(sems["weighed"], 1)
        dve.wait_ge(sems["weighed"], 2)
        dve.scalar_tensor_tensor(route["weight"][0][:], first[:], 0.5, valid[:], ALU.mult, ALU.mult).then_inc(sems["weighed"], 1)

    def tiles_vector(dve):
        for k, par, fixed in pipelined(dve, E0, 2):
            if fixed is None or fixed < E0:
                dve.wait_ge(sems["hidden"], k * 2 + 2)
                dve.tensor_scalar(hid[par % 2][:, 2:4, :], ps_scores[:, 2 * (par % 2) + 1, :].rearrange("p (c n) -> p c n", c=2), 0.0, None,
                                  ALU.max).then_inc(sems["hidden_dve"], 1)
            if fixed != 0:
                dve.wait_ge(sems["made"], k)
                last = (par + 3) % 4
                if fixed is None or fixed > 4:
                    dve.wait_ge(sems[f"stored{last}"], uses(k - 1, last, 16))
                dve.tensor_copy(made[last][:], made_bank[last % 2][:, 0:CT * D].rearrange("p (t d) -> p t d", t=CT)
                                ).then_inc(sems["made_out"], 1)

    def send_pool(pool, part):
        if part == 0:
            pool.wait_ge(sems["slots"], 1)
        for t in range(*SEND[part]):
            pool.indirect_dma_start(dram["sent0"], bass.IndirectOffsetOnAxis(ap=send_at[:, t:t + 1], axis=0),
                                    xn_all[:, t, :], None).then_inc(sems["sent"], 16)
        if part == len(SEND) - 1:
            pool.wait_ge(sems["sent"], 16 * NT)
            for i in range(4):
                pool.wait_ge(sems[f"stored{i}"], 16 * (E0 // 4))
            pool.wait_ge(sems["zeroed1"], 16 * zero_dmas(w, TILES1 * SLOTS1))

    parts = (tiles_sync, route_tensor, tiles_tensor, route_scalar, tiles_scalar, route_vector, weigh_vector,
             tiles_vector, send_pool)
    return sems, {f.__name__: f for f in parts}


def experts1(nc, ctx, xn_all, work, const, psum, dram, w, route):
    def sb(name, shape, dt=F32):
        return ctx.enter_context(nc.sbuf_tensor(f"m1_{name}", shape, dt))

    names = ("chosen", "gap", "gap_exp", "slots", "tiles", "all_in", "sent",
             *(f"{k}{i}" for k in ("pack_in", "rows_in", "stored") for i in range(4)),
             "rowsT", "rowsT_out", "hidden0", "hidden1", "silu", "hidden_out", "made", "made_out", "dve", "weighed")
    sems = {k: ctx.enter_context(nc.semaphore(f"m1_{k}")) for k in names}
    ps_scores, ps_max, ps_sum, ps_misc = psum
    logits, weight, at = route["logits"], route["weight"], route["at"]
    onehot_bf = const["onehot_bf"][:, 0:NT * E1].rearrange("p (t e) -> p t e", e=E1)
    tile_expert = sb("tile_expert", [1, TILES1], I32)
    by_expert, by_slot = "p (t e) -> p t e", "p (c n) -> p c n"
    take = columns(work)
    pack = [take(PACK1) for i in range(4)]
    take_early = columns(work[:, 4 * PACK1:WORK])
    rows = [take(CT1 * D).rearrange("p (t d) -> p t d", t=CT1) for i in range(4)]
    rows_T = [take(SLOTS1) for i in range(4)]
    silu = [take(FC1 * SLOTS1).rearrange(by_slot, c=FC1) for i in range(2)]
    hid = [take(FC1 * SLOTS1).rearrange(by_slot, c=FC1) for i in range(2)]
    made = [take(CT1 * D).rearrange("p (t d) -> p t d", t=CT1) for i in range(4)]
    gap, gap_exp, divisor = (take(NT) for _ in range(3))
    rest, flag, pos, *run = (take_early(NT * E1).rearrange(by_expert, e=E1) for _ in range(5))
    onehot = [take_early(NT * E1).rearrange(by_expert, e=E1) for i in range(TOP + 1)]
    best, first, slot = [take_early(NT) for i in range(2)], take_early(NT), take_early(NT)
    filled = take_early(E1 * FILLS).rearrange("p (e n) -> p e n", e=E1)
    used, *ends = (take_early(E1) for _ in range(3))
    past, tile_e = take_early(TILES1 * E1)[0:1].rearrange(by_expert, e=E1), take_early(TILES1)[0:1]
    W2_AT, B_AT, B2_AT = 2 * F1, 2 * F1 + FC1 * D, 2 * F1 + FC1 * D + 2 * FC1
    sent = dram["sent1"].rearrange("(n t p) d -> n p t d", t=CT1, p=P)
    made_dst = dram["made1"].rearrange("(n t p) d -> n p t d", t=CT1, p=P)

    def one(ap, k):
        return ap[k] if isinstance(k, int) else ap[bass.ds(k, 1)].rearrange("o p t d -> (o p) t d")

    def one2(ap, k):
        return ap[bass.ds(k, 1)].rearrange("o p f -> (o p) f")
    made_bank = (ps_max[:, 1, :], ps_misc[:])

    def hidden_bank(par, i):
        return ps_scores[:, 2 * (par % 2) + i, :].rearrange("p (c n) -> p c n", c=FC1)

    def route_sync(sp):
        sp.dma_start(xn_all[:], dram["xn2"].rearrange("(t p) d -> p t d", p=P)).then_inc(sems["all_in"], 16)

    def tiles_sync(sp):
        sp.wait_ge(sems["tiles"], 1)

        def weights(k, par):
            e = sp.value_load(tile_expert[0:1, k:k + 1] if isinstance(k, int) else tile_expert[0:1, bass.ds(k, 1)],
                              min_val=0, max_val=E1 - 1)
            sp.dma_start(pack[par][:], one2(w["pack1"], e)).then_inc(sems[f"pack_in{par}"], 16)

        def tokens(k, par):
            sp.dma_start(rows[par][:], one(sent, k)).then_inc(sems[f"rows_in{par}"], 16)

        def store(k, par):
            sp.wait_ge(sems["made_out"], k + 1)
            sp.dma_start(one(made_dst, k), made[par][:]).then_inc(sems[f"stored{par}"], 16)

        for k in range(4):
            weights(k, k)
        sp.wait_ge(sems["sent"], 16 * NT * TOP)
        for k in range(6):
            if k >= 4:
                sp.wait_ge(sems["rowsT"], k - 3)
            tokens(k, k % 4)
        with sp.Fori(0, TILES1 // 4 - 2) as i:
            for par in range(4):
                k = i * 4 + par
                store(k, par)
                weights(k + 4, par)
                tokens(k + 6, (par + 2) % 4)
        for k in range(TILES1 - 8, TILES1):
            store(k, k % 4)
            if k + 4 < TILES1:
                weights(k + 4, k % 4)
            if k + 6 < TILES1:
                tokens(k + 6, (k + 2) % 4)

    def route_tensor(pe):
        pe.wait_ge(sems["chosen"], 1)
        v = const["onehot_bf"][:, 0:NT * E1]
        pe.matmul(ps_misc[:, 0:NT * E1], const["before"][:], v, start=True, stop=True)
        return pe.matmul(ps_misc[:, NT * E1:2 * NT * E1], const["ones"][:], v, start=True, stop=True)

    def tiles_tensor(pe):
        def rows_transposed(k, par, fixed):
            pe.wait_ge(sems[f"rows_in{par}"], uses(k, par, 16) + 16)
            if fixed is None or fixed >= 1:
                pe.wait_ge(sems["rowsT_out"], k)
            for t in range(CT1):
                mm = pe.transpose(ps_max[:, 0, t * P:(t + 1) * P], rows[par][:, t, :], const["ident"])
            mm.then_inc(sems["rowsT"], 1)

        for k in range(2):
            rows_transposed(k, k, k)
        for k, par, fixed in pipelined(pe, TILES1, 2):
            if fixed is None or fixed < TILES1:
                pe.wait_ge(sems[f"pack_in{par}"], uses(k, par, 16) + 16)
                pe.wait_ge(sems["rowsT_out"], k + 1)
                for i in reversed(range(2)):
                    for c in range(FC1):
                        mm = pe.matmul(hidden_bank(par, i)[:, c, :], pack[par][:, (i * FC1 + c) * P:(i * FC1 + c + 1) * P], rows_T[par][:],
                                       start=True, stop=True)
                    mm.then_inc(sems[f"hidden{i}"], 1)
            if fixed is None or fixed < TILES1 - 2:
                rows_transposed(k + 2, (par + 2) % 4, None if fixed is None else fixed + 2)
            if fixed != 0:
                last = (par + 3) % 4
                pe.wait_ge(sems["hidden_out"], k)
                if fixed is None or fixed > 2:
                    pe.wait_ge(sems["made_out"], k - 2)
                for t in range(CT1):
                    for c in range(FC1):
                        mm = pe.matmul(made_bank[last % 2][:, t * D:(t + 1) * D], hid[last % 2][:, c, t * P:(t + 1) * P],
                                       pack[last][:, W2_AT + c * D:W2_AT + (c + 1) * D], start=c == 0, stop=c == FC1 - 1)
                mm.then_inc(sems["made"], 1)
        pe.wait_ge(sems["made_out"], TILES1)

    def route_scalar(act):
        act.wait_ge(sems["gap"], 1)
        act.activation(gap_exp[:], gap[:], ACT.Exp).then_inc(sems["gap_exp"], 1)

    def tiles_scalar(act):
        def rows_out(k, par):
            act.wait_ge(sems["rowsT"], k + 1)
            act.activation(rows_T[par][:], ps_max[:, 0, 0:SLOTS1], ACT.Copy).then_inc(sems["rowsT_out"], 1)

        for k in range(2):
            rows_out(k, k)
        for k, par, fixed in pipelined(act, TILES1, 2):
            if fixed == TILES1:
                continue
            act.wait_ge(sems["hidden1"], k + 1)
            if fixed is None or fixed > 1:
                act.wait_ge(sems["hidden_out"], k - 1)
            for c in range(FC1):
                op = act.activation(silu[par % 2][:, c, :], hidden_bank(par, 1)[:, c, :], ACT.Silu,
                                    bias=pack[par][:, B_AT + FC1 + c:B_AT + FC1 + c + 1])
            op.then_inc(sems["silu"], 1)
            if fixed is None or fixed < TILES1 - 2:
                rows_out(k + 2, (par + 2) % 4)

    linked = [0]

    def linking(dve):
        def link(op):
            linked[0] += 1
            op.then_inc(sems["dve"], 1)
            dve.wait_ge(sems["dve"], linked[0])
        return link

    def choose_vector(dve):
        link = linking(dve)
        number = const["all"][:, C_EXP1:C_EXP1 + E1]
        first_best(dve, link, logits[:], E1, number, best[0], flag, first, onehot[0])
        link(dve.scalar_tensor_tensor(rest[:], onehot[0][:], MASK, logits[:], ALU.mult, ALU.add))
        first_best(dve, link, rest[:], E1, number, best[1], flag, first, onehot[1])
        link(dve.tensor_tensor(onehot[2][:], onehot[0][:], onehot[1][:], ALU.add))
        dve.tensor_copy(onehot_bf[:], onehot[2][:]).then_inc(sems["chosen"], 1)
        dve.tensor_tensor(gap[:], best[1][:], best[0][:], ALU.subtract).then_inc(sems["gap"], 1)

    def place_vector(dve, read, value):
        link = linking(dve)

        def last_read(op):
            op.then_inc(read, 1)
            dve.wait_ge(read, value)

        before, totals = (ps_misc[:, i * NT * E1:(i + 1) * NT * E1].rearrange(by_expert, e=E1) for i in range(2))
        total = places(dve, link, last_read, before, totals, run, pos)
        link(dve.tensor_tensor(filled[:], total[:, NT - 1, :].unsqueeze(2).broadcast_to([P, E1, FILLS]),
                               const["all"][:, C_FILL:C_FILL + FILLS].unsqueeze(1).broadcast_to([P, E1, FILLS]), ALU.is_gt))
        link(dve.tensor_reduce(used[:], filled[:], AX.X, ALU.add))
        link(dve.tensor_copy(ends[0][:], used[:]))
        a, b, k = 0, 1, 1
        while k < E1:
            dve.tensor_copy(ends[b][:, 0:k], ends[a][:, 0:k])
            link(dve.tensor_tensor(ends[b][:, k:E1], ends[a][:, k:E1], ends[a][:, 0:E1 - k], ALU.add))
            a, b, k = b, a, 2 * k
        link(dve.tensor_tensor(past[:], const["all"][0:1, C_TILE:C_TILE + TILES1].unsqueeze(2).broadcast_to([1, TILES1, E1]),
                               ends[a][0:1, :].unsqueeze(1).broadcast_to([1, TILES1, E1]), ALU.is_ge))
        link(dve.tensor_reduce(tile_e[:], past[:], AX.X, ALU.add))
        link(dve.tensor_scalar(tile_e[:], tile_e[:], float(E1 - 1), None, ALU.min))
        dve.tensor_copy(tile_expert[:], tile_e[:]).then_inc(sems["tiles"], 1)
        link(dve.tensor_tensor(ends[b][:], ends[a][:], used[:], ALU.subtract))
        link(dve.tensor_scalar(ends[b][:], ends[b][:], float(SLOTS1), None, ALU.mult))
        link(dve.tensor_tensor(pos[:], pos[:], ends[b][:].unsqueeze(1).broadcast_to([P, NT, E1]), ALU.add))
        for i in range(TOP):
            link(dve.tensor_tensor(flag[:], pos[:], onehot[i][:], ALU.mult))
            link(dve.tensor_reduce(slot[:], flag[:], AX.X, ALU.add))
            op = dve.tensor_copy(at[i][:], slot[:])
            if i == 0:
                link(op)
        op.then_inc(sems["slots"], 1)

    def weigh_vector(dve):
        dve.wait_ge(sems["gap_exp"], 1)
        dve.tensor_scalar(divisor[:], gap_exp[:], 1.0, 2.0, ALU.add, ALU.mult).then_inc(sems["weighed"], 1)
        dve.wait_ge(sems["weighed"], 1)
        dve.reciprocal(weight[0][:], divisor[:]).then_inc(sems["weighed"], 1)
        dve.wait_ge(sems["weighed"], 2)
        dve.tensor_tensor(weight[1][:], gap_exp[:], weight[0][:], ALU.mult).then_inc(sems["weighed"], 1)

    def tiles_vector(dve):
        for k, par, fixed in pipelined(dve, TILES1, 2):
            if fixed is None or fixed < TILES1:
                dve.wait_ge(sems["hidden0"], k + 1)
                dve.wait_ge(sems["silu"], k + 1)
                for c in range(FC1):
                    op = dve.scalar_tensor_tensor(hid[par % 2][:, c, :], hidden_bank(par, 0)[:, c, :],
                                                  pack[par][:, B_AT + c:B_AT + c + 1], silu[par % 2][:, c, :], ALU.add, ALU.mult)
                op.then_inc(sems["hidden_out"], 1)
            if fixed != 0:
                last = (par + 3) % 4
                dve.wait_ge(sems["made"], k)
                if fixed is None or fixed > 4:
                    dve.wait_ge(sems[f"stored{last}"], uses(k - 1, last, 16))
                dve.tensor_tensor(made[last][:], made_bank[last % 2][:, 0:CT1 * D].rearrange("p (t d) -> p t d", t=CT1),
                                  pack[last][:, B2_AT:B2_AT + D].unsqueeze(1).broadcast_to([P, CT1, D]), ALU.add).then_inc(sems["made_out"], 1)

    def send_pool(pool, part):
        if part == 0:
            pool.wait_ge(sems["all_in"], 16)
            pool.wait_ge(sems["slots"], 1)
        for t in range(*SEND[part]):
            for i in range(TOP):
                pool.indirect_dma_start(dram["sent1"], bass.IndirectOffsetOnAxis(ap=at[i][:, t:t + 1], axis=0),
                                        xn_all[:, t, :], None).then_inc(sems["sent"], 16)
        if part == len(SEND) - 1:
            pool.wait_ge(sems["sent"], 16 * NT * TOP)

    def done_pool(pool):
        for i in range(4):
            pool.wait_ge(sems[f"stored{i}"], 16 * (TILES1 // 4))

    parts = (route_sync, tiles_sync, route_tensor, tiles_tensor, route_scalar, tiles_scalar, choose_vector, place_vector,
             weigh_vector, tiles_vector, send_pool, done_pool)
    return sems, {f.__name__: f for f in parts}


def build(nc, w, out):
    with ExitStack() as ctx:
        def sb(name, shape, dt=F32):
            return ctx.enter_context(nc.sbuf_tensor(name, shape, dt))

        def ps(name, shape):
            return ctx.enter_context(nc.psum_tensor(name, shape, F32))

        def scratch(name, shape, dt=F32):
            return nc.dram_tensor(name, shape, dt, kind="Internal").ap()

        psum = (ps("ps_scores", [P, 4, S]), ps("ps_max", [P, 2, S]), ps("ps_sum", [P, S]), ps("ps_misc", [P, S]))
        dram = {
            "x": w["x"], "xn": scratch("xn", [NB * S, D]), "x2": scratch("x2", [NB * S, D]), "xn2": scratch("xn2", [NB * S, D]),
            "q": scratch("q_rows", [H, ROW_END, S], BF16), "k": scratch("k_rows", [H, ROW_END, S], BF16),
            "sent0": scratch("sent0", [E0 * CAP + NB * S, D]), "made0": scratch("made0", [E0 * CAP, D]),
            "sent1": scratch("sent1", [TILES1 * SLOTS1, D]), "made1": scratch("made1", [TILES1 * SLOTS1, D]),
        }
        every = sb("consts", [P, C_END])
        const = {
            "all": every, "ident": every[:, C_IDENT:C_IDENT + P], "holt": every[:, C_HOLT:C_END],
            "minus_half": sb("minus_half", [P, 2 * QT]), "ones": sb("ones", [P, P], BF16),
            **{k: sb(k, [P, P], BF16) for k in ("ident_bf", "before", "mask_qk", "mask_kq")},
        }
        const["onehot_bf"] = sb("onehot_bf", [P, NT * E0], BF16)
        routes = [{"at": [sb(f"at{n}{i}", [P, NT], U32) for i in range(k)], "weight": [sb(f"weight{n}{i}", [P, NT]) for i in range(k)]}
                  for n, k in ((0, 1), (1, TOP))]
        work = sb("work", [P, WORK])
        logits0 = made_of(work)[:, 7 * NT:7 * NT + NT * E0].rearrange("p (t e) -> p t e", t=NT)
        routes[1]["logits"] = sb("logits1", [P, NT, E1])
        weights = {"by_layer": [{k: sb(f"w{k}{n}", [P, D]) for k in "qkvo"} for n in range(2)], "bqs": sb("bqs", [P, 1])}
        loads = [(t, w[f"a{n}_w{k}"]) for n in range(2) for k, t in weights["by_layer"][n].items()]
        for k, shape in {"bq": [P, 1], "bk": [P, 1], "w_ff1": [P, F0], "w_ff2": [P, FC0, D], "b_ff1": [P, FC0], "gate_w1": [P, E1],
                         "gate_b1": [P, E1], **{k: [P, D] for k in ("bv", "bo", "g12", "be12", "b_ff2", "g_ff", "be_ff")}}.items():
            src = w[f"a0_{k}"]
            weights[k] = sb(k, shape)
            loads.append((weights[k], src.partition_broadcast(P) if len(src.shape) == 1 else src))
        strips = {"q": [sb(f"q_strip{i}", [P, NG, S], BF16) for i in range(2)],
                  "k": [sb(f"k_strip{i}", [P, H, S], BF16) for i in range(2)],
                  "v": [sb(f"v_aug{i}", [P, QT, H, VW]) for i in range(2)]}
        tokens = sb("tokens", [P, NT, D])
        normalise0(nc, const, psum, strips, dram, w, tokens, logits0, weights, loads)
        attention(nc, const, psum, strips, tokens, work, dram, weights, routes, out, lambda ctx, probs: (
            experts0(nc, ctx, tokens, work, probs, logits0, routes[1]["at"][0], const, psum, dram, w, routes[0]),
            experts1(nc, ctx, tokens, work, const, psum, dram, w, routes[1])))


def layout(v):
    f = {k: np.asarray(a) for k, a in v.items()}

    order = np.arange(P).reshape(NG, 2, HD).transpose(1, 0, 2).reshape(P)

    def pair(name):
        m = np.zeros((P, P), np.float32)
        m[:HALF, :HALF], m[HALF:, HALF:] = f[f"L0_attn_{name}1"].T, f[f"L0_attn_{name}2"].T
        return m[:, order] if name in ("wq", "wk") else m

    def both(name):
        return np.concatenate([f[f"L0_attn_{name}1"], f[f"L0_attn_{name}2"]])

    pack = np.concatenate([
        f["L1_ffn_w0"].transpose(0, 2, 1), f["L1_ffn_w1"].transpose(0, 2, 1),
        f["L1_ffn_w2"].transpose(0, 2, 1).reshape(E1, FC1, P, D).transpose(0, 2, 1, 3).reshape(E1, P, FC1 * D),
        f["L1_ffn_b0"].reshape(E1, FC1, P).transpose(0, 2, 1), f["L1_ffn_b1"].reshape(E1, FC1, P).transpose(0, 2, 1),
        np.repeat(f["L1_ffn_b2"][:, None, :], P, 1)], 2)
    return {
        "x": f["L0_attn_x"].reshape(NB * S, D), "zeros": np.zeros((P, 1024), np.float32), "consts": constants(), "alibi": alibi(),
        "gate_w0": f["L0_ffn_Wg"], "w1_0": f["L0_ffn_w1"], "w2_0": f["L0_ffn_w2"], "pack1": pack,
        **{f"a0_w{k}": pair(f"w{k}") for k in "qkvo"},
        **{f"a0_b{k}": both(f"b{k}")[order].reshape(P, 1) if k in "qk" else both(f"b{k}") for k in "qkvo"},
        "a0_g12": both("g"), "a0_be12": both("be"),
        "a0_w_ff1": f["L0_attn_w_ff1"].T, "a0_b_ff1": f["L0_attn_b_ff1"].reshape(FC0, P).T,
        "a0_w_ff2": f["L0_attn_w_ff2"].T.reshape(FC0, P, D).transpose(1, 0, 2), "a0_b_ff2": f["L0_attn_b_ff2"],
        "a0_g_ff": f["L0_attn_g_ff"], "a0_be_ff": f["L0_attn_be_ff"],
        "a0_gate_w1": f["L1_ffn_gate_w"].T, "a0_gate_b1": f["L1_ffn_gate_b"],
        **{f"a1_w{k}": f[f"L1_attn_W{k}"].T[:, order if k in "qk" else slice(None)] for k in "qkvo"},
    }


def kernel(**inputs):
    import concourse.bacc as bacc
    from concourse.bass_utils import run_bass_kernel_spmd

    nc = bacc.Bacc("TRN2", target_bir_lowering=False, num_devices=1)
    arrays = {k: np.ascontiguousarray(a) for k, a in layout(inputs).items()}
    aps = {k: nc.dram_tensor(f"in_{k}", a.shape, mybir.dt.from_np(a.dtype), kind="ExternalInput").ap() for k, a in arrays.items()}
    out = nc.dram_tensor("out", (NB * S, D), F32, kind="ExternalOutput").ap()
    build(nc, aps, out)
    r = run_bass_kernel_spmd(nc, [{f"in_{k}": a for k, a in arrays.items()}], core_ids=[0])
    return r.results[0]["out"].reshape(NB, S, D)
```
